# Optimizing a Trainium2 kernel written in Bass

```python
import numpy as np
import jax
import jax.numpy as jnp

def _softmax(x, axis=-1):
    return jax.nn.softmax(x, axis=axis)

def _gelu(x):
    return jax.nn.gelu(x, approximate=True)

def _silu(x):
    return jax.nn.silu(x)

def _sigmoid(x):
    return jax.nn.sigmoid(x)

def _layernorm(x, axis=-1, eps=1e-05):
    m = jnp.mean(x, axis=axis, keepdims=True)
    v = jnp.var(x, axis=axis, keepdims=True)
    return (x - m) / jnp.sqrt(v + eps)

def _scatter_add(tgt, idx, src, axis=0):
    return tgt.at[idx].add(src)

def _segment_sum(src, seg, n):
    return jax.ops.segment_sum(src, seg, n)
kernel_name = 'mk_adj_resnorm_d4_adj_r2_c4c572'

def setup_inputs(seed: int=0):
    np.random.seed(seed)
    _w = jnp.asarray

    def _rec_inputs():
        import jax
        import jax.numpy as jnp
        _gk = jax.random.key(seed)
        x = -0.0002928 + 1 * jax.random.normal(jax.random.fold_in(_gk, 1), (2048, 256), jnp.float32)
        _a = jax.random.bernoulli(jax.random.fold_in(_gk, 2), 0.00390625, (2048, 2048))
        _a = jnp.logical_or(_a, jnp.swapaxes(_a, -1, -2))
        _a = jnp.logical_or(_a, jnp.eye(2048, dtype=bool))
        _af = _a.astype(jnp.float32)
        _af = _af * jax.random.uniform(jax.random.fold_in(_gk, 3), (2048, 2048), jnp.float32, 0.05, 1)
        adj = _af
        return (x, adj)
    x, adj = _rec_inputs()

    def _L0_gnn_setup():
        import jax, jax.numpy as jnp
        import numpy as np
        EPS = 1e-08
        key = jax.random.key(seed)
        k1, k2, k3, k4 = jax.random.split(key, 4)
        N, IN, OUT = (4096, 256, 256)
        x = jax.random.normal(k1, (N, IN), dtype=jnp.float32)
        adj = jax.random.uniform(k2, (N, N), dtype=jnp.float32)
        W = jax.random.normal(k3, (OUT, IN), dtype=jnp.float32) * (1.0 / np.sqrt(IN))
        b = jax.random.normal(k4, (OUT,), dtype=jnp.float32) * 0.01
        return {'x': x, 'adj': adj, 'W': W, 'b': b}
    _L0_gnn_all = _L0_gnn_setup()
    _L0_gnn_in = {k: v for k, v in _L0_gnn_all.items() if k in ('W', 'b')}
    del _L0_gnn_all

    def _L1_gnn_setup():
        import jax, jax.numpy as jnp
        import numpy as np
        N = 4096
        D_IN = 256
        D_OUT = 256
        NEG_BIG = -9000000000000000.0
        key = jax.random.key(seed)
        kx, ka, kw, kb, kn, ke = jax.random.split(key, 6)
        x = jax.random.normal(kx, (N, D_IN), dtype=jnp.float32)
        adj = (jax.random.uniform(ka, (N, N)) > 0.9).astype(jnp.float32)
        stdv = 1.0 / np.sqrt(D_OUT)
        weight = jax.random.uniform(kw, (D_IN, D_OUT), minval=-stdv, maxval=stdv, dtype=jnp.float32)
        bias = jax.random.uniform(kb, (D_OUT,), minval=-stdv, maxval=stdv, dtype=jnp.float32)
        node_w = jax.random.uniform(kn, (D_IN, 1), minval=-1.0, maxval=1.0, dtype=jnp.float32)
        stdv_e = 1.0 / np.sqrt(D_IN)
        edge_w = jax.random.uniform(ke, (D_IN, D_IN), minval=-stdv_e, maxval=stdv_e, dtype=jnp.float32)
        return {'x': x, 'adj': adj, 'weight': weight, 'bias': bias, 'node_w': node_w, 'edge_w': edge_w}
    _L1_gnn_all = _L1_gnn_setup()
    _L1_gnn_in = {k: v for k, v in _L1_gnn_all.items() if k in ('weight', 'bias', 'node_w', 'edge_w')}
    del _L1_gnn_all

    def _L2_gnn_setup():
        import jax, jax.numpy as jnp
        import numpy as np
        N = 3072
        D_IN = 256
        D_OUT = 256
        DENSITY = 0.005
        key = jax.random.key(seed)
        ks = jax.random.split(key, 12)
        x = jax.random.normal(ks[0], (N, D_IN), dtype=jnp.float32)
        adj_a = (jax.random.uniform(ks[1], (N, N)) < DENSITY).astype(jnp.float32)
        adj_b = (jax.random.uniform(ks[2], (N, N)) < DENSITY).astype(jnp.float32)
        W_sa = jax.random.normal(ks[3], (D_IN, D_OUT), dtype=jnp.float32) * (1.414 / np.sqrt(D_IN + D_OUT))
        a_sa = jax.random.normal(ks[4], (1, 2 * D_OUT), dtype=jnp.float32) * (1.414 / np.sqrt(1 + 2 * D_OUT))
        stdv = 1.0 / np.sqrt(D_OUT)
        W_gcnb = jax.random.uniform(ks[5], (D_IN, D_OUT), minval=-stdv, maxval=stdv, dtype=jnp.float32)
        b_gcnb = jax.random.uniform(ks[6], (D_OUT,), minval=-stdv, maxval=stdv, dtype=jnp.float32)
        s = 1.0 / np.sqrt(2 * D_IN)
        Wa = jax.random.uniform(ks[7], (1, 2 * D_IN), minval=-s, maxval=s, dtype=jnp.float32)
        ba = jax.random.uniform(ks[8], (1,), minval=-s, maxval=s, dtype=jnp.float32)
        Wb = jax.random.uniform(ks[9], (1, 2 * D_IN), minval=-s, maxval=s, dtype=jnp.float32)
        bb = jax.random.uniform(ks[10], (1,), minval=-s, maxval=s, dtype=jnp.float32)
        return {'x': x, 'adj_a': adj_a, 'adj_b': adj_b, 'W_sa': W_sa, 'a_sa': a_sa, 'W_gcnb': W_gcnb, 'b_gcnb': b_gcnb, 'Wa': Wa, 'ba': ba, 'Wb': Wb, 'bb': bb}
    _L2_gnn_all = _L2_gnn_setup()
    _L2_gnn_in = {k: v for k, v in _L2_gnn_all.items() if k in ('W_sa', 'a_sa', 'W_gcnb', 'b_gcnb', 'Wa', 'ba', 'Wb', 'bb')}
    del _L2_gnn_all

    def _L3_gnn_setup():
        import jax, jax.numpy as jnp
        import numpy as np
        N = 4096
        IN_F = 256
        OUT_F = 256
        key = jax.random.key(seed)
        k1, k2, k3, k4 = jax.random.split(key, 4)
        input = jax.random.normal(k1, (N, IN_F), dtype=jnp.float32)
        adj = jax.random.uniform(k2, (N, N), dtype=jnp.float32)
        W = jax.random.normal(k3, (OUT_F, IN_F), dtype=jnp.float32) / np.sqrt(IN_F)
        b = jax.random.normal(k4, (OUT_F,), dtype=jnp.float32) * 0.01
        return {'input': input, 'adj': adj, 'W': W, 'b': b}
    _L3_gnn_all = _L3_gnn_setup()
    _L3_gnn_in = {k: v for k, v in _L3_gnn_all.items() if k in ('W', 'b')}
    del _L3_gnn_all
    return {'x': x, 'adj': adj, 'L0_gnn_W': _L0_gnn_in['W'], 'L0_gnn_b': _L0_gnn_in['b'], 'L1_gnn_weight': _L1_gnn_in['weight'], 'L1_gnn_bias': _L1_gnn_in['bias'], 'L1_gnn_node_w': _L1_gnn_in['node_w'], 'L1_gnn_edge_w': _L1_gnn_in['edge_w'], 'L2_gnn_W_sa': _L2_gnn_in['W_sa'], 'L2_gnn_a_sa': _L2_gnn_in['a_sa'], 'L2_gnn_W_gcnb': _L2_gnn_in['W_gcnb'], 'L2_gnn_b_gcnb': _L2_gnn_in['b_gcnb'], 'L2_gnn_Wa': _L2_gnn_in['Wa'], 'L2_gnn_ba': _L2_gnn_in['ba'], 'L2_gnn_Wb': _L2_gnn_in['Wb'], 'L2_gnn_bb': _L2_gnn_in['bb'], 'L3_gnn_W': _L3_gnn_in['W'], 'L3_gnn_b': _L3_gnn_in['b']}

def reference(x, adj, L0_gnn_W, L0_gnn_b, L1_gnn_weight, L1_gnn_bias, L1_gnn_node_w, L1_gnn_edge_w, L2_gnn_W_sa, L2_gnn_a_sa, L2_gnn_W_gcnb, L2_gnn_b_gcnb, L2_gnn_Wa, L2_gnn_ba, L2_gnn_Wb, L2_gnn_bb, L3_gnn_W, L3_gnn_b):
    import jax
    import jax.numpy as jnp

    def _L0_gnn_ref(x, adj, W, b):
        import jax, jax.numpy as jnp
        import numpy as np
        EPS = 1e-08
        deg = adj.sum(axis=1)
        dis = (deg + EPS) ** (-0.5)
        a_norm = dis[:, None] * adj * dis[None, :]
        h = a_norm @ x
        return h @ W.T + b

    def _L1_gnn_ref(x, adj, weight, bias, node_w, edge_w):
        import jax, jax.numpy as jnp
        import numpy as np
        N = 4096
        D_IN = 256
        D_OUT = 256
        NEG_BIG = -9000000000000000.0
        node_att = jax.nn.softmax(x @ node_w, axis=0)
        h = x @ edge_w
        e = h @ h.T
        e = jnp.where(adj > 0, e, NEG_BIG)
        edge_att = jax.nn.softmax(e, axis=1)
        combined_att = node_att * edge_att
        support = x @ weight
        output = adj * combined_att @ support
        return output + bias

    def _L2_gnn_ref(x, adj_a, adj_b, W_sa, a_sa, W_gcnb, b_gcnb, Wa, ba, Wb, bb):
        import jax, jax.numpy as jnp
        import numpy as np
        N = 3072
        D_IN = 256
        D_OUT = 256
        DENSITY = 0.005
        type_sum_a = adj_a @ x
        type_sum_b = adj_b @ x
        attn_a = jax.nn.sigmoid(jnp.concatenate([type_sum_a, x], axis=1) @ Wa.T + ba)
        attn_b = jax.nn.sigmoid(jnp.concatenate([type_sum_b, x], axis=1) @ Wb.T + bb)
        h = x @ W_sa
        Hd = h.shape[1]
        s_left = h @ a_sa[0, :Hd]
        s_right = h @ a_sa[0, Hd:]
        scores = s_left[:, None] + s_right[None, :]
        e = jnp.where(adj_a != 0, jnp.exp(-jax.nn.leaky_relu(scores, 0.01)), 0.0)
        attn = e / (jnp.sum(e, axis=1, keepdims=True) + 1e-05)
        x_a = attn @ h
        x_b = adj_b @ (x @ W_gcnb) + b_gcnb
        return jax.nn.sigmoid(attn_a * x_a + attn_b * x_b)

    def _L3_gnn_ref(input, adj, W, b):
        import jax, jax.numpy as jnp
        import numpy as np
        N = 4096
        IN_F = 256
        OUT_F = 256
        h = jnp.einsum('ni,oi->no', input, W) + b
        return adj @ h
    x = _layernorm(x + _L0_gnn_ref(x, adj, L0_gnn_W, L0_gnn_b), axis=-1)
    x = _layernorm(x + _L1_gnn_ref(x, adj, L1_gnn_weight, L1_gnn_bias, L1_gnn_node_w, L1_gnn_edge_w), axis=-1)
    x = _layernorm(x + _L2_gnn_ref(x, adj, adj, L2_gnn_W_sa, L2_gnn_a_sa, L2_gnn_W_gcnb, L2_gnn_b_gcnb, L2_gnn_Wa, L2_gnn_ba, L2_gnn_Wb, L2_gnn_bb), axis=-1)
    x = _layernorm(x + _L3_gnn_ref(x, adj, L3_gnn_W, L3_gnn_b), axis=-1)
    return x

_drawn_inputs = setup_inputs


def setup_inputs(seed=0):
    import zlib

    import numpy as np

    out = dict(_drawn_inputs(seed))
    spreads = {}
    factors = {'L1_gnn_weight': 5.934,
     'L1_gnn_node_w': 4.83,
     'L2_gnn_a_sa': 3.262,
     'L2_gnn_b_gcnb': 5.569,
     'L2_gnn_Wa': 4.42}
    for name, (base, spread) in spreads.items():
        noise = np.random.default_rng([zlib.crc32(name.encode()), seed]).standard_normal(out[name].shape)
        drawn = base * np.exp(spread * noise) if base else spread * noise
        out[name] = jnp.asarray(drawn.astype(out[name].dtype))
    for name, factor in factors.items():
        out[name] = (out[name] * factor).astype(out[name].dtype)
    return out
```

```python
from contextlib import ExitStack

import concourse.bass as bass
from concourse import mybir

F32 = mybir.dt.float32
F32R = mybir.dt.float32r
ACT = mybir.ActivationFunctionType
ALU = mybir.AluOpType
AX_X = mybir.AxisListType.X
RMAX = bass.bass_isa.ReduceOp.max
RADD = bass.bass_isa.ReduceOp.add

P = 128
N = 2048
D = 256
NT = N // P
DK = D // P
CW = 512
NC = N // CW
TC = CW // P
UJ = 4
NU = NT // UJ
EPS_DEG = 1e-8
EPS_LN = 1e-5
EPS_ATT = 1e-5
NEG_BIG = -9000000000000000.0


class Steps:

    def __init__(self, engine, semaphore):
        self.engine, self.semaphore, self.base, self.count = engine, semaphore, 0, 0

    def __call__(self, instruction):
        instruction.then_inc(self.semaphore, 1)
        self.count += 1

    def wait(self):
        self.engine.wait_ge(self.semaphore, self.base + self.count)

    def restart(self, base):
        self.base, self.count = base, 0


def flat(ap):
    return ap.rearrange("p o d -> p (o d)")


def one(t):
    return bass.ds(t, 1)


def later(index, least):
    return not isinstance(index, int) or index >= least


def graph_kernel(nc, T):
    with ExitStack() as ctx:
        def sb(stack, name, shape, dt=F32):
            return stack.enter_context(nc.sbuf_tensor(name, shape, dt))

        def sem(name):
            return ctx.enter_context(nc.semaphore(name))

        X = sb(ctx, "X", [P, NT, D])
        UH = sb(ctx, "UH", [P, NT, D], F32R)
        UL = sb(ctx, "UL", [P, NT, D], F32R)
        ident = sb(ctx, "ident", [P, P])
        ones = sb(ctx, "ones", [P, P])
        deg = sb(ctx, "deg", [P, NT])
        dis = sb(ctx, "dis", [P, NT])
        stats = sb(ctx, "stats", [P, NT, 6])
        mv = sb(ctx, "mv", [P, NT, 2])
        rstd = sb(ctx, "rstd", [P, NT])
        PS = ctx.enter_context(nc.psum_tensor("PS", [P, 8, CW], F32))

        adj_units = T["adjT"].rearrange("(q r p) n -> q p r n", r=UJ, p=P)
        adj_rows = T["adj"].rearrange("(t p) n -> t p n", p=P)

        x_loaded, const_made = sem("x_loaded"), sem("const_made")
        with nc.Block() as block:
            @block.sync
            def _(sp):
                sp.dma_start(X[:, :, :], T["x"].rearrange("(t p) d -> p t d", p=P)).then_inc(x_loaded, 16)
                sp.wait_ge(x_loaded, 16)

            @block.gpsimd
            def _(pool):
                pool.memset(ones[:, :], 1.0).then_inc(const_made, 1)
                pool.memset(ident[:, :], 0.0).then_inc(const_made, 1)
                pool.wait_ge(const_made, 2)
                pool.affine_select(out=ident[:, :], in_=ident[:, :], compare_op=ALU.not_equal, fill=1.0,
                                   base=0, pattern=[[-1, P]], channel_multiplier=1).then_inc(const_made, 1)

        def load_all(sp, plan, loaded):
            for dst, src in plan:
                sp.dma_start(dst, src, allow_slow_non_contiguous=True).then_inc(loaded, 16)

        def weight(name):
            return T[name].rearrange("(k p) n -> p k n", p=P)

        def split_features(v, steps, src, features_split):
            for q in range(NU):
                t = slice(UJ * q, UJ * q + UJ)
                steps(v.tensor_copy(UH[:, t, :], src[:, t, :]))
                steps.wait()
                v.tensor_tensor(UL[:, t, :], src[:, t, :], UH[:, t, :].bitcast(F32),
                                ALU.subtract).then_inc(features_split, 1)

        def wait_apart(eng, semaphore, value):
            if not isinstance(value, int):
                value = eng.snap(value)
                eng.compute_val(value)
            eng.wait_ge(x_loaded, 16)
            eng.wait_ge(semaphore, value)

        def row_stats(v, steps, t):
            steps(v.bn_stats(flat(stats[:, one(t), :]), flat(X[:, one(t), :])))

        def norm_rows(v, steps, var_ready, roots_ready, tiles_normed):
            steps.wait()
            for t in range(NT):
                steps(v.bn_aggr(mv[:, t, :], stats[:, t, :]))
            steps.wait()
            v.tensor_scalar(rstd[:, :], mv[:, :, 1], EPS_LN, None, ALU.add).then_inc(var_ready, 1)
            v.wait_ge(roots_ready, 1)
            steps(v.reciprocal(rstd[:, :], rstd[:, :]))
            steps.wait()
            for t in range(NT):
                v.tensor_scalar(X[:, t, :], X[:, t, :], mv[:, t, 0:1], rstd[:, t:t + 1],
                                ALU.subtract, ALU.mult).then_inc(tiles_normed, 1)

        def take_roots(act, var_ready, roots_ready):
            act.wait_ge(var_ready, 1)
            act.activation(rstd[:, :], rstd[:, :], ACT.Sqrt).then_inc(roots_ready, 1)

        def aggregate_unit(pe, q, MH, ML, bank):
            last = None
            for r in range(UJ):
                jt = UJ * q + r
                for k in range(DK):
                    fc = slice(k * P, k * P + P)
                    for n, (u, m) in enumerate(((UH, MH), (UH, ML), (UL, MH))):
                        last = pe.matmul(PS[:, bank + k, :], u[:, jt, fc], m[:, r, :],
                                         start=(jt == 0 and n == 0), stop=(jt == NT - 1 and n == 2))
            return last

        def gcn_layer(tag, first):
            with ExitStack() as lay:
                def lsem(name):
                    return sem(f"{name}_{tag}")

                raw = sb(lay, f"raw{tag}", [P, NU, UJ, CW])
                MH = sb(lay, f"MH{tag}", [P, 2, UJ, CW], F32R)
                ML = sb(lay, f"ML{tag}", [P, 2, UJ, CW], F32R)
                TT = sb(lay, f"TT{tag}", [P, DK, CW])
                WT = sb(lay, f"WT{tag}", [P, DK, D])
                bias = sb(lay, f"bias{tag}", [P, D])
                if first:
                    XS = sb(lay, f"XS{tag}", [P, NT, D])
                row_slots = raw[:, :, :, :].rearrange("p s r w -> p s (r w)")
                out_rows = T["out"].rearrange("(t p) d -> p t d", p=P)

                consts_loaded = lsem("consts_loaded")
                rows_loaded = [lsem(f"rows_loaded{i}") for i in range(NU)]
                rows_summed = lsem("rows_summed")
                deg_eps, deg_root = lsem("deg_eps"), lsem("deg_root")
                unit_loaded = [lsem(f"unit_loaded{i}") for i in range(NU)]
                unit_high, unit_low = lsem("unit_high"), lsem("unit_low")
                unit_done = lsem("unit_done")
                features_split = lsem("features_split")
                copied = lsem("copied")
                rows_out, rows_read = lsem("rows_out"), lsem("rows_read")
                var_ready, roots_ready = lsem("var_ready"), lsem("roots_ready")
                tiles_normed, stored = lsem("tiles_normed"), lsem("stored")
                dve_steps = lsem("dve_steps")

                with nc.Block() as block:
                    @block.sync
                    def _(sp):
                        def load_rows(g, i):
                            if later(g, 1):
                                sp.wait_ge(rows_summed, g * NU + i - NU + 1)
                            sp.dma_start(row_slots[:, i, :], adj_rows[one(g * NU + i), :, :].rearrange(
                                "o p n -> (o p) n")).then_inc(rows_loaded[i], 16)

                        def load_unit(c, q):
                            if later(c, 1):
                                sp.wait_ge(unit_low, c * NU + q - NU + 1)
                            sp.dma_start(raw[:, q, :, :], adj_units[q, :, :, bass.ds(c * CW, CW)])\
                              .then_inc(unit_loaded[q], 16)

                        if first:
                            for i in range(NU):
                                load_rows(0, i)
                            with sp.Fori(1, NT // NU) as g:
                                for i in range(NU):
                                    load_rows(g, i)
                        load_all(sp, [(WT[:, :, :], weight(f"W{tag}T")),
                                      (bias[:, :], T[f"b{tag}"].partition_broadcast(P))], consts_loaded)
                        for q in range(NU):
                            if first:
                                sp.wait_ge(rows_summed, NT - NU + q + 1)
                            load_unit(0, q)
                        with sp.Fori(1, NC) as c:
                            for q in range(NU):
                                load_unit(c, q)
                        if not first:
                            for g in range(NC):
                                sp.wait_ge(tiles_normed, TC * (g + 1))
                                t = slice(TC * g, TC * g + TC)
                                sp.dma_start(out_rows[:, t, :], X[:, t, :]).then_inc(stored, 16)
                            sp.wait_ge(stored, 16 * NC)

                    @block.scalar
                    def _(act):
                        if first:
                            for t in range(NT):
                                i = t % NU
                                act.wait_ge(rows_loaded[i], (t // NU) * 16 + 16)
                                act.activation(row_slots[:, i, :], row_slots[:, i, :], ACT.Copy,
                                               accum_out=deg[:, t:t + 1]).then_inc(rows_summed, 1)
                            act.wait_ge(deg_eps, 1)
                            act.activation(dis[:, :], dis[:, :], ACT.Sqrt).then_inc(deg_root, 1)

                        def high(c, q):
                            act.wait_ge(unit_loaded[q], c * 16 + 16)
                            if later(c * NU + q, 2):
                                act.wait_ge(unit_done, c * NU + q - 1)
                            act.activation(MH[:, q % 2, :, :], raw[:, q, :, :], ACT.Copy).then_inc(unit_high, 1)

                        def copy_aggregate(c):
                            act.wait_ge(unit_done, c * NU + NU)
                            if later(c, 1):
                                act.wait_ge(rows_out, c * TC)
                            for k in range(DK):
                                act.activation(TT[:, k, :], PS[:, k, :], ACT.Copy).then_inc(copied, 1)

                        for q in range(NU):
                            high(0, q)

                        def chunk(c):
                            high(c, 0)
                            copy_aggregate(c - 1)
                            for q in range(1, NU):
                                high(c, q)

                        chunk(1)
                        with act.Fori(2, NC) as c:
                            chunk(c)
                        copy_aggregate(NC - 1)
                        take_roots(act, var_ready, roots_ready)

                    @block.tensor
                    def _(pe):
                        def unit(c, q):
                            pe.wait_ge(unit_low, c * NU + q + 1)
                            if isinstance(c, int):
                                pe.wait_ge(features_split, q + 1)
                            if q == 0 and later(c, 1):
                                pe.wait_ge(copied, c * DK)
                            aggregate_unit(pe, q, MH[:, q % 2, :, :], ML[:, q % 2, :, :], 0)\
                                .then_inc(unit_done, 1)

                        def out_rows_of(c):
                            pe.wait_ge(copied, c * DK + DK)
                            if isinstance(c, int):
                                pe.wait_ge(consts_loaded, 32)
                            for j in range(TC):
                                if later(c, 1):
                                    pe.wait_ge(rows_read, c * TC + j - TC + 1)
                                for k in range(DK):
                                    last = pe.matmul(PS[:, 4 + j, 0:D], TT[:, k, j * P:j * P + P], WT[:, k, :],
                                                     start=(k == 0), stop=(k == DK - 1))
                                last.then_inc(rows_out, 1)

                        for q in range(NU):
                            unit(0, q)
                        pe.wait_ge(consts_loaded, 32)

                        def chunk(c):
                            unit(c, 0)
                            out_rows_of(c - 1)
                            for q in range(1, NU):
                                unit(c, q)

                        chunk(1)
                        with pe.Fori(2, NC) as c:
                            chunk(c)
                        out_rows_of(NC - 1)

                    @block.vector
                    def _(v):
                        steps = Steps(v, dve_steps)
                        if first:
                            v.wait_ge(rows_summed, NT)
                            v.tensor_scalar(dis[:, :], deg[:, :], EPS_DEG, None, ALU.add).then_inc(deg_eps, 1)
                            v.wait_ge(deg_root, 1)
                            steps(v.reciprocal(dis[:, :], dis[:, :]))
                            steps.wait()
                            for t in range(NT):
                                steps(v.tensor_scalar(XS[:, t, :], X[:, t, :], dis[:, t:t + 1], None, ALU.mult))
                            steps.wait()
                        split_features(v, steps, XS if first else X, features_split)

                        def low(c, q):
                            v.wait_ge(unit_high, c * NU + q + 1)
                            v.tensor_tensor(ML[:, q % 2, :, :], raw[:, q, :, :],
                                            MH[:, q % 2, :, :].bitcast(F32), ALU.subtract).then_inc(unit_low, 1)

                        def take_rows(c):
                            for j in range(TC):
                                t = c * TC + j
                                v.wait_ge(rows_out, t + 1)
                                Xt = flat(X[:, one(t), :])
                                if first:
                                    v.scalar_tensor_tensor(out=Xt, in0=PS[:, 4 + j, 0:D], scalar=dis[:, one(t)],
                                                           in1=Xt, op0=ALU.mult, op1=ALU.add).then_inc(rows_read, 1)
                                else:
                                    v.tensor_tensor(Xt, PS[:, 4 + j, 0:D], Xt, ALU.add).then_inc(rows_read, 1)
                                wait_apart(v, rows_read, t + 1)
                                row_stats(v, steps, t)

                        for q in range(2):
                            low(0, q)
                        v.wait_ge(consts_loaded, 32)
                        v.wait_ge(features_split, NU)
                        for t in range(NT):
                            if first:
                                steps(v.tensor_tensor(X[:, t, :], X[:, t, :], bias[:, :], ALU.add))
                            else:
                                steps(v.scalar_tensor_tensor(out=X[:, t, :], in0=bias[:, :], scalar=deg[:, t:t + 1],
                                                             in1=X[:, t, :], op0=ALU.mult, op1=ALU.add))
                        steps.wait()
                        for q in range(2, NU):
                            low(0, q)
                        entry = steps.count
                        with v.Fori(1, NC) as c:
                            low(c, 0)
                            low(c, 1)
                            take_rows(c - 1)
                            low(c, 2)
                            low(c, 3)
                        take_rows(NC - 1)
                        steps.restart(entry + NT)
                        norm_rows(v, steps, var_ready, roots_ready, tiles_normed)

        def attention_layer():
            with ExitStack() as lay:
                XT = sb(lay, "XT", [P, DK, N])
                HH = sb(lay, "HH", [P, DK, N], F32R)
                HL = sb(lay, "HL", [P, DK, N], F32R)
                arow = sb(lay, "arow", [P, 2, N])
                bias_m = sb(lay, "bias_m", [P, N])
                S = sb(lay, "S", [P, 2, N])
                WH = sb(lay, "WH", [P, NT, P], F32R)
                WL = sb(lay, "WL", [P, NT, P], F32R)
                SH = sb(lay, "SH", [P, 2, DK, P], F32R)
                SL = sb(lay, "SL", [P, 2, DK, P], F32R)
                Wedge = sb(lay, "Wedge", [P, DK, D])
                Wsup = sb(lay, "Wsup", [P, DK, D])
                nodew = sb(lay, "nodew", [P, D])
                bias = sb(lay, "bias1", [P, D])
                logit = sb(lay, "logit", [P, NT])
                natt = sb(lay, "natt", [P, NT])
                small = sb(lay, "small", [P, 8])
                mx = sb(lay, "mx", [P, 2, NC])
                nmax = sb(lay, "nmax", [P, 2])
                Z = sb(lay, "Z", [P, 2])
                scale = sb(lay, "scale", [P, 2])

                consts_loaded = sem("consts_loaded_1")
                arow_loaded = [sem(f"arow_loaded{i}") for i in range(2)]
                job_done, job_act, job_dve = sem("job_done"), sem("job_act"), sem("job_dve")
                logits_ready, logit_max, logit_gmax = sem("logits_ready"), sem("logit_max"), sem("logit_gmax")
                logit_exp, logit_sum = sem("logit_exp"), sem("logit_sum")
                staged = sem("staged")
                scored = sem("scored")
                masked = sem("masked")
                max_ready, exp_ready = sem("max_ready"), sem("exp_ready")
                weighted = sem("weighted")
                turned = sem("turned")
                turned_high, turned_low = sem("turned_high"), sem("turned_low")
                summed, rows_read = sem("summed"), sem("rows_read_1")
                var_ready, roots_ready = sem("var_ready_1"), sem("roots_ready_1")
                tiles_normed, dve_steps = sem("tiles_normed_1"), sem("dve_steps_1")

                jobs = []
                for c in range(NC):
                    jobs += [("turn", c, k) for k in range(DK)]
                for c in range(NC):
                    jobs += [("edge", c, k) for k in range(DK)]
                jobs += [("support", t, 0) for t in range(0, NT, 2)]
                split_count = [sum(j[0] != "turn" for j in jobs[:n + 1]) for n in range(len(jobs))]
                n_turn = NC * DK

                def job_target(job):
                    kind, i, k = job
                    cols = slice(i * CW, i * CW + CW)
                    if kind == "turn":
                        return XT[:, k, cols], None
                    if kind == "edge":
                        return HH[:, k, cols], HL[:, k, cols]
                    return (UH[:, i:i + 2, :].rearrange("p t d -> p (t d)"),
                            UL[:, i:i + 2, :].rearrange("p t d -> p (t d)"))

                with nc.Block() as block:
                    @block.sync
                    def _(sp):
                        load_all(sp, [(Wedge[:, :, :], weight("edge_w")), (Wsup[:, :, :], weight("weight")),
                                      (nodew[:, :], T["node_w"].rearrange("d o -> (d o)").partition_broadcast(P)),
                                      (bias[:, :], T["b1"].partition_broadcast(P))], consts_loaded)

                        def load(t, s):
                            if later(t, 2):
                                sp.wait_ge(weighted, t - 1)
                            sp.dma_start(arow[:, s, :], adj_rows[one(t), :, :].rearrange("o p n -> (o p) n"))\
                              .then_inc(arow_loaded[s], 16)

                        load(0, 0)
                        load(1, 1)
                        with sp.Fori(1, NT // 2) as g:
                            load(g * 2, 0)
                            load(g * 2 + 1, 1)

                    @block.tensor
                    def _(pe):
                        pe.wait_ge(consts_loaded, 64)
                        for n, (kind, i, k) in enumerate(jobs):
                            if n >= 8:
                                pe.wait_ge(job_act, n - 7)
                                if split_count[n - 8]:
                                    pe.wait_ge(job_dve, split_count[n - 8])
                            bank = PS[:, n % 8, :]
                            if kind == "turn":
                                for j in range(TC):
                                    last = pe.transpose(bank[:, j * P:j * P + P],
                                                        X[:, i * TC + j, k * P:k * P + P], ident[:, :])
                            elif kind == "edge":
                                pe.wait_ge(job_act, max(n - 7, n_turn))
                                for kk in range(DK):
                                    last = pe.matmul(bank, Wedge[:, kk, k * P:k * P + P],
                                                     XT[:, kk, i * CW:i * CW + CW],
                                                     start=(kk == 0), stop=(kk == DK - 1))
                            else:
                                for h in range(2):
                                    for kk in range(DK):
                                        last = pe.matmul(bank[:, h * D:h * D + D],
                                                         XT[:, kk, (i + h) * P:(i + h) * P + P], Wsup[:, kk, :],
                                                         start=(kk == 0), stop=(kk == DK - 1))
                            last.then_inc(job_done, 1)

                        def score(t, s, c):
                            if c == 0:
                                pe.wait_ge(staged, t + 1)
                            if later(t, 1):
                                pe.wait_ge(masked, (t - 1) * NC + c + 1)
                            cols = slice(c * CW, c * CW + CW)
                            for k in range(DK):
                                for n, (a, b) in enumerate(((SH, HH), (SH, HL), (SL, HH))):
                                    last = pe.matmul(PS[:, c, :], a[:, s, k, :], b[:, k, cols],
                                                     start=(k == 0 and n == 0), stop=(k == DK - 1 and n == 2))
                            last.then_inc(scored, 1)

                        def turn(t, s, g):
                            if g == 0:
                                pe.wait_ge(weighted, t + 1)
                            if later(t * NU + g, 2):
                                pe.wait_ge(turned_high, t * NU + g - 1)
                                pe.wait_ge(turned_low, t * NU + g - 1)
                            for r in range(UJ):
                                jt = UJ * g + r
                                last = pe.transpose(PS[:, 4 + g % 2, r * P:r * P + P],
                                                    S[:, s, jt * P:jt * P + P], ident[:, :])
                            last.then_inc(turned, 1)

                        def weigh(t, s):
                            if later(t, 2):
                                pe.wait_ge(rows_read, t - 1)
                            for g in range(NU):
                                pe.wait_ge(turned_low, t * NU + g + 1)
                                for r in range(UJ):
                                    jt = UJ * g + r
                                    for n, (w, u) in enumerate(((WH, UH), (WH, UL), (WL, UH))):
                                        last = pe.matmul(PS[:, 6 + s, 0:D], w[:, jt, :], u[:, jt, :],
                                                         start=(jt == 0 and n == 0),
                                                         stop=(jt == NT - 1 and n == 2))
                            last.then_inc(summed, 1)

                        def tile(t, s):
                            score(t, s, 0)
                            score(t, s, 1)
                            turn(t - 1, 1 - s, 0)
                            score(t, s, 2)
                            turn(t - 1, 1 - s, 1)
                            score(t, s, 3)
                            turn(t - 1, 1 - s, 2)
                            turn(t - 1, 1 - s, 3)
                            weigh(t - 1, 1 - s)

                        pe.wait_ge(job_act, len(jobs))
                        pe.wait_ge(job_dve, split_count[-1])
                        for c in range(NC):
                            score(0, 0, c)
                        tile(1, 1)
                        tile(2, 0)
                        with pe.Fori(1, NT // 2 - 1) as g:
                            tile(g * 2 + 1, 1)
                            tile(g * 2 + 2, 0)
                        tile(NT - 1, 1)
                        for g in range(NU):
                            turn(NT - 1, 1, g)
                        weigh(NT - 1, 1)

                    @block.scalar
                    def _(act):
                        for n, job in enumerate(jobs):
                            act.wait_ge(job_done, n + 1)
                            act.activation(job_target(job)[0], PS[:, n % 8, :], ACT.Copy).then_inc(job_act, 1)
                        act.wait_ge(logit_gmax, 1)
                        act.activation(natt[:, :], logit[:, :], ACT.Exp, bias=small[:, 2:3],
                                       accum_out=small[:, 3:4]).then_inc(logit_exp, 1)

                        def exponent(t, s):
                            act.wait_ge(max_ready, t + 1)
                            act.activation(S[:, s, :], S[:, s, :], ACT.Exp, bias=nmax[:, s:s + 1],
                                           accum_out=Z[:, s:s + 1]).then_inc(exp_ready, 1)

                        def high(t, s):
                            for g in range(NU):
                                act.wait_ge(turned, t * NU + g + 1)
                                act.activation(WH[:, UJ * g:UJ * g + UJ, :].rearrange("p t i -> p (t i)"),
                                               PS[:, 4 + g % 2, :], ACT.Copy).then_inc(turned_high, 1)

                        exponent(0, 0)
                        high(0, 0)
                        exponent(1, 1)
                        high(1, 1)
                        exponent(2, 0)
                        with act.Fori(1, NT // 2 - 1) as g:
                            for s in (1, 0):
                                high(g * 2 + 1 - s, 1 - s)
                                exponent(g * 2 + 2 - s, s)
                        high(NT - 2, 0)
                        exponent(NT - 1, 1)
                        high(NT - 1, 1)
                        take_roots(act, var_ready, roots_ready)

                    @block.gpsimd
                    def _(pool):
                        pool.wait_ge(logit_max, 1)
                        pool.partition_all_reduce(small[:, 1:2], small[:, 0:1], P, RMAX).then_inc(logit_max, 1)
                        pool.wait_ge(logit_exp, 1)
                        pool.partition_all_reduce(small[:, 4:5], small[:, 3:4], P, RADD).then_inc(logit_sum, 1)

                    @block.vector
                    def _(v):
                        steps = Steps(v, dve_steps)
                        v.wait_ge(consts_loaded, 64)
                        for t in range(NT):
                            v.tensor_tensor_reduce(S[:, t // 8, (t % 8) * D:(t % 8) * D + D], X[:, t, :],
                                                   nodew[:, :], 1.0, 0.0, ALU.mult, ALU.add,
                                                   logit[:, t:t + 1]).then_inc(logits_ready, 1)
                        v.wait_ge(logits_ready, NT)
                        v.tensor_reduce(small[:, 0:1], logit[:, :], AX_X, ALU.max).then_inc(logit_max, 1)
                        v.wait_ge(logit_max, 2)
                        v.tensor_scalar(small[:, 2:3], small[:, 1:2], -1.0, None, ALU.mult).then_inc(logit_gmax, 1)
                        for n, job in enumerate(jobs):
                            hi, lo = job_target(job)
                            if lo is not None:
                                v.wait_ge(job_act, n + 1)
                                v.tensor_tensor(lo, PS[:, n % 8, :], hi.bitcast(F32),
                                                ALU.subtract).then_inc(job_dve, 1)
                        v.wait_ge(logit_sum, 1)
                        steps(v.reciprocal(small[:, 5:6], small[:, 4:5]))
                        steps.wait()
                        steps(v.tensor_scalar(natt[:, :], natt[:, :], small[:, 5:6], None, ALU.mult))
                        v.wait_ge(job_done, n_turn)
                        for t in range(NT):
                            steps(v.tensor_tensor(X[:, t, :], X[:, t, :], bias[:, :], ALU.add))
                        v.wait_ge(job_dve, split_count[-1])
                        v.wait_ge(job_act, len(jobs))
                        steps.wait()

                        def stage(t, s):
                            if later(t, 2):
                                v.wait_ge(scored, (t - 1) * NC)
                            cols = bass.ds(t * P, P)
                            steps(v.tensor_scalar(SH[:, s, :, :], HH[:, :, cols].bitcast(F32), 1.0, None, ALU.mult))
                            v.tensor_scalar(SL[:, s, :, :], HL[:, :, cols].bitcast(F32), 1.0, None,
                                            ALU.mult).then_inc(staged, 1)

                        def mask_bias(t, s, turns):
                            v.wait_ge(arow_loaded[s], turns * 16 + 16)
                            steps(v.tensor_scalar(bias_m[:, :], arow[:, s, :], 0.0, NEG_BIG, ALU.is_le, ALU.mult))

                        def mask(t, s, c):
                            cols = slice(c * CW, c * CW + CW)
                            wait_apart(v, scored, t * NC + c + 1)
                            v.tensor_tensor_reduce(S[:, s, cols], PS[:, c, :], bias_m[:, cols], 1.0, -3.0e38,
                                                   ALU.add, ALU.max, mx[:, s, c:c + 1]).then_inc(masked, 1)

                        def row_max(t, s):
                            v.wait_ge(masked, t * NC + NC)
                            v.tensor_reduce(nmax[:, s:s + 1], mx[:, s, :], AX_X, ALU.max,
                                            negate=True).then_inc(max_ready, 1)

                        def low(t, s, g):
                            v.wait_ge(turned_high, t * NU + g + 1)
                            w = slice(UJ * g, UJ * g + UJ)
                            v.tensor_tensor(WL[:, w, :].rearrange("p t i -> p (t i)"), PS[:, 4 + g % 2, :],
                                            WH[:, w, :].rearrange("p t i -> p (t i)").bitcast(F32),
                                            ALU.subtract).then_inc(turned_low, 1)

                        def weight_rows(t, s):
                            v.wait_ge(exp_ready, t + 1)
                            v.tensor_tensor(S[:, s, :], S[:, s, :], arow[:, s, :], ALU.mult).then_inc(weighted, 1)

                        def take_rows(t, s):
                            steps(v.reciprocal(scale[:, s:s + 1], Z[:, s:s + 1]))
                            steps.wait()
                            steps(v.tensor_tensor(scale[:, s:s + 1], scale[:, s:s + 1], natt[:, one(t)], ALU.mult))
                            steps.wait()
                            v.wait_ge(summed, t + 1)
                            Xt = flat(X[:, one(t), :])
                            v.scalar_tensor_tensor(out=Xt, in0=PS[:, 6 + s, 0:D], scalar=scale[:, s:s + 1],
                                                   in1=Xt, op0=ALU.mult, op1=ALU.add).then_inc(rows_read, 1)
                            wait_apart(v, rows_read, t + 1)
                            row_stats(v, steps, t)

                        TILE_STEPS = 5

                        def tile(t, s, half):
                            mask(t, s, 0)
                            mask(t, s, 1)
                            low(t - 1, 1 - s, 0)
                            mask(t, s, 2)
                            low(t - 1, 1 - s, 1)
                            mask(t, s, 3)
                            row_max(t, s)
                            low(t - 1, 1 - s, 2)
                            low(t - 1, 1 - s, 3)
                            if not (isinstance(t, int) and t == NT - 1):
                                stage(t + 1, 1 - s)
                                mask_bias(t + 1, 1 - s, half)
                            weight_rows(t, s)
                            take_rows(t - 1, 1 - s)
                            steps.wait()

                        stage(0, 0)
                        mask_bias(0, 0, 0)
                        steps.wait()
                        for c in range(NC):
                            mask(0, 0, c)
                        row_max(0, 0)
                        stage(1, 1)
                        mask_bias(1, 1, 0)
                        weight_rows(0, 0)
                        steps.wait()
                        before = steps.count
                        tile(1, 1, 1)
                        assert steps.count - before == TILE_STEPS
                        tile(2, 0, 1)
                        entry = steps.count
                        with v.Fori(1, NT // 2 - 1) as g:
                            steps.restart(entry + (g - 1) * (2 * TILE_STEPS))
                            tile(g * 2 + 1, 1, g + 1)
                            tile(g * 2 + 2, 0, g + 1)
                        steps.restart(entry + (NT // 2 - 2) * 2 * TILE_STEPS)
                        tile(NT - 1, 1, None)
                        for g in range(NU):
                            low(NT - 1, 1, g)
                        take_rows(NT - 1, 1)
                        norm_rows(v, steps, var_ready, roots_ready, tiles_normed)

        def gated_layer():
            with ExitStack() as lay:
                raw = sb(lay, "raw2", [P, 2, UJ, CW])
                MH = sb(lay, "MH2", [P, 2, UJ, CW], F32R)
                ML = sb(lay, "ML2", [P, 2, UJ, CW], F32R)
                Ea = sb(lay, "Ea", [P, UJ, CW])
                Eb = sb(lay, "Eb", [P, UJ, CW])
                EM = sb(lay, "EM", [P, UJ, CW])
                EH = sb(lay, "EH", [P, 2, UJ, CW], F32R)
                EL = sb(lay, "EL", [P, 2, UJ, CW], F32R)
                sleft = sb(lay, "sleft", [P, N])
                Zacc = sb(lay, "Zacc", [P, UJ, CW])
                TA = sb(lay, "TA", [P, DK, CW])
                TE = sb(lay, "TE", [P, DK, CW])
                RA = sb(lay, "RA", [P, TC, D + 2])
                RE = sb(lay, "RE", [P, TC, D + 1])
                Wgcn = sb(lay, "Wgcn", [P, DK, D + 2])
                Wsa = sb(lay, "Wsa", [P, DK, D])
                WsaT = Ea[:, 0:DK, 0:D]
                wlr = Eb[:, 0:2, 0:D]
                avec = EM[:, 0:UJ, 0:P]
                diag = Zacc
                junk = EM[:, 2:4, 0:D]
                bg = sb(lay, "bg", [P, D])
                War = sb(lay, "War", [P, D])
                Wbr = sb(lay, "Wbr", [P, D])
                gate_b = sb(lay, "gate_b", [P, 2])
                asa = sb(lay, "asa", [P, 2 * DK])
                sl = sb(lay, "sl", [P, NT])
                nsr = sb(lay, "nsr", [P, NT])
                nsr01 = sb(lay, "nsr01", [P, NT])
                gx = sb(lay, "gx", [P, NT, 2])
                gate = sb(lay, "gate", [P, TC, 2])
                zr = sb(lay, "zr", [P, TC])

                consts_loaded = sem("consts_loaded_2")
                unit_loaded = [sem(f"unit_loaded{i}_2") for i in range(2)]
                features_split = sem("features_split_2")
                avec_made, wlr_out, wlr_copied = sem("avec_made"), sem("wlr_out"), sem("wlr_copied")
                diag_made, left_out, left_copied = sem("diag_made"), sem("left_out"), sem("left_copied")
                unit_high, unit_low = sem("unit_high_2"), sem("unit_low_2")
                exps = sem("exps")
                smaller, att_masked = sem("smaller"), sem("att_masked")
                att_high, att_low = sem("att_high"), sem("att_low")
                z_cleared, z_added = sem("z_cleared"), sem("z_added")
                adj_done, att_done = sem("adj_done"), sem("att_done")
                copied_a, copied_e = sem("copied_a"), sem("copied_e")
                rows_out, rows_read = sem("rows_out_2"), sem("rows_read_2")
                gates_in, gates_tanh = sem("gates_in"), sem("gates_tanh")
                mix_in, mix_tanh = sem("mix_in"), sem("mix_tanh")
                var_ready, roots_ready = sem("var_ready_2"), sem("roots_ready_2")
                tiles_normed, dve_steps = sem("tiles_normed_2"), sem("dve_steps_2")

                with nc.Block() as block:
                    @block.sync
                    def _(sp):
                        plan = [(WsaT, weight("W_saT")),
                                (asa[:, :], T["a_sa"][0, :].rearrange("(k p) -> p k", p=P)),
                                (gate_b[:, 0:1], T["ba"].partition_broadcast(P)),
                                (gate_b[:, 1:2], T["bb"].partition_broadcast(P)),
                                (War[:, :], T["Wa"][0, D:2 * D].partition_broadcast(P)),
                                (Wbr[:, :], T["Wb"][0, D:2 * D].partition_broadcast(P)),
                                (bg[:, :], T["b_gcnb"].partition_broadcast(P)),
                                (Wsa[:, :, :], weight("W_sa")), (Wgcn[:, :, 0:D], weight("W_gcnb"))]
                        for g, name in enumerate(("Wa", "Wb")):
                            for k in range(DK):
                                plan.append((Wgcn[:, k, D + g:D + g + 1],
                                             T[name][0, k * P:k * P + P].rearrange("(p o) -> p o", o=1)))
                        load_all(sp, plan, consts_loaded)

                        def load_unit(c, q):
                            if later(c * NU + q, 2):
                                sp.wait_ge(unit_low, c * NU + q - 1)
                                sp.wait_ge(att_masked, c * NU + q - 1)
                            sp.dma_start(raw[:, q % 2, :, :], adj_units[q, :, :, bass.ds(c * CW, CW)])\
                              .then_inc(unit_loaded[q % 2], 16)

                        for q in range(NU):
                            load_unit(0, q)
                        with sp.Fori(1, NC) as c:
                            for q in range(NU):
                                load_unit(c, q)
                    N_CONSTS = 16 * 13

                    @block.gpsimd
                    def _(pool):
                        def low(c, q):
                            pool.wait_ge(unit_high, c * NU + q + 1)
                            pool.tensor_tensor(ML[:, q % 2, :, :], raw[:, q % 2, :, :],
                                               MH[:, q % 2, :, :].bitcast(F32), ALU.subtract).then_inc(unit_low, 1)

                        def add_z(c, q):
                            if q == 0:
                                pool.wait_ge(z_cleared, c + 1)
                            else:
                                pool.wait_ge(z_added, c * NU + q)
                            pool.wait_ge(att_masked, c * NU + q + 1)
                            pool.tensor_tensor(Zacc[:, :, :], Zacc[:, :, :], EM[:, :, :], ALU.add)\
                                .then_inc(z_added, 1)

                        with pool.Fori(0, NC) as c:
                            low(c, 0)
                            low(c, 1)
                            add_z(c, 0)
                            low(c, 2)
                            add_z(c, 1)
                            low(c, 3)
                            add_z(c, 2)
                            add_z(c, 3)

                    @block.scalar
                    def _(act):
                        act.wait_ge(wlr_out, 1)
                        act.activation(wlr[:, :, :], PS[:, 0, :].rearrange("p (a d) -> p a d", a=2),
                                       ACT.Copy).then_inc(wlr_copied, 1)

                        def high(c, q):
                            act.wait_ge(unit_loaded[q % 2], (c * 2 + q // 2) * 16 + 16)
                            if later(c * NU + q, 2):
                                act.wait_ge(adj_done, c * NU + q - 1)
                            act.activation(MH[:, q % 2, :, :], raw[:, q % 2, :, :], ACT.Copy).then_inc(unit_high, 1)

                        def exponents(c, q):
                            if later(c * NU + q, 1):
                                wait_apart(act, att_masked, c * NU + q)
                            for r in range(UJ):
                                jt = UJ * q + r
                                zl = sleft[:, bass.ds(c * CW, CW)]
                                act.activation(Ea[:, r, :], zl, ACT.Exp, bias=nsr[:, jt:jt + 1],
                                               scale=-1.0).then_inc(exps, 1)
                                act.activation(Eb[:, r, :], zl, ACT.Exp, bias=nsr01[:, jt:jt + 1],
                                               scale=-0.01).then_inc(exps, 1)

                        def copy_a(c):
                            act.wait_ge(adj_done, c * NU + NU)
                            if later(c, 1):
                                act.wait_ge(rows_out, c * TC)
                            for k in range(DK):
                                act.activation(TA[:, k, :], PS[:, k, :], ACT.Copy).then_inc(copied_a, 1)

                        def copy_e(c):
                            act.wait_ge(att_done, c * NU + NU)
                            for k in range(DK):
                                act.activation(TE[:, k, :], PS[:, 2 + k, :], ACT.Copy).then_inc(copied_e, 1)

                        def tanh_gates(c):
                            act.wait_ge(gates_in, c + 1)
                            act.activation(gate[:, :, :], gate[:, :, :], ACT.Tanh, scale=0.5).then_inc(gates_tanh, 1)

                        def tanh_mix(c):
                            act.wait_ge(mix_in, c + 1)
                            act.activation(RA[:, :, 0:D], RA[:, :, 0:D], ACT.Tanh, scale=0.5).then_inc(mix_tanh, 1)

                        high(0, 0)
                        high(0, 1)
                        for c in range(NC):
                            act.wait_ge(left_out, c + 1)
                            act.activation(sleft[:, c * CW:c * CW + CW], PS[:, 4 + c, :], ACT.Copy)\
                                .then_inc(left_copied, 1)
                        act.wait_ge(left_copied, NC)
                        act.wait_ge(z_cleared, 1)
                        exponents(0, 0)
                        for q in range(1, NU):
                            if q > 1:
                                high(0, q)
                            exponents(0, q)

                        def chunk(c):
                            high(c, 0)
                            copy_a(c - 1)
                            copy_e(c - 1)
                            high(c, 1)
                            exponents(c, 0)
                            high(c, 2)
                            exponents(c, 1)
                            tanh_gates(c - 1)
                            high(c, 3)
                            exponents(c, 2)
                            tanh_mix(c - 1)
                            exponents(c, 3)

                        chunk(1)
                        with act.Fori(2, NC) as c:
                            chunk(c)
                        copy_a(NC - 1)
                        copy_e(NC - 1)
                        tanh_gates(NC - 1)
                        tanh_mix(NC - 1)
                        take_roots(act, var_ready, roots_ready)

                    @block.tensor
                    def _(pe):
                        pe.wait_ge(consts_loaded, N_CONSTS)
                        pe.wait_ge(avec_made, 2 * DK)
                        for h in range(2):
                            for k in range(DK):
                                last = pe.matmul(PS[:, 0, h * D:h * D + D], avec[:, 2 * h + k, :], WsaT[:, k, :],
                                                 start=(k == 0), stop=(k == DK - 1))
                        last.then_inc(wlr_out, 1)
                        for t in range(NT):
                            pe.wait_ge(diag_made, t + 1)
                            last = pe.matmul(PS[:, 4 + t // TC, (t % TC) * P:(t % TC) * P + P], ones[:, :],
                                             diag[:, t // TC, (t % TC) * P:(t % TC) * P + P],
                                             start=True, stop=True)
                            if t % TC == TC - 1:
                                last.then_inc(left_out, 1)

                        def adj_unit(c, q):
                            pe.wait_ge(unit_low, c * NU + q + 1)
                            if isinstance(c, int):
                                pe.wait_ge(features_split, q + 1)
                            if q == 0 and later(c, 1):
                                pe.wait_ge(copied_a, c * DK)
                            aggregate_unit(pe, q, MH[:, q % 2, :, :], ML[:, q % 2, :, :], 0).then_inc(adj_done, 1)

                        def att_unit(c, q):
                            pe.wait_ge(att_low, c * NU + q + 1)
                            if q == 0 and later(c, 1):
                                pe.wait_ge(copied_e, c * DK)
                            aggregate_unit(pe, q, EH[:, q % 2, :, :], EL[:, q % 2, :, :], 2).then_inc(att_done, 1)

                        def out_rows_of(c):
                            pe.wait_ge(copied_a, c * DK + DK)
                            pe.wait_ge(copied_e, c * DK + DK)
                            pe.wait_ge(z_added, c * NU + NU)
                            for j in range(TC):
                                if later(c * TC + j, 2):
                                    pe.wait_ge(rows_read, 2 * (c * TC + j) - 2)
                                i = slice(j * P, j * P + P)
                                for k in range(DK):
                                    pe.matmul(PS[:, 4 + j % 2, 0:D + 2], TA[:, k, i], Wgcn[:, k, :],
                                              start=(k == 0), stop=(k == DK - 1))
                                for k in range(DK):
                                    pe.matmul(PS[:, 6 + j % 2, 0:D], TE[:, k, i], Wsa[:, k, :],
                                              start=(k == 0), stop=(k == DK - 1))
                                for r in range(UJ):
                                    last = pe.matmul(PS[:, 6 + j % 2, D:D + 1], Zacc[:, r, i], ones[:, 0:1],
                                                     start=(r == 0), stop=(r == UJ - 1))
                                last.then_inc(rows_out, 1)

                        pe.wait_ge(wlr_copied, 1)
                        pe.wait_ge(left_copied, NC)
                        adj_unit(0, 0)
                        adj_unit(0, 1)
                        att_unit(0, 0)
                        adj_unit(0, 2)
                        att_unit(0, 1)
                        adj_unit(0, 3)
                        att_unit(0, 2)
                        att_unit(0, 3)

                        def chunk(c):
                            adj_unit(c, 0)
                            adj_unit(c, 1)
                            out_rows_of(c - 1)
                            att_unit(c, 0)
                            adj_unit(c, 2)
                            att_unit(c, 1)
                            adj_unit(c, 3)
                            att_unit(c, 2)
                            att_unit(c, 3)

                        chunk(1)
                        with pe.Fori(2, NC) as c:
                            chunk(c)
                        out_rows_of(NC - 1)

                    @block.vector
                    def _(v):
                        steps = Steps(v, dve_steps)
                        v.wait_ge(consts_loaded, N_CONSTS)
                        for k in range(2 * DK):
                            v.tensor_scalar(avec[:, k, :], ones[:, :], asa[:, k:k + 1], None,
                                            ALU.mult).then_inc(avec_made, 1)
                        split_features(v, steps, X, features_split)
                        v.wait_ge(wlr_copied, 1)
                        for t in range(NT):
                            steps.wait()
                            steps(v.tensor_tensor_reduce(junk[:, 0, :], X[:, t, :], wlr[:, 0, :], 1.0, 0.0,
                                                         ALU.mult, ALU.add, sl[:, t:t + 1]))
                        steps.wait()
                        for t in range(NT):
                            v.tensor_scalar(diag[:, t // TC, (t % TC) * P:(t % TC) * P + P], ident[:, :],
                                            sl[:, t:t + 1], None, ALU.mult).then_inc(diag_made, 1)
                        for t in range(NT):
                            steps.wait()
                            steps(v.tensor_tensor_reduce(junk[:, 0, :], X[:, t, :], wlr[:, 1, :], 1.0, 0.0,
                                                         ALU.mult, ALU.add, nsr[:, t:t + 1]))
                        steps.wait()
                        steps(v.tensor_scalar(nsr01[:, :], nsr[:, :], -0.01, None, ALU.mult))
                        steps.wait()
                        steps(v.tensor_scalar(nsr[:, :], nsr[:, :], -1.0, None, ALU.mult))
                        v.wait_ge(left_copied, NC)
                        steps.wait()
                        v.memset(Zacc[:, :, :], 0.0).then_inc(z_cleared, 1)

                        def gates_from_x(tiles):
                            for t in tiles:
                                for g, w in enumerate((War, Wbr)):
                                    steps.wait()
                                    steps(v.tensor_tensor_reduce(gate_junk, X[:, t, :], w[:, :], 1.0, 0.0,
                                                                 ALU.mult, ALU.add, gx[:, t, g:g + 1]))

                        def attention(c, q):
                            u = c * NU + q
                            v.wait_ge(exps, u * 2 * UJ + 2 * UJ)
                            v.tensor_tensor(Eb[:, :, :], Ea[:, :, :], Eb[:, :, :], ALU.min).then_inc(smaller, 1)
                            v.wait_ge(smaller, u + 1)
                            if later(u, 1):
                                v.wait_ge(z_added, u)
                                v.wait_ge(att_low, u)
                            v.scalar_tensor_tensor(out=EM[:, :, :].rearrange("p r w -> p (r w)"),
                                                   in0=raw[:, q % 2, :, :].rearrange("p r w -> p (r w)"),
                                                   scalar=0.0, in1=Eb[:, :, :].rearrange("p r w -> p (r w)"),
                                                   op0=ALU.not_equal, op1=ALU.mult).then_inc(att_masked, 1)
                            v.wait_ge(att_masked, u + 1)
                            if later(u, 2):
                                v.wait_ge(att_done, u - 1)
                            v.tensor_copy(EH[:, q % 2, :, :], EM[:, :, :]).then_inc(att_high, 1)
                            v.wait_ge(att_high, u + 1)
                            v.tensor_tensor(EL[:, q % 2, :, :], EM[:, :, :], EH[:, q % 2, :, :].bitcast(F32),
                                            ALU.subtract).then_inc(att_low, 1)

                        def copy_rows(c):
                            for j in range(TC):
                                t = c * TC + j
                                v.wait_ge(rows_out, t + 1)
                                v.tensor_tensor(RA[:, j, 0:D], PS[:, 4 + j % 2, 0:D], bg[:, :],
                                                ALU.add).then_inc(rows_read, 1)
                                steps(v.tensor_tensor(gate[:, j, :], PS[:, 4 + j % 2, D:D + 2],
                                                      flat(gx[:, one(t), :]), ALU.add))
                                v.tensor_copy(RE[:, j, :], PS[:, 6 + j % 2, 0:D + 1]).then_inc(rows_read, 1)
                            steps.wait()
                            for g in range(2):
                                ins = v.tensor_scalar(gate[:, :, g], gate[:, :, g], gate_b[:, g:g + 1], None, ALU.add)
                                steps(ins) if g == 0 else ins.then_inc(gates_in, 1)

                        def mix_rows(c):
                            v.wait_ge(rows_read, 2 * TC * (c + 1))
                            steps(v.tensor_scalar(zr[:, :], RE[:, :, D], EPS_ATT, None, ALU.add))
                            steps.wait()
                            steps(v.reciprocal(zr[:, :], zr[:, :]))
                            v.wait_ge(gates_tanh, c + 1)
                            steps(v.tensor_scalar(gate[:, :, :], gate[:, :, :], 0.5, 0.5, ALU.mult, ALU.add))
                            steps.wait()
                            steps(v.tensor_tensor(zr[:, :], zr[:, :], gate[:, :, 0], ALU.mult))
                            steps.wait()
                            for j in range(TC):
                                steps(v.tensor_scalar(RE[:, j, 0:D], RE[:, j, 0:D], zr[:, j:j + 1], None, ALU.mult))
                            steps.wait()
                            for j in range(TC):
                                ins = v.scalar_tensor_tensor(out=RA[:, j, 0:D], in0=RA[:, j, 0:D],
                                                             scalar=gate[:, j, 1:2], in1=RE[:, j, 0:D],
                                                             op0=ALU.mult, op1=ALU.add)
                                steps(ins) if j < TC - 1 else ins.then_inc(mix_in, 1)

                        def take_rows(c):
                            v.wait_ge(mix_tanh, c + 1)
                            steps(v.tensor_scalar(RA[:, :, 0:D], RA[:, :, 0:D], 0.5, 0.5, ALU.mult, ALU.add))
                            steps.wait()
                            Xc = X[:, bass.ds(c * TC, TC), :]
                            steps(v.tensor_tensor(Xc, Xc, RA[:, :, 0:D], ALU.add))
                            for j in range(TC):
                                wait_apart(v, steps.semaphore, steps.base + steps.count)
                                row_stats(v, steps, c * TC + j)

                        PER_CHUNK = TC + 1 + 4 + TC + (TC - 1) + 2 + TC
                        gate_junk = RE[:, 0, 0:D]

                        attention(0, 0)
                        gates_from_x(range(0, 8))
                        attention(0, 1)
                        gates_from_x(range(8, NT))
                        attention(0, 2)
                        attention(0, 3)
                        steps.wait()
                        entry = steps.count
                        with v.Fori(1, NC) as c:
                            steps.restart(entry + (c - 1) * PER_CHUNK)
                            copy_rows(c - 1)
                            v.memset(Zacc[:, :, :], 0.0).then_inc(z_cleared, 1)
                            attention(c, 0)
                            attention(c, 1)
                            mix_rows(c - 1)
                            attention(c, 2)
                            take_rows(c - 1)
                            assert steps.count == PER_CHUNK
                            attention(c, 3)
                        steps.restart(entry + (NC - 1) * PER_CHUNK)
                        copy_rows(NC - 1)
                        mix_rows(NC - 1)
                        take_rows(NC - 1)
                        norm_rows(v, steps, var_ready, roots_ready, tiles_normed)

        gcn_layer("0", True)
        attention_layer()
        gated_layer()
        gcn_layer("3", False)


def kernel(x, adj, L0_gnn_W, L0_gnn_b, L1_gnn_weight, L1_gnn_bias, L1_gnn_node_w, L1_gnn_edge_w,
           L2_gnn_W_sa, L2_gnn_a_sa, L2_gnn_W_gcnb, L2_gnn_b_gcnb, L2_gnn_Wa, L2_gnn_ba, L2_gnn_Wb,
           L2_gnn_bb, L3_gnn_W, L3_gnn_b):
    import numpy as np
    import concourse.bacc as bacc
    from concourse.bass_utils import run_bass_kernel_spmd

    arrays = {
        "x": x, "adj": adj, "adjT": np.transpose(adj), "W0T": np.transpose(L0_gnn_W), "b0": L0_gnn_b,
        "weight": L1_gnn_weight, "b1": L1_gnn_bias, "node_w": L1_gnn_node_w, "edge_w": L1_gnn_edge_w,
        "W_sa": L2_gnn_W_sa, "W_saT": np.transpose(L2_gnn_W_sa), "a_sa": L2_gnn_a_sa,
        "W_gcnb": L2_gnn_W_gcnb, "b_gcnb": L2_gnn_b_gcnb, "Wa": L2_gnn_Wa, "ba": L2_gnn_ba,
        "Wb": L2_gnn_Wb, "bb": L2_gnn_bb, "W3T": np.transpose(L3_gnn_W), "b3": L3_gnn_b,
    }
    arrays = {name: np.ascontiguousarray(a) for name, a in arrays.items()}
    nc = bacc.Bacc("TRN2", target_bir_lowering=False, num_devices=1)
    T = {name: nc.dram_tensor(name, a.shape, mybir.dt.from_np(a.dtype), kind="ExternalInput").ap()
         for name, a in arrays.items()}
    T["out"] = nc.dram_tensor("out", (N, D), F32, kind="ExternalOutput").ap()
    graph_kernel(nc, T)
    r = run_bass_kernel_spmd(nc, [arrays], core_ids=[0])
    return r.results[0]["out"]
```

```python
from contextlib import ExitStack

import concourse.bass as bass
from concourse import mybir

F32 = mybir.dt.float32
F32R = mybir.dt.float32r
ACT = mybir.ActivationFunctionType
ALU = mybir.AluOpType
AX_X = mybir.AxisListType.X
RMAX = bass.bass_isa.ReduceOp.max
RADD = bass.bass_isa.ReduceOp.add

P = 128
N = 2048
D = 256
NT = N // P
DK = D // P
CW = 512
NC = N // CW
TC = CW // P
UJ = 4
NU = NT // UJ
HJ = 2
NH = NT // HJ
SLOTS0 = 4
HS = 4
EPS_DEG = 1e-8
EPS_LN = 1e-5
EPS_ATT = 1e-5
NEG_BIG = -9000000000000000.0


class Steps:

    def __init__(self, engine, semaphore):
        self.engine, self.semaphore, self.base, self.count = engine, semaphore, 0, 0

    def __call__(self, instruction):
        instruction.then_inc(self.semaphore, 1)
        self.count += 1

    def wait(self):
        self.engine.wait_ge(self.semaphore, self.base + self.count)

    def restart(self, base):
        self.base, self.count = base, 0


def flat(ap):
    return ap.rearrange("p o d -> p (o d)")


def one(t):
    return bass.ds(t, 1)


def later(index, least):
    return not isinstance(index, int) or index >= least



class Parts:

    def __init__(self):
        self.of = {"sync": [], "scalar": [], "vector": [], "tensor": [], "gpsimd": []}

    def sync(self, part):
        self.of["sync"].append(part)

    def scalar(self, part):
        self.of["scalar"].append(part)

    def vector(self, part):
        self.of["vector"].append(part)

    def tensor(self, part):
        self.of["tensor"].append(part)

    def gpsimd(self, part):
        self.of["gpsimd"].append(part)

    def run(self, nc):
        with nc.Block() as block:
            @block.sync
            def _(sp):
                for part in self.of["sync"]:
                    part(sp)

            @block.scalar
            def _(act):
                for part in self.of["scalar"]:
                    part(act)

            @block.vector
            def _(v):
                for part in self.of["vector"]:
                    part(v)

            @block.tensor
            def _(pe):
                for part in self.of["tensor"]:
                    part(pe)

            @block.gpsimd
            def _(pool):
                for part in self.of["gpsimd"]:
                    part(pool)


def graph_kernel(nc, T):
    with ExitStack() as ctx:
        def sb(stack, name, shape, dt=F32):
            return stack.enter_context(nc.sbuf_tensor(name, shape, dt))

        def sem(name):
            return ctx.enter_context(nc.semaphore(name))

        X = sb(ctx, "X", [P, NT, D])
        UH = sb(ctx, "UH", [P, NT, D], F32R)
        UL = sb(ctx, "UL", [P, NT, D], F32R)
        ring = sb(ctx, "ring", [P, NT, CW])
        GW = sb(ctx, "GW", [P, 4, D])
        ident = sb(ctx, "ident", [P, P])
        ones = sb(ctx, "ones", [P, P])
        deg = sb(ctx, "deg", [P, NT])
        dis = sb(ctx, "dis", [P, NT])
        mhalf = sb(ctx, "mhalf", [P, TC])
        dots = sb(ctx, "dots", [P, NT, 4])
        asa = sb(ctx, "asa", [P, 2 * DK])
        stats = sb(ctx, "stats", [P, NT, 6])
        mv = sb(ctx, "mv", [P, NT, 2])
        rstd = sb(ctx, "rstd", [P, NT])
        PS = ctx.enter_context(nc.psum_tensor("PS", [P, 8, CW], F32))

        flat_ring = ring[:, :, :].rearrange("p a b -> p (a b)")
        adj_units = T["adjT"].rearrange("(q r p) n -> q p r n", r=UJ, p=P)
        adj_rows = T["adj"].rearrange("(t p) n -> t p n", p=P)
        x_rows = T["x"].rearrange("(t p) d -> p t d", p=P)
        out_rows = T["out"].rearrange("(t p) d -> p t d", p=P)

        parts = Parts()
        made = sem("const_made")
        gw_loaded, avec_made, wlr_out, gw_made = sem("gw_loaded"), sem("avec_made"), sem("wlr_out"), sem("gw_made")
        dve_steps = sem("dve_steps")
        steps = Steps(nc.vector, dve_steps)

        def load_all(sp, plan, loaded):
            for dst, src in plan:
                sp.dma_start(dst, src, allow_slow_non_contiguous=True).then_inc(loaded, 16)

        def weight(name):
            return T[name].rearrange("(k p) n -> p k n", p=P)

        def wait_apart(eng, semaphore, value):
            if not isinstance(value, int):
                value = eng.snap(value)
                eng.compute_val(value)
            eng.wait_ge(made, 4)
            eng.wait_ge(semaphore, value)

        def split_unit(v, src, q, features_split):
            t = slice(UJ * q, UJ * q + UJ)
            steps(v.tensor_copy(UH[:, t, :], src[:, t, :]))
            steps.wait()
            v.tensor_tensor(UL[:, t, :], src[:, t, :], UH[:, t, :].bitcast(F32),
                            ALU.subtract).then_inc(features_split, 1)

        def tile_product(pe, jt, mh, ml, bank):
            last = None
            for k in range(DK):
                fc = slice(k * P, k * P + P)
                for n, (u, m) in enumerate(((UH, mh), (UH, ml), (UL, mh))):
                    last = pe.matmul(PS[:, bank + k, :], u[:, jt, fc], m,
                                     start=(jt == 0 and n == 0), stop=(jt == NT - 1 and n == 2))
            return last

        def half_unit(pe, h, mh, ml, bank):
            for r in range(HJ):
                last = tile_product(pe, HJ * h + r, mh[:, r, :], ml[:, r, :], bank)
            return last

        def small_product(pe, bank, TT, W, j, width=D):
            for k in range(DK):
                last = pe.matmul(PS[:, bank, 0:width], TT[:, k, j * P:j * P + P], W[:, k, :],
                                 start=(k == 0), stop=(k == DK - 1))
            return last

        def variances(v, tiles, var_ready):
            for j, t in enumerate(tiles):
                wait_apart(v, steps.semaphore, steps.base + steps.count)
                steps(v.bn_stats(stats[:, j, :], flat(X[:, one(t), :])))
            wait_apart(v, steps.semaphore, steps.base + steps.count)
            for j in range(len(tiles)):
                steps(v.bn_aggr(mv[:, j, :], stats[:, j, :]))
            steps.wait()
            n = len(tiles)
            v.tensor_scalar(rstd[:, 0:n], mv[:, 0:n, 1], EPS_LN, None, ALU.add).then_inc(var_ready, 1)

        def inverse_roots(pool, n, index, var_ready, roots_ready):
            pool.wait_ge(var_ready, index + 1)
            pool.tensor_tensor(rstd[:, 0:n], rstd[:, 0:n], mhalf[:, 0:n], ALU.pow).then_inc(roots_ready, 1)

        def normalise(v, tiles, index, roots_ready, normed):
            v.wait_ge(roots_ready, index + 1)
            for j, t in enumerate(tiles):
                Xt = flat(X[:, one(t), :])
                v.tensor_scalar(Xt, Xt, mv[:, j, 0:1], rstd[:, j:j + 1],
                                ALU.subtract, ALU.mult).then_inc(normed, 1)

        def chunk_tiles(c):
            return [c * TC + j for j in range(TC)]

        normed0 = sem("normed_0")
        with ExitStack() as lay:
            A = [ring] + [sb(lay, f"A{c}", [P, NT, CW]) for c in range(1, NC)]
            MH = sb(lay, "MH0", [P, SLOTS0, CW], F32R)
            ML = sb(lay, "ML0", [P, SLOTS0, CW], F32R)
            TT = sb(lay, "TT0", [P, DK, CW])
            W0T = sb(lay, "W0T_sb", [P, DK, D])
            bias0 = sb(lay, "bias0", [P, D])
            avec = GW[:, 2:4, :].rearrange("p a d -> p (a d)")

        order = [(q, c) for n in range(NC - 1) for q, c in
                 [(q, n) for q in range(n)] + [(n, c) for c in range(n + 1)]]
        order += [(NU - 1, c) for c in range(NC - 1)] + [(q, NC - 1) for q in range(NU)]
        products0 = [(UJ * q + i, c) for q, c in order for i in range(UJ)]
        stage_end = [sum(max(q, c) <= n for q, c in order) * UJ for n in range(NC)]
        first_tile = {c: min(n for n, p in enumerate(products0) if p[1] == c) for c in range(NC)}
        last_tile = {c: max(n for n, p in enumerate(products0) if p[1] == c) for c in range(NC)}
        degrees_after = {1: stage_end[0] - 1, 2: stage_end[1] - 4, 3: stage_end[2] - 11}
        AHEAD = SLOTS0

        x_loaded = [sem(f"x_loaded{q}") for q in range(NU)]
        w0_loaded = sem("w0_loaded")
        a_loaded = [[sem(f"a_loaded{c}_{q}") for q in range(NU)] for c in range(NC)]
        deg_even, deg_odd = sem("deg_even"), sem("deg_odd")
        deg_out, deg_read, dis_ready = sem("deg_out"), sem("deg_read"), sem("dis_ready")
        scaled_high, features0, bias_added0 = sem("scaled_high"), sem("features_0"), sem("bias_added_0")
        high0, low0, done0 = sem("high_0"), sem("low_0"), sem("done_0")
        copied0, rows_out0, rows_read0 = sem("copied_0"), sem("rows_out_0"), sem("rows_read_0")
        var0, roots0 = sem("var_0"), sem("roots_0")
        ADDS = NT // 2 - 1

        def add_degrees(eng, c, q, odd, added):
            a = A[c]
            t = UJ * q + odd
            eng.wait_ge(a_loaded[c][q], 16)
            if q == 0:
                if c:
                    eng.wait_ge(deg_out, c)
                eng.tensor_tensor(TT[:, odd, :], a[:, t, :], a[:, t + 2, :], ALU.add).then_inc(added, 1)
            else:
                for i in range(2):
                    eng.wait_ge(added, c * ADDS + 2 * q - 1 + i)
                    eng.tensor_tensor(TT[:, odd, :], TT[:, odd, :], a[:, t + 2 * i, :],
                                      ALU.add).then_inc(added, 1)

        @parts.sync
        def _(sp):
            sp.dma_start(asa[:, :], T["a_sa"][0, :].rearrange("(k p) -> p k", p=P),
                         allow_slow_non_contiguous=True).then_inc(gw_loaded, 16)
            sp.dma_start(W0T[:, :, :], weight("W_saT")).then_inc(gw_loaded, 16)
            for c in range(NC):
                for q in range(NU):
                    sp.dma_start(A[c][:, UJ * q:UJ * q + UJ, :], adj_units[q, :, :, c * CW:c * CW + CW])\
                        .then_inc(a_loaded[c][q], 16)
                t = slice(TC * c, TC * c + TC)
                sp.dma_start(X[:, t, :], x_rows[:, t, :]).then_inc(x_loaded[c], 16)
                if c == 0:
                    sp.wait_ge(wlr_out, 1)
                    load_all(sp, [(W0T[:, :, :], weight("W0T")),
                                  (bias0[:, :], T["b0"].partition_broadcast(P)),
                                  (GW[:, 2, :], T["Wa"][0, D:2 * D].partition_broadcast(P)),
                                  (GW[:, 3, :], T["Wb"][0, D:2 * D].partition_broadcast(P))], w0_loaded)

        @parts.gpsimd
        def _(pool):
            pool.memset(ones[:, :], 1.0).then_inc(made, 1)
            pool.memset(ident[:, :], 0.0).then_inc(made, 1)
            pool.memset(mhalf[:, :], -0.5).then_inc(made, 1)
            pool.wait_ge(made, 3)
            pool.affine_select(out=ident[:, :], in_=ident[:, :], compare_op=ALU.not_equal, fill=1.0,
                               base=0, pattern=[[-1, P]], channel_multiplier=1).then_inc(made, 1)
            for c in range(NC):
                for q in range(NU):
                    add_degrees(pool, c, q, 1, deg_odd)
                t = slice(TC * c, TC * c + TC)
                pool.wait_ge(made, 4)
                pool.wait_ge(deg_read, 2 * c + 2)
                pool.tensor_tensor(dis[:, t], dis[:, t], mhalf[:, :], ALU.pow).then_inc(dis_ready, 1)
            pool.wait_ge(w0_loaded, 64)
            for t in range(NT):
                if t % TC == 0:
                    pool.wait_ge(features0, t // TC + 1)
                pool.tensor_tensor(X[:, t, :], X[:, t, :], bias0[:, :], ALU.add).then_inc(bias_added0, 1)
            for c in range(NC):
                inverse_roots(pool, TC, c, var0, roots0)

        @parts.scalar
        def _(act):
            def scale_features(c):
                act.wait_ge(x_loaded[c], 16)
                act.wait_ge(dis_ready, c + 1)
                for j in chunk_tiles(c):
                    act.activation(UH[:, j, :], X[:, j, :], ACT.Copy, scale=dis[:, j:j + 1])\
                        .then_inc(scaled_high, 1)

            def copy_aggregate(c):
                act.wait_ge(done0, last_tile[c] + 1)
                if c == 0:
                    act.wait_ge(deg_out, NC)
                else:
                    act.wait_ge(rows_out0, c * TC)
                for k in range(DK):
                    act.activation(TT[:, k, :], PS[:, 2 * c + k, :], ACT.Copy).then_inc(copied0, 1)

            def high(n):
                t, c = products0[n]
                act.wait_ge(a_loaded[c][t // UJ], 16)
                if n >= SLOTS0:
                    act.wait_ge(done0, n - SLOTS0 + 1)
                act.activation(MH[:, n % SLOTS0, :], A[c][:, t, :], ACT.Copy).then_inc(high0, 1)

            for n in range(len(products0)):
                if n == AHEAD - 1:
                    scale_features(0)
                for c in range(1, NC):
                    if n == degrees_after[c] + AHEAD:
                        scale_features(c)
                high(n)
                for c in range(NC - 1):
                    if n == last_tile[c] + AHEAD - 1:
                        copy_aggregate(c)
            copy_aggregate(NC - 1)

        @parts.tensor
        def _(pe):
            pe.wait_ge(gw_loaded, 32)
            pe.wait_ge(avec_made, 2 * DK)
            for h in range(2):
                for k in range(DK):
                    last = pe.matmul(PS[:, 7, h * D:h * D + D], avec[:, (2 * h + k) * P:(2 * h + k) * P + P],
                                     W0T[:, k, :], start=(k == 0), stop=(k == DK - 1))
            last.then_inc(wlr_out, 1)

            def degrees(c):
                pe.wait_ge(deg_even, (c + 1) * ADDS)
                pe.wait_ge(deg_odd, (c + 1) * ADDS)
                if c:
                    pe.wait_ge(deg_read, 2 * c)
                for j in range(TC):
                    for r in range(2):
                        last = pe.matmul(PS[:, 6, j:j + 1], TT[:, r, j * P:j * P + P], ones[:, 0:1],
                                         start=(r == 0), stop=(r == 1))
                last.then_inc(deg_out, 1)

            def product(n):
                t, c = products0[n]
                pe.wait_ge(features0, t // UJ + 1)
                pe.wait_ge(low0, n + 1)
                if n == first_tile[NC - 1]:
                    pe.wait_ge(deg_read, 2 * NC)
                    pe.wait_ge(gw_made, 1)
                tile_product(pe, t, MH[:, n % SLOTS0, :], ML[:, n % SLOTS0, :], 2 * c).then_inc(done0, 1)

            def small(c, j):
                if j == 0:
                    pe.wait_ge(copied0, DK * (c + 1))
                    pe.wait_ge(w0_loaded, 64)
                if j >= 2:
                    pe.wait_ge(rows_read0, TC * c + j - 1)
                small_product(pe, 2 * c + j % 2, TT, W0T, j).then_inc(rows_out0, 1)

            degrees(0)
            for n in range(len(products0)):
                product(n)
                for c in range(NC - 1):
                    if n == last_tile[c] + 2:
                        small(c, 0)
                        small(c, 1)
                    if n == last_tile[c] + 4:
                        small(c, 2)
                        small(c, 3)
                for c in range(1, NC):
                    if n == degrees_after[c]:
                        degrees(c)
            for j in range(TC):
                small(NC - 1, j)

        @parts.vector
        def _(v):
            v.wait_ge(gw_loaded, 32)
            v.wait_ge(made, 4)
            for k in range(2 * DK):
                v.tensor_scalar(avec[:, k * P:k * P + P], ones[:, :], asa[:, k:k + 1], None,
                                ALU.mult).then_inc(avec_made, 1)
            v.wait_ge(wlr_out, 1)
            v.tensor_copy(GW[:, 0:2, :], PS[:, 7, :].rearrange("p (a d) -> p a d", a=2)).then_inc(gw_made, 1)

            def degree_columns(c):
                t = slice(TC * c, TC * c + TC)
                v.wait_ge(deg_out, c + 1)
                v.tensor_scalar(dis[:, t], PS[:, 6, 0:TC], EPS_DEG, None, ALU.add).then_inc(deg_read, 1)
                v.tensor_copy(deg[:, t], PS[:, 6, 0:TC]).then_inc(deg_read, 1)

            def features_low(c):
                v.wait_ge(scaled_high, TC * (c + 1))
                for j in chunk_tiles(c):
                    ins = v.scalar_tensor_tensor(out=UL[:, j, :], in0=X[:, j, :], scalar=dis[:, j:j + 1],
                                                 in1=UH[:, j, :].bitcast(F32), op0=ALU.mult, op1=ALU.subtract)
                    if j % TC < TC - 1:
                        steps(ins)
                    else:
                        ins.then_inc(features0, 1)

            def low(n):
                t, c = products0[n]
                v.wait_ge(high0, n + 1)
                v.tensor_tensor(ML[:, n % SLOTS0, :], A[c][:, t, :], MH[:, n % SLOTS0, :].bitcast(F32),
                                ALU.subtract).then_inc(low0, 1)

            def take_rows(c, j):
                t = TC * c + j
                v.wait_ge(rows_out0, t + 1)
                v.wait_ge(bias_added0, t + 1)
                v.scalar_tensor_tensor(out=X[:, t, :], in0=PS[:, 2 * c + j % 2, 0:D], scalar=dis[:, t:t + 1],
                                       in1=X[:, t, :], op0=ALU.mult, op1=ALU.add).then_inc(rows_read0, 1)

            def row_variances(c):
                v.wait_ge(rows_read0, TC * (c + 1))
                if c:
                    v.wait_ge(normed0, TC * c)
                variances(v, chunk_tiles(c), var0)

            for q in range(NU):
                add_degrees(v, 0, q, 0, deg_even)
            degree_columns(0)
            adds = {AHEAD - 4: (1, 0), AHEAD - 3: (1, 1), AHEAD - 2: (1, 2), AHEAD - 1: (1, 3)}
            for c, gap in ((2, 1), (3, 2)):
                for q in range(NU):
                    adds[stage_end[c - 2] + AHEAD + 1 + gap * q] = (c, q)
            for n in range(len(products0)):
                if n == AHEAD - 1:
                    features_low(0)
                for c in range(1, NC):
                    if n == degrees_after[c] + AHEAD - (c > 1):
                        degree_columns(c)
                    if n == degrees_after[c] + AHEAD:
                        features_low(c)
                low(n)
                if n in adds:
                    add_degrees(v, *adds[n], 0, deg_even)
                for c in range(NC - 1):
                    if n == last_tile[c] + AHEAD + 2:
                        take_rows(c, 0)
                        take_rows(c, 1)
                    if n == last_tile[c] + AHEAD + 4:
                        take_rows(c, 2)
                        take_rows(c, 3)
                        row_variances(c)
                    if n == last_tile[c] + AHEAD + 6:
                        normalise(v, chunk_tiles(c), c, roots0, normed0)
            for j in range(TC):
                take_rows(NC - 1, j)
            row_variances(NC - 1)
            normalise(v, chunk_tiles(NC - 1), NC - 1, roots0, normed0)

        normed1, dots_taken = sem("normed_1"), sem("dots_taken")
        summed, weighted = sem("summed"), sem("weighted")
        with ExitStack() as lay:
            Wedge = sb(lay, "Wedge", [P, DK, D])
            Wsup = sb(lay, "Wsup", [P, DK, D])
            nodew = sb(lay, "nodew", [P, D])
            bias1 = sb(lay, "bias1", [P, D])
            XT = sb(lay, "XT", [P, DK, N])
            HH = sb(lay, "HH", [P, DK, N], F32R)
            HL = sb(lay, "HL", [P, DK, N], F32R)
            bias_m = sb(lay, "bias_m", [P, N])
            WH = sb(lay, "WH", [P, NT, P], F32R)
            WL = sb(lay, "WL", [P, NT, P], F32R)
            SH = sb(lay, "SH", [P, 2, DK, P], F32R)
            SL = sb(lay, "SL", [P, 2, DK, P], F32R)
            row_dots = sb(lay, "row_dots", [P, 4, D])
            logit = sb(lay, "logit", [P, NT])
            natt = sb(lay, "natt", [P, NT])
            small1 = sb(lay, "small1", [P, 8])
            mx = sb(lay, "mx", [P, 2, NC])
            nmax = sb(lay, "nmax", [P, 2])
            Z = sb(lay, "Z", [P, 2])
            scale1 = sb(lay, "scale1", [P, 2])
        arow = flat_ring[:, 0:2 * N].rearrange("p (s n) -> p s n", s=2)
        S = flat_ring[:, 2 * N:4 * N].rearrange("p (s n) -> p s n", s=2)

        w1_loaded = sem("w1_loaded")
        arow_loaded = [sem(f"arow_loaded{i}") for i in range(2)]
        job_done, job_act, job_dve = sem("job_done"), sem("job_act"), sem("job_dve")
        logits_ready, logit_max, logit_gmax = sem("logits_ready"), sem("logit_max"), sem("logit_gmax")
        logit_exp, logit_sum = sem("logit_exp"), sem("logit_sum")
        staged = sem("staged")
        scored = sem("scored")
        masked = sem("masked")
        max_ready, exp_ready = sem("max_ready"), sem("exp_ready")
        turned = sem("turned")
        turned_high, turned_low = sem("turned_high"), sem("turned_low")
        rows_read1 = sem("rows_read_1")
        var1, roots1, multiplied = sem("var_1"), sem("roots_1"), sem("multiplied")

        jobs = []
        for some in (range(NC - 1), range(NC - 1, NC)):
            for kind in ("turn", "edge"):
                jobs += [(kind, c, k) for c in some for k in range(DK)]
            jobs += [("support", t, 0) for c in some for t in range(c * TC, c * TC + TC, 2)]
        split_count = [sum(j[0] != "turn" for j in jobs[:n + 1]) for n in range(len(jobs))]
        turns_done = {c: max(n for n, j in enumerate(jobs) if j[:2] == ("turn", c)) + 1 for c in range(NC)}
        BANKS1 = 6

        def job_target(job):
            kind, i, k = job
            cols = slice(i * CW, i * CW + CW)
            if kind == "turn":
                return XT[:, k, cols], None
            if kind == "edge":
                return HH[:, k, cols], HL[:, k, cols]
            return (UH[:, i:i + 2, :].rearrange("p t d -> p (t d)"),
                    UL[:, i:i + 2, :].rearrange("p t d -> p (t d)"))

        @parts.sync
        def _(sp):
            sp.wait_ge(high0, last_tile[0] + 1)
            sp.wait_ge(low0, last_tile[0] + 1)
            sp.wait_ge(deg_odd, 2 * ADDS)

            def load(t, s):
                if later(t, 2):
                    sp.wait_ge(weighted, t - 1)
                sp.dma_start(arow[:, s, :], adj_rows[one(t), :, :].rearrange("o p n -> (o p) n"))\
                  .then_inc(arow_loaded[s], 16)

            load(0, 0)
            load(1, 1)
            sp.wait_ge(high0, last_tile[1] + 1)
            sp.wait_ge(low0, last_tile[1] + 1)
            load_all(sp, [(Wedge[:, :, :], weight("edge_w")), (Wsup[:, :, :], weight("weight")),
                          (nodew[:, :], T["node_w"].rearrange("d o -> (d o)").partition_broadcast(P)),
                          (bias1[:, :], T["b1"].partition_broadcast(P))], w1_loaded)
            with sp.Fori(1, NT // 2) as g:
                load(g * 2, 0)
                load(g * 2 + 1, 1)

        @parts.tensor
        def _(pe):
            pe.wait_ge(w1_loaded, 64)
            for n, (kind, i, k) in enumerate(jobs):
                if n >= BANKS1:
                    pe.wait_ge(job_act, n - BANKS1 + 1)
                    if split_count[n - BANKS1]:
                        pe.wait_ge(job_dve, split_count[n - BANKS1])
                bank = PS[:, n % BANKS1, :]
                if kind == "turn":
                    pe.wait_ge(normed0, TC * i + TC)
                    for j in range(TC):
                        last = pe.transpose(bank[:, j * P:j * P + P],
                                            X[:, i * TC + j, k * P:k * P + P], ident[:, :])
                elif kind == "edge":
                    pe.wait_ge(job_act, turns_done[i])
                    for kk in range(DK):
                        last = pe.matmul(bank, Wedge[:, kk, k * P:k * P + P],
                                         XT[:, kk, i * CW:i * CW + CW],
                                         start=(kk == 0), stop=(kk == DK - 1))
                else:
                    for h in range(2):
                        for kk in range(DK):
                            last = pe.matmul(bank[:, h * D:h * D + D],
                                             XT[:, kk, (i + h) * P:(i + h) * P + P], Wsup[:, kk, :],
                                             start=(kk == 0), stop=(kk == DK - 1))
                last.then_inc(job_done, 1)

            def score(t, s, c):
                if c == 0:
                    pe.wait_ge(staged, t + 1)
                if later(t, 1):
                    pe.wait_ge(masked, (t - 1) * NC + c + 1)
                cols = slice(c * CW, c * CW + CW)
                for k in range(DK):
                    for n, (a, b) in enumerate(((SH, HH), (SH, HL), (SL, HH))):
                        last = pe.matmul(PS[:, c, :], a[:, s, k, :], b[:, k, cols],
                                         start=(k == 0 and n == 0), stop=(k == DK - 1 and n == 2))
                last.then_inc(scored, 1)

            def turn(t, s, g):
                if g == 0:
                    pe.wait_ge(weighted, t + 1)
                if later(t * NU + g, 2):
                    pe.wait_ge(turned_high, t * NU + g - 1)
                    pe.wait_ge(turned_low, t * NU + g - 1)
                for r in range(UJ):
                    jt = UJ * g + r
                    last = pe.transpose(PS[:, 4 + g % 2, r * P:r * P + P],
                                        S[:, s, jt * P:jt * P + P], ident[:, :])
                last.then_inc(turned, 1)

            def weigh(t, s):
                if later(t, 2):
                    pe.wait_ge(rows_read1, t - 1)
                for g in range(NU):
                    pe.wait_ge(turned_low, t * NU + g + 1)
                    for r in range(UJ):
                        jt = UJ * g + r
                        for n, (w, u) in enumerate(((WH, UH), (WH, UL), (WL, UH))):
                            last = pe.matmul(PS[:, 6 + s, 0:D], w[:, jt, :], u[:, jt, :],
                                             start=(jt == 0 and n == 0),
                                             stop=(jt == NT - 1 and n == 2))
                last.then_inc(summed, 1)

            def tile(t, s):
                score(t, s, 0)
                score(t, s, 1)
                turn(t - 1, 1 - s, 0)
                score(t, s, 2)
                turn(t - 1, 1 - s, 1)
                score(t, s, 3)
                turn(t - 1, 1 - s, 2)
                turn(t - 1, 1 - s, 3)
                weigh(t - 1, 1 - s)

            pe.wait_ge(job_act, len(jobs))
            pe.wait_ge(job_dve, split_count[-1])
            for c in range(NC):
                score(0, 0, c)
            tile(1, 1)
            tile(2, 0)
            with pe.Fori(1, NT // 2 - 1) as g:
                tile(g * 2 + 1, 1)
                tile(g * 2 + 2, 0)
            tile(NT - 1, 1)
            for g in range(NU):
                turn(NT - 1, 1, g)
            weigh(NT - 1, 1)

        def sum_dots(act, t):
            wait_apart(act, multiplied, t * 4 + 4)
            for g in range(4):
                act.activation(row_dots[:, g, :], row_dots[:, g, :], ACT.Copy,
                               accum_out=flat(dots[:, one(t), g:g + 1])).then_inc(dots_taken, 1)

        @parts.scalar
        def _(act):
            for n, job in enumerate(jobs):
                act.wait_ge(job_done, n + 1)
                act.activation(job_target(job)[0], PS[:, n % BANKS1, :], ACT.Copy).then_inc(job_act, 1)
            act.wait_ge(logit_gmax, 1)
            act.activation(natt[:, :], logit[:, :], ACT.Exp, bias=small1[:, 2:3],
                           accum_out=small1[:, 3:4]).then_inc(logit_exp, 1)

            def exponent(t, s):
                act.wait_ge(max_ready, t + 1)
                act.activation(S[:, s, :], S[:, s, :], ACT.Exp, bias=nmax[:, s:s + 1],
                               accum_out=Z[:, s:s + 1]).then_inc(exp_ready, 1)

            def high(t, s):
                for g in range(NU):
                    act.wait_ge(turned, t * NU + g + 1)
                    act.activation(WH[:, UJ * g:UJ * g + UJ, :].rearrange("p t i -> p (t i)"),
                                   PS[:, 4 + g % 2, :], ACT.Copy).then_inc(turned_high, 1)

            exponent(0, 0)
            high(0, 0)
            exponent(1, 1)
            high(1, 1)
            exponent(2, 0)
            high(2, 0)
            exponent(3, 1)
            sum_dots(act, 0)
            high(3, 1)
            exponent(4, 0)
            sum_dots(act, 1)
            with act.Fori(2, NT // 2 - 1) as g:
                for s in (1, 0):
                    high(g * 2 + 1 - s, 1 - s)
                    exponent(g * 2 + 2 - s, s)
                    sum_dots(act, g * 2 - 1 - s)
            high(NT - 2, 0)
            exponent(NT - 1, 1)
            sum_dots(act, NT - 4)
            high_half(act, 0, 0)
            high_half(act, 0, 1)
            high(NT - 1, 1)

        @parts.gpsimd
        def _(pool):
            pool.wait_ge(logit_max, 1)
            pool.partition_all_reduce(small1[:, 1:2], small1[:, 0:1], P, RMAX).then_inc(logit_max, 1)
            pool.wait_ge(logit_exp, 1)
            pool.partition_all_reduce(small1[:, 4:5], small1[:, 3:4], P, RADD).then_inc(logit_sum, 1)

            def inverse_root(t, s):
                pool.wait_ge(var1, t + 1)
                pool.tensor_tensor(rstd[:, s:s + 1], rstd[:, s:s + 1], mhalf[:, 0:1],
                                   ALU.pow).then_inc(roots1, 1)

            def multiply(t):
                if later(t, 1):
                    pool.wait_ge(dots_taken, t * 4)
                wait_apart(pool, normed1, t + 1)
                for g in range(4):
                    pool.tensor_tensor(row_dots[:, g, :], flat(X[:, one(t), :]), GW[:, g, :],
                                       ALU.mult).then_inc(multiplied, 1)

            inverse_root(0, 0)
            inverse_root(1, 1)
            multiply(0)
            with pool.Fori(1, NT // 2 - 1) as g:
                for s in range(2):
                    inverse_root(g * 2 + s, s)
                    multiply(g * 2 + s - 1)
            inverse_root(NT - 2, 0)
            multiply(NT - 3)
            for h in range(2):
                low_half(pool, 0, h, raw_half(h))
            inverse_root(NT - 1, 1)
            multiply(NT - 2)
            multiply(NT - 1)

        @parts.vector
        def _(v):
            v.wait_ge(w1_loaded, 64)
            v.wait_ge(normed0, NT)
            for t in range(NT):
                v.tensor_tensor_reduce(S[:, t // 8, (t % 8) * D:(t % 8) * D + D], X[:, t, :],
                                       nodew[:, :], 1.0, 0.0, ALU.mult, ALU.add,
                                       logit[:, t:t + 1]).then_inc(logits_ready, 1)
            v.wait_ge(logits_ready, NT)
            v.tensor_reduce(small1[:, 0:1], logit[:, :], AX_X, ALU.max).then_inc(logit_max, 1)
            for n, job in enumerate(jobs):
                hi, lo = job_target(job)
                if lo is not None:
                    v.wait_ge(job_act, n + 1)
                    v.tensor_tensor(lo, PS[:, n % BANKS1, :], hi.bitcast(F32),
                                    ALU.subtract).then_inc(job_dve, 1)
                if n == 8:
                    v.wait_ge(logit_max, 2)
                    v.tensor_scalar(small1[:, 2:3], small1[:, 1:2], -1.0, None, ALU.mult).then_inc(logit_gmax, 1)
                if n >= 10 and n < 10 + NC - 1:
                    add_bias(v, n - 10)
            v.wait_ge(job_dve, split_count[-1])
            v.wait_ge(job_act, len(jobs))
            steps.wait()

            def stage(t, s):
                if later(t, 2):
                    v.wait_ge(scored, (t - 1) * NC)
                cols = bass.ds(t * P, P)
                steps(v.tensor_scalar(SH[:, s, :, :], HH[:, :, cols].bitcast(F32), 1.0, None, ALU.mult))
                v.tensor_scalar(SL[:, s, :, :], HL[:, :, cols].bitcast(F32), 1.0, None,
                                ALU.mult).then_inc(staged, 1)

            def mask_bias(t, s, turns):
                v.wait_ge(arow_loaded[s], turns * 16 + 16)
                steps(v.tensor_scalar(bias_m[:, :], arow[:, s, :], 0.0, NEG_BIG, ALU.is_le, ALU.mult))

            def mask(t, s, c):
                cols = slice(c * CW, c * CW + CW)
                wait_apart(v, scored, t * NC + c + 1)
                v.tensor_tensor_reduce(S[:, s, cols], PS[:, c, :], bias_m[:, cols], 1.0, -3.0e38,
                                       ALU.add, ALU.max, mx[:, s, c:c + 1]).then_inc(masked, 1)

            def row_max(t, s):
                v.wait_ge(masked, t * NC + NC)
                v.tensor_reduce(nmax[:, s:s + 1], mx[:, s, :], AX_X, ALU.max,
                                negate=True).then_inc(max_ready, 1)

            def low(t, s, g):
                v.wait_ge(turned_high, t * NU + g + 1)
                w = slice(UJ * g, UJ * g + UJ)
                v.tensor_tensor(WL[:, w, :].rearrange("p t i -> p (t i)"), PS[:, 4 + g % 2, :],
                                WH[:, w, :].rearrange("p t i -> p (t i)").bitcast(F32),
                                ALU.subtract).then_inc(turned_low, 1)

            def weight_rows(t, s):
                v.wait_ge(exp_ready, t + 1)
                v.tensor_tensor(S[:, s, :], S[:, s, :], arow[:, s, :], ALU.mult).then_inc(weighted, 1)

            def take_rows(t, s):
                steps(v.reciprocal(scale1[:, s:s + 1], Z[:, s:s + 1]))
                steps.wait()
                steps(v.tensor_tensor(scale1[:, s:s + 1], scale1[:, s:s + 1], natt[:, one(t)], ALU.mult))
                steps.wait()
                v.wait_ge(summed, t + 1)
                Xt = flat(X[:, one(t), :])
                v.scalar_tensor_tensor(out=Xt, in0=PS[:, 6 + s, 0:D], scalar=scale1[:, s:s + 1],
                                       in1=Xt, op0=ALU.mult, op1=ALU.add).then_inc(rows_read1, 1)
                wait_apart(v, rows_read1, t + 1)
                steps(v.bn_stats(stats[:, s, :], Xt))
                wait_apart(v, steps.semaphore, steps.base + steps.count)
                steps(v.bn_aggr(mv[:, s, :], stats[:, s, :]))
                steps.wait()
                v.tensor_scalar(rstd[:, s:s + 1], mv[:, s, 1:2], EPS_LN, None, ALU.add).then_inc(var1, 1)

            def normalise_tile(t, s):
                v.wait_ge(roots1, t + 1)
                Xt = flat(X[:, one(t), :])
                v.tensor_scalar(Xt, Xt, mv[:, s, 0:1], rstd[:, s:s + 1],
                                ALU.subtract, ALU.mult).then_inc(normed1, 1)

            TILE_STEPS = 6

            def tile(t, s, half):
                if later(t, 2):
                    normalise_tile(t - 2, s)
                mask(t, s, 0)
                mask(t, s, 1)
                low(t - 1, 1 - s, 0)
                mask(t, s, 2)
                low(t - 1, 1 - s, 1)
                mask(t, s, 3)
                row_max(t, s)
                low(t - 1, 1 - s, 2)
                low(t - 1, 1 - s, 3)
                if not (isinstance(t, int) and t == NT - 1):
                    stage(t + 1, 1 - s)
                    mask_bias(t + 1, 1 - s, half)
                weight_rows(t, s)
                take_rows(t - 1, 1 - s)
                steps.wait()

            stage(0, 0)
            mask_bias(0, 0, 0)
            add_bias(v, NC - 1)
            v.wait_ge(logit_sum, 1)
            steps(v.reciprocal(small1[:, 5:6], small1[:, 4:5]))
            steps.wait()
            steps(v.tensor_scalar(natt[:, :], natt[:, :], small1[:, 5:6], None, ALU.mult))
            steps.wait()
            for c in range(NC):
                mask(0, 0, c)
            row_max(0, 0)
            stage(1, 1)
            mask_bias(1, 1, 0)
            weight_rows(0, 0)
            steps.wait()
            before = steps.count
            tile(1, 1, 1)
            assert steps.count - before == TILE_STEPS
            tile(2, 0, 1)
            entry = steps.count
            with v.Fori(1, NT // 2 - 1) as g:
                steps.restart(entry + (g - 1) * (2 * TILE_STEPS))
                tile(g * 2 + 1, 1, g + 1)
                tile(g * 2 + 2, 0, g + 1)
            steps.restart(0)
            steps.count = entry + (NT // 2 - 2) * 2 * TILE_STEPS
            tile(NT - 1, 1, None)
            for g in range(NU):
                low(NT - 1, 1, g)
            normalise_tile(NT - 2, 0)
            take_rows(NT - 1, 1)
            normalise_tile(NT - 1, 1)

        def add_bias(v, c):
            v.wait_ge(job_done, turns_done[c])
            v.wait_ge(logits_ready, NT)
            for t in chunk_tiles(c):
                steps(v.tensor_tensor(X[:, t, :], X[:, t, :], bias1[:, :], ALU.add))

        with ExitStack() as lay:
            Wgcn = sb(lay, "Wgcn", [P, DK, D + 2])
            Wsa = sb(lay, "Wsa", [P, DK, D])
            W3T = sb(lay, "W3T_sb", [P, DK, D])
            bg = sb(lay, "bg", [P, D])
            bias3 = sb(lay, "bias3", [P, D])
            gate_b = sb(lay, "gate_b", [P, 2])
            MH2 = sb(lay, "MH2", [P, HS, HJ, CW], F32R)
            ML2 = sb(lay, "ML2", [P, HS, HJ, CW], F32R)
            sleft = sb(lay, "sleft", [P, N])
            EM = sb(lay, "EM", [P, 2, HJ, CW])
            TA = sb(lay, "TA", [P, DK, CW])
            EH = sb(lay, "EH", [P, HS, HJ, CW], F32R)
            Zacc = sb(lay, "Zacc", [P, CW])
            Zsum = sb(lay, "Zsum", [P, CW])
            RA = sb(lay, "RA", [P, TC, D])
            RE = sb(lay, "RE", [P, TC, D + 1])
            EL = sb(lay, "EL", [P, HS, HJ, CW], F32R)
            TE = sb(lay, "TE", [P, DK, CW])
            nsr = sb(lay, "nsr", [P, NT])
            nsr01 = sb(lay, "nsr01", [P, NT])
            gate = sb(lay, "gate", [P, TC, 2])
            zr = sb(lay, "zr", [P, TC])
        diag = TE

        def raw_half(h):
            return ring[:, HJ * (h % 4):HJ * (h % 4) + HJ, :]

        def exp_half(which, h):
            first = NT // 2 + 4 * which + HJ * (h % 2)
            return ring[:, first:first + HJ, :]

        w2_loaded, w3_loaded = sem("w2_loaded"), sem("w3_loaded")
        unit_loaded = [sem(f"unit_loaded{i}") for i in range(2)]
        unit3_loaded = [sem(f"unit3_loaded{i}") for i in range(NU)]
        high2, features2, high3, features3 = sem("high_2"), sem("features_2"), sem("high_3"), sem("features_3")
        nsr_made, diag_made, left_out, left_copied = sem("nsr_made"), sem("diag_made"), sem("left_out"), sem("left_copied")
        half_high, half_low = sem("half_high"), sem("half_low")
        exps = sem("exps")
        smaller, att_masked = sem("smaller"), sem("att_masked")
        att_high, att_low = sem("att_high"), sem("att_low")
        z_half, z_added = sem("z_half"), sem("z_added")
        adj_done, att_done = sem("adj_done"), sem("att_done")
        copied_a, copied_e = sem("copied_a"), sem("copied_e")
        rows_out2, rows_read2 = sem("rows_out_2"), sem("rows_read_2")
        gates_in, gates_tanh = sem("gates_in"), sem("gates_tanh")
        mix_in, mix_tanh = sem("mix_in"), sem("mix_tanh")
        var2, roots2, normed2 = sem("var_2"), sem("roots_2"), sem("normed_2")
        rows_out3, rows_read3, normed3, stored = sem("rows_out_3"), sem("rows_read_3"), sem("normed_3"), sem("stored")
        var3, roots3 = sem("var_3"), sem("roots_3")
        C3 = NC
        N_W2 = 16 * 9

        @parts.sync
        def _(sp):
            sp.wait_ge(job_done, len(jobs))
            plan = [(Wsa[:, :, :], weight("W_sa")), (Wgcn[:, :, 0:D], weight("W_gcnb")),
                    (bg[:, :], T["b_gcnb"].partition_broadcast(P)),
                    (gate_b[:, 0:1], T["ba"].partition_broadcast(P)),
                    (gate_b[:, 1:2], T["bb"].partition_broadcast(P))]
            for g, name in enumerate(("Wa", "Wb")):
                for k in range(DK):
                    plan.append((Wgcn[:, k, D + g:D + g + 1],
                                 T[name][0, k * P:k * P + P].rearrange("(p o) -> p o", o=1)))

            def load(c, q):
                if isinstance(c, int) and c == 0 and q < 2:
                    sp.wait_ge(weighted, NT - 1 + q)
                else:
                    sp.wait_ge(half_low, c * NH + 2 * q - 2)
                    sp.wait_ge(att_masked, c * NH + 2 * q - 2)
                sp.dma_start(ring[:, UJ * (q % 2):UJ * (q % 2) + UJ, :], adj_units[q, :, :, bass.ds(c * CW, CW)])\
                  .then_inc(unit_loaded[q % 2], 16)

            load(0, 0)
            load(0, 1)
            sp.wait_ge(job_act, len(jobs))
            sp.wait_ge(logits_ready, NT)
            load_all(sp, plan, w2_loaded)
            load_all(sp, [(W3T[:, :, :], weight("W3T")), (bias3[:, :], T["b3"].partition_broadcast(P))], w3_loaded)
            load(0, 2)
            load(0, 3)
            with sp.Fori(1, NC) as c:
                for q in range(NU):
                    load(c, q)

            def load3(c, q):
                if isinstance(c, int):
                    last = (NC - 1) * NH + 2 * (q + 2) + 2 if q < 2 else NC * NH
                    sp.wait_ge(att_masked, last)
                    if q < 2:
                        sp.wait_ge(half_low, last)
                else:
                    sp.wait_ge(half_low, c * NH + NC * NH - NH + 2 * q + 2)
                sp.dma_start(ring[:, UJ * q:UJ * q + UJ, :], adj_units[q, :, :, bass.ds(c * CW, CW)])\
                  .then_inc(unit3_loaded[q], 16)

            for q in range(NU):
                load3(0, q)
            with sp.Fori(1, NC) as c:
                for q in range(NU):
                    load3(c, q)
            for c in range(NC):
                sp.wait_ge(normed3, TC * (c + 1))
                t = slice(TC * c, TC * c + TC)
                sp.dma_start(out_rows[:, t, :], X[:, t, :]).then_inc(stored, 16)
            sp.wait_ge(stored, 16 * NC)

        def low_half(eng, c, h, raw):
            eng.wait_ge(half_high, c * NH + h + 1)
            eng.tensor_tensor(ML2[:, h % HS, :, :], raw, MH2[:, h % HS, :, :].bitcast(F32),
                              ALU.subtract).then_inc(half_low, 1)

        @parts.gpsimd
        def _(pool):
            def low(c, h):
                low_half(pool, c, h, raw_half(h))

            def add_z(c, h):
                s = h % 2
                if h:
                    pool.wait_ge(z_added, c * NH + h)
                elif later(c, 1):
                    pool.wait_ge(z_added, c * NH)
                pool.wait_ge(att_masked, c * NH + h + 1)
                if h == 0:
                    pool.tensor_tensor(Zacc[:, :], EM[:, s, 0, :], EM[:, s, 1, :], ALU.add).then_inc(z_added, 1)
                    return
                pool.tensor_tensor(Zacc[:, :], Zacc[:, :], EM[:, s, 0, :], ALU.add).then_inc(z_half, 1)
                pool.wait_ge(z_half, c * (NH - 1) + h)
                out = Zacc if h < NH - 1 else Zsum
                if h == NH - 1 and later(c, 1):
                    pool.wait_ge(rows_out2, c * TC)
                pool.tensor_tensor(out[:, :], Zacc[:, :], EM[:, s, 1, :], ALU.add).then_inc(z_added, 1)

            def chunk(c, first=0):
                if first < 3:
                    for h in range(first, 3):
                        low(c, h)
                for h in range(3, NH):
                    add_z(c, h - 3)
                    low(c, h)
                add_z(c, NH - 3)
                add_z(c, NH - 2)
                if later(c, 1):
                    inverse_roots(pool, TC, c - 1, var2, roots2)
                add_z(c, NH - 1)

            chunk(0, 2)
            with pool.Fori(1, NC) as c:
                chunk(c)
            for h in range(NH - 2):
                low_half(pool, C3, h, ring[:, HJ * h:HJ * h + HJ, :])
            inverse_roots(pool, TC, NC - 1, var2, roots2)
            for h in range(NH - 2, NH):
                low_half(pool, C3, h, ring[:, HJ * h:HJ * h + HJ, :])
            for c in range(NC):
                inverse_roots(pool, TC, c, var3, roots3)

        def high_half(act, c, h):
            act.wait_ge(unit_loaded[(h // 2) % 2], (c * 2 + h // 4) * 16 + 16)
            if later(c * NH + h, HS):
                act.wait_ge(adj_done, c * NH + h - HS + 1)
            act.activation(MH2[:, h % HS, :, :], raw_half(h), ACT.Copy).then_inc(half_high, 1)

        def split_high(act, q, normed, high):
            act.wait_ge(normed, TC * q + TC)
            t = slice(UJ * q, UJ * q + UJ)
            act.activation(UH[:, t, :], X[:, t, :], ACT.Copy).then_inc(high, 1)

        def split_low(v, q, high, features):
            v.wait_ge(high, q + 1)
            t = slice(UJ * q, UJ * q + UJ)
            v.tensor_tensor(UL[:, t, :], X[:, t, :], UH[:, t, :].bitcast(F32), ALU.subtract).then_inc(features, 1)

        @parts.scalar
        def _(act):
            def high(c, h):
                high_half(act, c, h)

            def exponents(c, h):
                if later(c * NH + h, 2):
                    wait_apart(act, att_masked, c * NH + h - 1)
                if isinstance(c, int) and c == 0:
                    act.wait_ge(nsr_made, 2 * (h // 2) + 2)
                    act.wait_ge(left_copied, 1)
                for r in range(HJ):
                    jt = HJ * h + r
                    zl = sleft[:, bass.ds(c * CW, CW)]
                    act.activation(exp_half(0, h)[:, r, :], zl, ACT.Exp, bias=nsr[:, jt:jt + 1],
                                   scale=-1.0).then_inc(exps, 1)
                    act.activation(exp_half(1, h)[:, r, :], zl, ACT.Exp, bias=nsr01[:, jt:jt + 1],
                                   scale=-0.01).then_inc(exps, 1)

            def copy_a(c):
                act.wait_ge(adj_done, c * NH + NH)
                if later(c, 1):
                    act.wait_ge(rows_out2, c * TC)
                for k in range(DK):
                    act.activation(TA[:, k, :], PS[:, k, :], ACT.Copy).then_inc(copied_a, 1)

            def copy_e(c):
                act.wait_ge(att_done, c * NH + NH)
                if later(c, 1):
                    act.wait_ge(rows_out2, c * TC)
                for k in range(DK):
                    act.activation(TE[:, k, :], PS[:, 2 + k, :], ACT.Copy).then_inc(copied_e, 1)

            def tanh_gates(c):
                act.wait_ge(gates_in, c + 1)
                act.activation(gate[:, :, :], gate[:, :, :], ACT.Tanh, scale=0.5).then_inc(gates_tanh, 1)

            def tanh_mix(c):
                act.wait_ge(mix_in, c + 1)
                act.activation(RA[:, :, :], RA[:, :, :], ACT.Tanh, scale=0.5).then_inc(mix_tanh, 1)

            def copy_left(c):
                act.wait_ge(left_out, c + 1)
                act.activation(sleft[:, c * CW:c * CW + CW], PS[:, 2 + c % 2, :], ACT.Copy).then_inc(left_copied, 1)

            act.wait_ge(summed, NT)
            for q in range(NU - 1):
                split_high(act, q, normed1, high2)
            sum_dots(act, NT - 3)
            sum_dots(act, NT - 2)
            split_high(act, NU - 1, normed1, high2)
            high(0, 2)
            copy_left(0)
            exponents(0, 0)
            high(0, 3)
            sum_dots(act, NT - 1)
            copy_left(1)
            exponents(0, 1)
            copy_left(2)
            high(0, 4)
            exponents(0, 2)
            copy_left(3)
            for h in range(5, NH):
                high(0, h)
                exponents(0, h - 2)
            exponents(0, NH - 2)
            exponents(0, NH - 1)

            def chunk(c):
                high(c, 0)
                high(c, 1)
                copy_a(c - 1)
                high(c, 2)
                high(c, 3)
                exponents(c, 0)
                copy_e(c - 1)
                exponents(c, 1)
                for h in range(4, NH):
                    high(c, h)
                    exponents(c, h - 2)
                exponents(c, NH - 2)
                tanh_gates(c - 1)
                exponents(c, NH - 1)
                tanh_mix(c - 1)

            chunk(1)
            with act.Fori(2, NC) as c:
                chunk(c)

            def high3_half(c, h):
                act.wait_ge(unit3_loaded[h // 2], c * 16 + 16)
                act.wait_ge(adj_done, c * NH + NC * NH + h - HS + 1)
                act.activation(MH2[:, h % HS, :, :], ring[:, HJ * h:HJ * h + HJ, :], ACT.Copy)\
                    .then_inc(half_high, 1)

            high3_half(0, 0)
            high3_half(0, 1)
            copy_a(NC - 1)
            high3_half(0, 2)
            high3_half(0, 3)
            copy_e(NC - 1)
            for q in range(NU - 1):
                split_high(act, q, normed2, high3)
            high3_half(0, 4)
            tanh_gates(NC - 1)
            high3_half(0, 5)
            tanh_mix(NC - 1)
            split_high(act, NU - 1, normed2, high3)
            high3_half(0, 6)
            high3_half(0, 7)

            def copy_a3(c):
                wait_apart(act, adj_done, c * NH + NC * NH + NH)
                if isinstance(c, int) and c == 0:
                    act.wait_ge(rows_out2, NC * TC)
                else:
                    wait_apart(act, rows_out3, c * TC)
                for k in range(DK):
                    act.activation(TA[:, k, :], flat(PS[:, one(c * 2 + k), :]), ACT.Copy).then_inc(copied_a, 1)

            def chunk3(c):
                for h in range(3):
                    high3_half(c, h)
                copy_a3(c - 1)
                for h in range(3, NH):
                    high3_half(c, h)

            chunk3(1)
            with act.Fori(2, NC) as c:
                chunk3(c)
            copy_a3(NC - 1)

        @parts.tensor
        def _(pe):
            def left(c):
                pe.wait_ge(diag_made, (c + 1) * TC)
                if c >= 2:
                    pe.wait_ge(left_copied, c - 1)
                pe.matmul(PS[:, 2 + c % 2, :], ones[:, :], diag[:, c % 2, :],
                          start=True, stop=True).then_inc(left_out, 1)

            def adj(c, h):
                pe.wait_ge(half_low, c * NH + h + 1)
                if isinstance(c, int) and c == 0:
                    pe.wait_ge(features2, h // 2 + 1)
                if h == 0 and later(c, 1):
                    pe.wait_ge(copied_a, c * DK)
                half_unit(pe, h, MH2[:, h % HS, :, :], ML2[:, h % HS, :, :], 0).then_inc(adj_done, 1)

            def att(c, h):
                pe.wait_ge(att_low, c * NH + h + 1)
                if h == 0:
                    if isinstance(c, int) and c == 0:
                        pe.wait_ge(left_copied, NC)
                    else:
                        pe.wait_ge(copied_e, c * DK)
                half_unit(pe, h, EH[:, h % HS, :, :], EL[:, h % HS, :, :], 2).then_inc(att_done, 1)

            def rows(c, j):
                if j == 0:
                    pe.wait_ge(copied_a, c * DK + DK)
                    pe.wait_ge(copied_e, c * DK + DK)
                    pe.wait_ge(z_added, c * NH + NH)
                if later(c * TC + j, 2):
                    pe.wait_ge(rows_read2, 2 * (c * TC + j) - 2)
                small_product(pe, 4 + j % 2, TA, Wgcn, j, D + 2)
                small_product(pe, 6 + j % 2, TE, Wsa, j)
                pe.matmul(PS[:, 6 + j % 2, D:D + 1], Zsum[:, j * P:j * P + P], ones[:, 0:1],
                          start=True, stop=True).then_inc(rows_out2, 1)

            def last_halves(c):
                adj(c, 6)
                att(c, 4)
                adj(c, 7)
                att(c, 5)
                att(c, 6)
                att(c, 7)

            for n in range(3):
                left(n)
            adj(0, 0)
            adj(0, 1)
            left(3)
            adj(0, 2)
            for h in range(3, 6):
                adj(0, h)
                att(0, h - 3)
            att(0, 3)
            last_halves(0)
            pe.wait_ge(w2_loaded, N_W2)

            def chunk(c):
                adj(c, 0)
                adj(c, 1)
                adj(c, 2)
                rows(c - 1, 0)
                att(c, 0)
                adj(c, 3)
                rows(c - 1, 1)
                att(c, 1)
                adj(c, 4)
                rows(c - 1, 2)
                att(c, 2)
                adj(c, 5)
                rows(c - 1, 3)
                att(c, 3)
                last_halves(c)

            chunk(1)
            with pe.Fori(2, NC) as c:
                chunk(c)
            for j in range(TC):
                rows(NC - 1, j)

            def adj3(c, h):
                pe.wait_ge(half_low, c * NH + NC * NH + h + 1)
                if isinstance(c, int) and c == 0:
                    pe.wait_ge(features3, h // 2 + 1)
                for r in range(HJ):
                    jt = HJ * h + r
                    for k in range(DK):
                        fc = slice(k * P, k * P + P)
                        for n, (u, m) in enumerate(((UH, MH2), (UH, ML2), (UL, MH2))):
                            last = pe.matmul(flat(PS[:, one(c * 2 + k), :]), u[:, jt, fc], m[:, h % HS, r, :],
                                             start=(jt == 0 and n == 0), stop=(jt == NT - 1 and n == 2))
                last.then_inc(adj_done, 1)

            def rows3(c, j):
                if j == 0:
                    pe.wait_ge(copied_a, c * DK + NC * DK + DK)
                if j >= 2:
                    pe.wait_ge(rows_read3, c * TC + j - 1)
                for k in range(DK):
                    last = pe.matmul(flat(PS[:, one(c * 2 + j % 2), 0:D]), TA[:, k, j * P:j * P + P],
                                     W3T[:, k, :], start=(k == 0), stop=(k == DK - 1))
                last.then_inc(rows_out3, 1)

            pe.wait_ge(w3_loaded, 32)
            for h in range(NH):
                adj3(0, h)
            with pe.Fori(1, NC) as c:
                adj3(c, 0)
                adj3(c, 1)
                rows3(c - 1, 0)
                rows3(c - 1, 1)
                adj3(c, 2)
                rows3(c - 1, 2)
                rows3(c - 1, 3)
                for h in range(3, NH):
                    adj3(c, h)
            for j in range(TC):
                rows3(NC - 1, j)

        @parts.vector
        def _(v):
            def right(q):
                t = slice(UJ * q, UJ * q + UJ)
                v.wait_ge(dots_taken, 4 * UJ * (q + 1))
                v.tensor_scalar(nsr[:, t], dots[:, t, 1], -1.0, None, ALU.mult).then_inc(nsr_made, 1)
                v.tensor_scalar(nsr01[:, t], dots[:, t, 1], -0.01, None, ALU.mult).then_inc(nsr_made, 1)

            def diagonals(c):
                if c >= 2:
                    v.wait_ge(left_out, c - 1)
                for j in range(TC):
                    v.tensor_scalar(diag[:, c % 2, j * P:j * P + P], ident[:, :],
                                    dots[:, c * TC + j, 0:1], None, ALU.mult).then_inc(diag_made, 1)

            def attention(c, h):
                u = c * NH + h
                s = h % 2
                Ea, Eb = exp_half(0, h), exp_half(1, h)
                v.wait_ge(exps, u * 4 + 4)
                v.tensor_tensor(Eb, Ea, Eb, ALU.min).then_inc(smaller, 1)
                v.wait_ge(smaller, u + 1)
                if later(u, 2):
                    v.wait_ge(z_added, u - 1)
                    v.wait_ge(att_low, u - 1)
                v.scalar_tensor_tensor(out=EM[:, s, :, :].rearrange("p r w -> p (r w)"),
                                       in0=raw_half(h).rearrange("p r w -> p (r w)"),
                                       scalar=0.0, in1=Eb.rearrange("p r w -> p (r w)"),
                                       op0=ALU.not_equal, op1=ALU.mult).then_inc(att_masked, 1)
                v.wait_ge(att_masked, u + 1)
                if later(u, HS):
                    v.wait_ge(att_done, u - HS + 1)
                v.tensor_copy(EH[:, h % HS, :, :], EM[:, s, :, :]).then_inc(att_high, 1)
                v.wait_ge(att_high, u + 1)
                v.tensor_tensor(EL[:, h % HS, :, :], EM[:, s, :, :], EH[:, h % HS, :, :].bitcast(F32),
                                ALU.subtract).then_inc(att_low, 1)

            def copy_rows(c, j):
                v.wait_ge(rows_out2, c * TC + j + 1)
                v.tensor_tensor(RA[:, j, :], PS[:, 4 + j % 2, 0:D], bg[:, :], ALU.add).then_inc(rows_read2, 1)
                steps(v.tensor_copy(gate[:, j, :], PS[:, 4 + j % 2, D:D + 2]))
                v.tensor_copy(RE[:, j, :], PS[:, 6 + j % 2, 0:D + 1]).then_inc(rows_read2, 1)

            def add_gates(c):
                steps.wait()
                v.tensor_tensor(gate[:, :, :], gate[:, :, :], dots[:, bass.ds(c * TC, TC), 2:4],
                                ALU.add).then_inc(gates_in, 1)

            def mix_rows(c):
                v.wait_ge(rows_read2, 2 * TC * (c + 1))
                steps(v.tensor_scalar(zr[:, :], RE[:, :, D], EPS_ATT, None, ALU.add))
                steps.wait()
                steps(v.reciprocal(zr[:, :], zr[:, :]))
                v.wait_ge(gates_tanh, c + 1)
                steps(v.tensor_scalar(gate[:, :, :], gate[:, :, :], 0.5, 0.5, ALU.mult, ALU.add))
                steps.wait()
                steps(v.tensor_tensor(zr[:, :], zr[:, :], gate[:, :, 0], ALU.mult))
                steps.wait()
                for j in range(TC):
                    steps(v.tensor_scalar(RE[:, j, 0:D], RE[:, j, 0:D], zr[:, j:j + 1], None, ALU.mult))
                steps.wait()
                for j in range(TC):
                    ins = v.scalar_tensor_tensor(out=RA[:, j, :], in0=RA[:, j, :],
                                                 scalar=gate[:, j, 1:2], in1=RE[:, j, 0:D],
                                                 op0=ALU.mult, op1=ALU.add)
                    steps(ins) if j < TC - 1 else ins.then_inc(mix_in, 1)

            def take_rows(c):
                v.wait_ge(mix_tanh, c + 1)
                steps(v.tensor_scalar(RA[:, :, :], RA[:, :, :], 0.5, 0.5, ALU.mult, ALU.add))
                steps.wait()
                Xc = X[:, bass.ds(c * TC, TC), :]
                steps(v.tensor_tensor(Xc, Xc, RA[:, :, :], ALU.add))
                variances(v, chunk_tiles(c), var2)

            def add_bias3(q):
                if q == 0:
                    v.wait_ge(w3_loaded, 32)
                v.wait_ge(features3, q + 1)
                for t in range(UJ * q, UJ * q + UJ):
                    steps(v.scalar_tensor_tensor(out=X[:, t, :], in0=bias3[:, :], scalar=deg[:, t:t + 1],
                                                 in1=X[:, t, :], op0=ALU.mult, op1=ALU.add))

            PER_CHUNK = TC + 4 + TC + (TC - 1) + 2 + 2 * TC

            split_low(v, 0, high2, features2)
            right(0)
            diagonals(0)
            diagonals(1)
            split_low(v, 1, high2, features2)
            right(1)
            right(2)
            diagonals(2)
            split_low(v, 2, high2, features2)
            split_low(v, 3, high2, features2)
            attention(0, 0)
            right(3)
            diagonals(3)
            for h in range(1, NH - 1):
                attention(0, h)
            v.wait_ge(w2_loaded, N_W2)
            for g in range(2):
                steps(v.tensor_scalar(dots[:, :, 2 + g], dots[:, :, 2 + g], gate_b[:, g:g + 1], None, ALU.add))
            attention(0, NH - 1)
            steps.wait()
            entry = steps.count
            with v.Fori(1, NC) as c:
                steps.restart(entry + (c - 1) * PER_CHUNK)
                attention(c, 0)
                attention(c, 1)
                for j in range(TC):
                    copy_rows(c - 1, j)
                    if j < TC - 1:
                        attention(c, 2 + j)
                add_gates(c - 1)
                attention(c, 5)
                mix_rows(c - 1)
                attention(c, 6)
                take_rows(c - 1)
                assert steps.count == PER_CHUNK, (steps.count, PER_CHUNK)
                attention(c, 7)
                normalise(v, chunk_tiles(c - 1), c - 1, roots2, normed2)
            steps.restart(0)
            steps.count = entry + (NC - 1) * PER_CHUNK
            copy_rows(NC - 1, 0)
            copy_rows(NC - 1, 1)
            split_low(v, 0, high3, features3)
            copy_rows(NC - 1, 2)
            copy_rows(NC - 1, 3)
            add_gates(NC - 1)
            split_low(v, 1, high3, features3)
            split_low(v, 2, high3, features3)
            mix_rows(NC - 1)
            take_rows(NC - 1)
            normalise(v, chunk_tiles(NC - 1), NC - 1, roots2, normed2)
            split_low(v, 3, high3, features3)
            for q in range(NU):
                add_bias3(q)
            steps.wait()
            v.wait_ge(half_low, NC * NH + NH)

            def low3(c, h):
                low_half(v, c + C3, h, ring[:, HJ * h:HJ * h + HJ, :])

            def take_rows3(c, j):
                v.wait_ge(rows_out3, c * TC + j + 1)
                Xt = flat(X[:, one(c * TC + j), :])
                v.tensor_tensor(Xt, flat(PS[:, one(c * 2 + j % 2), 0:D]), Xt, ALU.add).then_inc(rows_read3, 1)

            def row_variances3(c):
                wait_apart(v, rows_read3, c * TC + TC)
                variances(v, chunk_tiles(c), var3)

            entry = steps.count
            with v.Fori(1, NC) as c:
                steps.restart(entry + (c - 1) * (2 * TC))
                for h in range(6):
                    low3(c, h)
                take_rows3(c - 1, 0)
                take_rows3(c - 1, 1)
                low3(c, 6)
                take_rows3(c - 1, 2)
                take_rows3(c - 1, 3)
                row_variances3(c - 1)
                assert steps.count == 2 * TC
                low3(c, 7)
                normalise(v, chunk_tiles(c - 1), c - 1, roots3, normed3)
            steps.restart(0)
            steps.count = entry + (NC - 1) * 2 * TC
            for j in range(TC):
                take_rows3(NC - 1, j)
            row_variances3(NC - 1)
            normalise(v, chunk_tiles(NC - 1), NC - 1, roots3, normed3)

        parts.run(nc)


def kernel(x, adj, L0_gnn_W, L0_gnn_b, L1_gnn_weight, L1_gnn_bias, L1_gnn_node_w, L1_gnn_edge_w,
           L2_gnn_W_sa, L2_gnn_a_sa, L2_gnn_W_gcnb, L2_gnn_b_gcnb, L2_gnn_Wa, L2_gnn_ba, L2_gnn_Wb,
           L2_gnn_bb, L3_gnn_W, L3_gnn_b):
    import numpy as np
    import concourse.bacc as bacc
    from concourse.bass_utils import run_bass_kernel_spmd

    arrays = {
        "x": x, "adj": adj, "adjT": np.transpose(adj), "W0T": np.transpose(L0_gnn_W), "b0": L0_gnn_b,
        "weight": L1_gnn_weight, "b1": L1_gnn_bias, "node_w": L1_gnn_node_w, "edge_w": L1_gnn_edge_w,
        "W_sa": L2_gnn_W_sa, "W_saT": np.transpose(L2_gnn_W_sa), "a_sa": L2_gnn_a_sa,
        "W_gcnb": L2_gnn_W_gcnb, "b_gcnb": L2_gnn_b_gcnb, "Wa": L2_gnn_Wa, "ba": L2_gnn_ba,
        "Wb": L2_gnn_Wb, "bb": L2_gnn_bb, "W3T": np.transpose(L3_gnn_W), "b3": L3_gnn_b,
    }
    arrays = {name: np.ascontiguousarray(a) for name, a in arrays.items()}
    nc = bacc.Bacc("TRN2", target_bir_lowering=False, num_devices=1)
    T = {name: nc.dram_tensor(name, a.shape, mybir.dt.from_np(a.dtype), kind="ExternalInput").ap()
         for name, a in arrays.items()}
    T["out"] = nc.dram_tensor("out", (N, D), F32, kind="ExternalOutput").ap()
    graph_kernel(nc, T)
    r = run_bass_kernel_spmd(nc, [arrays], core_ids=[0])
    return r.results[0]["out"]
```

```python
from contextlib import ExitStack

import concourse.bass as bass
from concourse import mybir

F32 = mybir.dt.float32
F32R = mybir.dt.float32r
ACT = mybir.ActivationFunctionType
ALU = mybir.AluOpType
AX_X = mybir.AxisListType.X
RMAX = bass.bass_isa.ReduceOp.max
RADD = bass.bass_isa.ReduceOp.add

P = 128
N = 2048
D = 256
NT = N // P
DK = D // P
CW = 512
NC = N // CW
TC = CW // P
UJ = 4
NU = NT // UJ
HJ = 2
NH = NT // HJ
SLOTS0 = 4
HS = 4
EPS_DEG = 1e-8
EPS_LN = 1e-5
EPS_ATT = 1e-5
NEG_BIG = -9000000000000000.0


class Steps:

    def __init__(self, engine, semaphore):
        self.engine, self.semaphore, self.base, self.count = engine, semaphore, 0, 0

    def __call__(self, instruction):
        instruction.then_inc(self.semaphore, 1)
        self.count += 1

    def wait(self):
        self.engine.wait_ge(self.semaphore, self.base + self.count)

    def restart(self, base):
        self.base, self.count = base, 0


def flat(ap):
    return ap.rearrange("p o d -> p (o d)")


def one(t):
    return bass.ds(t, 1)


def later(index, least):
    return not isinstance(index, int) or index >= least



class Parts:

    def __init__(self):
        self.of = {"sync": [], "scalar": [], "vector": [], "tensor": [], "gpsimd": []}

    def sync(self, part):
        self.of["sync"].append(part)

    def scalar(self, part):
        self.of["scalar"].append(part)

    def vector(self, part):
        self.of["vector"].append(part)

    def tensor(self, part):
        self.of["tensor"].append(part)

    def gpsimd(self, part):
        self.of["gpsimd"].append(part)

    def run(self, nc):
        with nc.Block() as block:
            @block.sync
            def _(sp):
                for part in self.of["sync"]:
                    part(sp)

            @block.scalar
            def _(act):
                for part in self.of["scalar"]:
                    part(act)

            @block.vector
            def _(v):
                for part in self.of["vector"]:
                    part(v)

            @block.tensor
            def _(pe):
                for part in self.of["tensor"]:
                    part(pe)

            @block.gpsimd
            def _(pool):
                for part in self.of["gpsimd"]:
                    part(pool)


def graph_kernel(nc, T):
    with ExitStack() as ctx:
        def sb(stack, name, shape, dt=F32):
            return stack.enter_context(nc.sbuf_tensor(name, shape, dt))

        def sem(name):
            return ctx.enter_context(nc.semaphore(name))

        X = sb(ctx, "X", [P, NT, D])
        UH = sb(ctx, "UH", [P, NT, D], F32R)
        UL = sb(ctx, "UL", [P, NT, D], F32R)
        ring = sb(ctx, "ring", [P, NT, CW])
        GW = sb(ctx, "GW", [P, 4, D])
        ident = sb(ctx, "ident", [P, P])
        ones = sb(ctx, "ones", [P, P])
        deg = sb(ctx, "deg", [P, NT])
        dis = sb(ctx, "dis", [P, NT])
        mhalf = sb(ctx, "mhalf", [P, TC])
        dots = sb(ctx, "dots", [P, NT, 4])
        asa = sb(ctx, "asa", [P, 2 * DK])
        stats = sb(ctx, "stats", [P, NT, 6])
        mv = sb(ctx, "mv", [P, NT, 2])
        rstd = sb(ctx, "rstd", [P, NT])
        PS = ctx.enter_context(nc.psum_tensor("PS", [P, 8, CW], F32))

        flat_ring = ring[:, :, :].rearrange("p a b -> p (a b)")
        adj_units = T["adjT"].rearrange("(q r p) n -> q p r n", r=UJ, p=P)
        adj_rows = T["adj"].rearrange("(t p) n -> t p n", p=P)
        x_rows = T["x"].rearrange("(t p) d -> p t d", p=P)
        out_rows = T["out"].rearrange("(t p) d -> p t d", p=P)

        parts = Parts()
        made = sem("const_made")
        gw_loaded, avec_made, wlr_out, gw_made = sem("gw_loaded"), sem("avec_made"), sem("wlr_out"), sem("gw_made")
        dve_steps = sem("dve_steps")
        steps = Steps(nc.vector, dve_steps)

        def load_all(sp, plan, loaded):
            for dst, src in plan:
                sp.dma_start(dst, src, allow_slow_non_contiguous=True).then_inc(loaded, 16)

        def weight(name):
            return T[name].rearrange("(k p) n -> p k n", p=P)

        def wait_apart(eng, semaphore, value):
            if not isinstance(value, int):
                value = eng.snap(value)
                eng.compute_val(value)
            eng.wait_ge(made, 4)
            eng.wait_ge(semaphore, value)

        def split_unit(v, src, q, features_split):
            t = slice(UJ * q, UJ * q + UJ)
            steps(v.tensor_copy(UH[:, t, :], src[:, t, :]))
            steps.wait()
            v.tensor_tensor(UL[:, t, :], src[:, t, :], UH[:, t, :].bitcast(F32),
                            ALU.subtract).then_inc(features_split, 1)

        def tile_product(pe, jt, mh, ml, bank):
            last = None
            for k in range(DK):
                fc = slice(k * P, k * P + P)
                for n, (u, m) in enumerate(((UH, mh), (UH, ml), (UL, mh))):
                    last = pe.matmul(PS[:, bank + k, :], u[:, jt, fc], m,
                                     start=(jt == 0 and n == 0), stop=(jt == NT - 1 and n == 2))
            return last

        def half_unit(pe, h, mh, ml, bank):
            for r in range(HJ):
                last = tile_product(pe, HJ * h + r, mh[:, r, :], ml[:, r, :], bank)
            return last

        def small_product(pe, out, TH, TL, WH, WL, j):
            for k in range(DK):
                for n, (t, w) in enumerate(((TH, WH), (TH, WL), (TL, WH))):
                    last = pe.matmul(out, t[:, k, j * P:j * P + P], w[:, k, :],
                                     start=(k == 0 and n == 0), stop=(k == DK - 1 and n == 2))
            return last

        def split_weights(v, raw, high, low, made):
            steps(v.tensor_copy(high, raw))
            steps.wait()
            v.tensor_tensor(low, raw, high.bitcast(F32), ALU.subtract).then_inc(made, 1)

        def variances(v, tiles, var_ready):
            wait_apart(v, steps.semaphore, steps.base + steps.count)
            for j, t in enumerate(tiles):
                steps(v.bn_stats(stats[:, j, :], flat(X[:, one(t), :])))
            variances_of_stats(v, len(tiles), var_ready)

        def variances_of_stats(v, n, var_ready):
            wait_apart(v, steps.semaphore, steps.base + steps.count)
            for j in range(n):
                steps(v.bn_aggr(mv[:, j, :], stats[:, j, :]))
            steps.wait()
            v.tensor_scalar(rstd[:, 0:n], mv[:, 0:n, 1], EPS_LN, None, ALU.add).then_inc(var_ready, 1)

        def inverse_roots(pool, n, index, var_ready, roots_ready):
            pool.wait_ge(var_ready, index + 1)
            pool.tensor_tensor(rstd[:, 0:n], rstd[:, 0:n], mhalf[:, 0:n], ALU.pow).then_inc(roots_ready, 1)

        def normalise(v, tiles, index, roots_ready, normed):
            v.wait_ge(roots_ready, index + 1)
            for j, t in enumerate(tiles):
                Xt = flat(X[:, one(t), :])
                v.tensor_scalar(Xt, Xt, mv[:, j, 0:1], rstd[:, j:j + 1],
                                ALU.subtract, ALU.mult).then_inc(normed, 1)

        def chunk_tiles(c):
            return [c * TC + j for j in range(TC)]

        normed0 = sem("normed_0")
        with ExitStack() as lay:
            A = [ring] + [sb(lay, f"A{c}", [P, NT, CW]) for c in range(1, NC)]
            MH = sb(lay, "MH0", [P, SLOTS0, CW], F32R)
            ML = sb(lay, "ML0", [P, SLOTS0, CW], F32R)
            TT = sb(lay, "TT0", [P, 2, CW])
            W0T = sb(lay, "W0T_sb", [P, DK, D])
            zeros = sb(lay, "zeros", [P, P], F32R)
            bias0 = sb(lay, "bias0", [P, D])
            XT0 = A[NC - 1][:, NT - 4:NT - 2, :]
            WsaT = A[NC - 1][:, NT - 2, :].rearrange("p (k d) -> p k d", k=DK)
            avec = GW[:, 2:4, :].rearrange("p a d -> p (a d)")

        order = [(q, c) for n in range(NC - 1) for q, c in
                 [(q, n) for q in range(n)] + [(n, c) for c in range(n + 1)]]
        order += [(NU - 1, c) for c in range(NC - 1)] + [(q, NC - 1) for q in range(NU)]
        products0 = [(UJ * q + i, c) for q, c in order for i in range(UJ)]
        stage_end = [sum(max(q, c) <= n for q, c in order) * UJ for n in range(NC)]
        last_tile = {c: max(n for n, p in enumerate(products0) if p[1] == c) for c in range(NC)}
        degrees_after = {1: 5, 2: 16, 3: 24}
        turned_after = (52, 56, 60)
        transformed_after = {2: 7, 3: 10}
        AHEAD = SLOTS0

        x_loaded = [sem(f"x_loaded{q}") for q in range(NU)]
        w0_loaded, zeros_made = sem("w0_loaded"), sem("zeros_made")
        a_loaded = [[sem(f"a_loaded{c}_{q}") for q in range(NU)] for c in range(NC)]
        deg_even, deg_odd = sem("deg_even"), sem("deg_odd")
        deg_summed = sem("deg_summed")
        deg_out, deg_read, dis_ready = sem("deg_out"), sem("deg_read"), sem("dis_ready")
        xt_out, xt_copied, xw_out = sem("xt_out"), sem("xt_copied"), sem("xw_out")
        xw_high, features0, bias_added0 = sem("xw_high"), sem("features_0"), sem("bias_added_0")
        high0, low0, done0 = sem("high_0"), sem("low_0"), sem("done_0")
        rows_read0 = sem("rows_read_0")
        var0, roots0 = sem("var_0"), sem("roots_0")
        ADDS = NT // 2 - 1

        def transpose_bank(c, k):
            return k if c == 1 else 4 + k

        def xw_bank(c, p):
            return (2, 0)[p] if c == 1 else (6, 4)[p]

        def add_degrees(eng, c, q, odd, added):
            a = A[c]
            t = UJ * q + odd
            eng.wait_ge(a_loaded[c][q], 16)
            if q == 0:
                if c:
                    eng.wait_ge(deg_out, c)
                eng.tensor_tensor(TT[:, odd, :], a[:, t, :], a[:, t + 2, :], ALU.add).then_inc(added, 1)
            else:
                for i in range(2):
                    eng.wait_ge(added, c * ADDS + 2 * q - 1 + i)
                    eng.tensor_tensor(TT[:, odd, :], TT[:, odd, :], a[:, t + 2 * i, :],
                                      ALU.add).then_inc(added, 1)

        @parts.sync
        def _(sp):
            sp.dma_start(asa[:, :], T["a_sa"][0, :].rearrange("(k p) -> p k", p=P),
                         allow_slow_non_contiguous=True).then_inc(gw_loaded, 16)
            sp.dma_start(WsaT, weight("W_saT")).then_inc(gw_loaded, 16)
            sp.dma_start(W0T[:, :, :], weight("W0T")).then_inc(w0_loaded, 16)

            def load_x(c):
                t = slice(TC * c, TC * c + TC)
                sp.dma_start(X[:, t, :], x_rows[:, t, :]).then_inc(x_loaded[c], 16)

            def load_unit(c, q):
                sp.dma_start(A[c][:, UJ * q:UJ * q + UJ, :], adj_units[q, :, :, c * CW:c * CW + CW])\
                    .then_inc(a_loaded[c][q], 16)

            load_x(0)
            load_unit(0, 0)
            load_unit(0, 1)
            load_x(1)
            load_unit(0, 2)
            load_unit(0, 3)
            for q in range(NU):
                load_unit(1, q)
            load_x(2)
            load_x(3)
            for q in range(NU):
                load_unit(2, q)
            for q in range(NU - 1):
                load_unit(3, q)
            sp.wait_ge(wlr_out, 1)
            sp.wait_ge(xw_out, 2 * NC)
            load_unit(3, NU - 1)
            load_all(sp, [(bias0[:, :], T["b0"].partition_broadcast(P)),
                          (GW[:, 2, :], T["Wa"][0, D:2 * D].partition_broadcast(P)),
                          (GW[:, 3, :], T["Wb"][0, D:2 * D].partition_broadcast(P))], w0_loaded)

        @parts.gpsimd
        def _(pool):
            pool.memset(ones[:, :], 1.0).then_inc(made, 1)
            pool.memset(ident[:, :], 0.0).then_inc(made, 1)
            pool.memset(mhalf[:, :], -0.5).then_inc(made, 1)
            pool.wait_ge(made, 3)
            pool.affine_select(out=ident[:, :], in_=ident[:, :], compare_op=ALU.not_equal, fill=1.0,
                               base=0, pattern=[[-1, P]], channel_multiplier=1).then_inc(made, 1)
            for c in range(NC):
                for q in range(NU):
                    add_degrees(pool, c, q, 1, deg_odd)
                t = slice(TC * c, TC * c + TC)
                pool.wait_ge(made, 4)
                pool.wait_ge(deg_read, 2 * c + 2)
                pool.tensor_tensor(dis[:, t], dis[:, t], mhalf[:, :], ALU.pow).then_inc(dis_ready, 1)
            pool.wait_ge(w0_loaded, 64)
            for t in range(NT):
                if t % TC == 0:
                    pool.wait_ge(xt_out, DK * (t // TC + 1))
                pool.tensor_tensor(X[:, t, :], X[:, t, :], bias0[:, :], ALU.add).then_inc(bias_added0, 1)
            for c in range(NC):
                inverse_roots(pool, TC, c, var0, roots0)

        @parts.scalar
        def _(act):
            def transform(c):
                for k in range(DK):
                    act.wait_ge(xt_out, DK * c + k + 1)
                    if c:
                        act.wait_ge(xw_out, 2 * c)
                    act.activation(XT0[:, k, :], PS[:, transpose_bank(c, k), :], ACT.Copy).then_inc(xt_copied, 1)
                for p in range(2):
                    act.wait_ge(xw_out, 2 * c + p + 1)
                    t = TC * c + 2 * p
                    act.activation(UH[:, t:t + 2, :].rearrange("p t d -> p (t d)"), PS[:, xw_bank(c, p), :],
                                   ACT.Copy).then_inc(xw_high, 1)

            def high(n):
                t, c = products0[n]
                act.wait_ge(a_loaded[c][t // UJ], 16)
                act.wait_ge(dis_ready, t // UJ + 1)
                if n >= SLOTS0:
                    act.wait_ge(done0, n - SLOTS0 + 1)
                act.activation(MH[:, n % SLOTS0, :], A[c][:, t, :], ACT.Copy,
                               scale=dis[:, t:t + 1]).then_inc(high0, 1)

            transform(0)
            transform(1)
            for n in range(len(products0)):
                for c in (2, 3):
                    if n == transformed_after[c] + AHEAD:
                        transform(c)
                if n - 4 in turned_after[:2]:
                    for i in range(DK):
                        job_high(act, DK * turned_after.index(n - 4) + i)
                high(n)
            for i in range(DK):
                job_high(act, 2 * DK + i)

        @parts.tensor
        def _(pe):
            pe.wait_ge(gw_loaded, 32)
            pe.wait_ge(avec_made, 2 * DK)
            for h in range(2):
                for k in range(DK):
                    last = pe.matmul(PS[:, 7, h * D:h * D + D], avec[:, (2 * h + k) * P:(2 * h + k) * P + P],
                                     WsaT[:, k, :], start=(k == 0), stop=(k == DK - 1))
            last.then_inc(wlr_out, 1)

            def degrees(c):
                pe.wait_ge(deg_summed, c + 1)
                if c:
                    pe.wait_ge(deg_read, 2 * c)
                else:
                    pe.wait_ge(gw_made, 1)
                for j in range(TC):
                    last = pe.matmul(PS[:, 7, j:j + 1], TT[:, 0, j * P:j * P + P], ones[:, 0:1],
                                     start=True, stop=True)
                last.then_inc(deg_out, 1)

            def transform(c):
                pe.wait_ge(x_loaded[c], 16)
                if c > 1:
                    pe.wait_ge(features0, 2 * c)
                for k in range(DK):
                    for j in range(TC):
                        last = pe.transpose(PS[:, transpose_bank(c, k), j * P:j * P + P],
                                            X[:, TC * c + j, k * P:k * P + P], ident[:, :])
                    last.then_inc(xt_out, 1)
                pe.wait_ge(xt_copied, DK * (c + 1))
                for p in range(2):
                    for j in range(2):
                        for k in range(DK):
                            last = pe.matmul(PS[:, xw_bank(c, p), j * D:j * D + D],
                                             XT0[:, k, (2 * p + j) * P:(2 * p + j) * P + P], W0T[:, k, :],
                                             start=(k == 0), stop=(k == DK - 1))
                    last.then_inc(xw_out, 1)

            def product(n):
                t, c = products0[n]
                pe.wait_ge(features0, 4 if n == 0 else t // 2 + 1)
                pe.wait_ge(low0, n + 1)
                if t == 0 and c == NC - 1:
                    pe.wait_ge(deg_read, 2 * NC)
                if t == 0:
                    for b in range(2):
                        pe.matmul(PS[:, 2 * c + b, :], zeros[:, :], UH[:, 0:2, :].rearrange("p t d -> p (t d)"),
                                  start=True, stop=False)
                for i in range(TC):
                    cols = slice(i * P, i * P + P)
                    for k, (m, u) in enumerate(((MH, UH), (MH, UL), (ML, UH))):
                        last = pe.matmul(PS[:, 2 * c + i // 2, (i % 2) * D:(i % 2) * D + D],
                                         m[:, n % SLOTS0, cols], u[:, t, :],
                                         start=False, stop=(t == NT - 1 and k == 2 and i % 2 == 1))
                last.then_inc(done0, 1)

            pe.wait_ge(w0_loaded, 16)
            transform(0)
            transform(1)
            degrees(0)
            pe.wait_ge(zeros_made, 1)
            for n in range(len(products0)):
                product(n)
                if n in turned_after:
                    for i in range(DK):
                        prepare_job(pe, DK * turned_after.index(n) + i)
                for c in (2, 3):
                    if n == transformed_after[c]:
                        transform(c)
                for c in range(1, NC):
                    if n == degrees_after[c]:
                        degrees(c)

        @parts.vector
        def _(v):
            v.wait_ge(gw_loaded, 32)
            v.wait_ge(made, 4)
            for k in range(2 * DK):
                v.tensor_scalar(avec[:, k * P:k * P + P], ones[:, :], asa[:, k:k + 1], None,
                                ALU.mult).then_inc(avec_made, 1)
            v.tensor_scalar(zeros[:, :], ones[:, :], 0.0, None, ALU.mult).then_inc(zeros_made, 1)
            v.wait_ge(wlr_out, 1)
            v.tensor_copy(GW[:, 0:2, :], PS[:, 7, :].rearrange("p (a d) -> p a d", a=2)).then_inc(gw_made, 1)

            def sum_degrees(c):
                v.wait_ge(deg_even, (c + 1) * ADDS)
                v.wait_ge(deg_odd, (c + 1) * ADDS)
                v.tensor_tensor(TT[:, 0, :], TT[:, 0, :], TT[:, 1, :], ALU.add).then_inc(deg_summed, 1)

            def degree_columns(c):
                t = slice(TC * c, TC * c + TC)
                v.wait_ge(deg_out, c + 1)
                v.tensor_scalar(dis[:, t], PS[:, 7, 0:TC], EPS_DEG, None, ALU.add).then_inc(deg_read, 1)
                v.tensor_copy(deg[:, t], PS[:, 7, 0:TC]).then_inc(deg_read, 1)

            def transform(c):
                for p in range(2):
                    v.wait_ge(xw_high, 2 * c + p + 1)
                    t = TC * c + 2 * p
                    v.tensor_tensor(UL[:, t:t + 2, :].rearrange("p t d -> p (t d)"), PS[:, xw_bank(c, p), :],
                                    UH[:, t:t + 2, :].bitcast(F32).rearrange("p t d -> p (t d)"),
                                    ALU.subtract).then_inc(features0, 1)

            def low(n):
                t, c = products0[n]
                v.wait_ge(high0, n + 1)
                v.scalar_tensor_tensor(out=ML[:, n % SLOTS0, :], in0=A[c][:, t, :], scalar=dis[:, t:t + 1],
                                       in1=MH[:, n % SLOTS0, :].bitcast(F32), op0=ALU.mult,
                                       op1=ALU.subtract).then_inc(low0, 1)

            def take_rows(c, j):
                t = TC * c + j
                v.wait_ge(done0, last_tile[c] + 1)
                v.wait_ge(bias_added0, t + 1)
                v.scalar_tensor_tensor(out=X[:, t, :], in0=PS[:, 2 * c + j // 2, (j % 2) * D:(j % 2) * D + D],
                                       scalar=dis[:, t:t + 1], in1=X[:, t, :], op0=ALU.mult,
                                       op1=ALU.add).then_inc(rows_read0, 1)

            def row_variances(c):
                v.wait_ge(rows_read0, TC * (c + 1))
                if c:
                    v.wait_ge(normed0, TC * c)
                variances(v, chunk_tiles(c), var0)

            add_degrees(v, 0, 0, 0, deg_even)
            add_degrees(v, 0, 1, 0, deg_even)
            transform(0)
            add_degrees(v, 0, 2, 0, deg_even)
            add_degrees(v, 0, 3, 0, deg_even)
            sum_degrees(0)
            degree_columns(0)
            transform(1)
            adds = {}
            for c, start, gap in ((1, 1, 2), (2, 9, 2), (3, 20, 2)):
                for q in range(NU):
                    adds[start + gap * q] = (c, q)
            for n in range(len(products0)):
                for c in (2, 3):
                    if n == transformed_after[c] + AHEAD:
                        transform(c)
                if n in adds:
                    add_degrees(v, *adds[n], 0, deg_even)
                for c in range(1, NC):
                    if n == degrees_after[c] + 2:
                        sum_degrees(c)
                    if n == degrees_after[c] + 3:
                        degree_columns(c)
                if n - 5 in turned_after[:2]:
                    for i in range(DK):
                        job_low(v, DK * turned_after.index(n - 5) + i)
                low(n)
                for c in range(NC - 1):
                    if AHEAD <= n - last_tile[c] < AHEAD + TC:
                        take_rows(c, n - last_tile[c] - AHEAD)
                    if n == last_tile[c] + AHEAD + TC:
                        row_variances(c)
                    if n == last_tile[c] + AHEAD + TC + 2:
                        normalise(v, chunk_tiles(c), c, roots0, normed0)
            v.wait_ge(w1_loaded, 64)
            split_weights(v, Wedge_raw, EdgeH[:, :, :], EdgeL[:, :, :], w1_split)
            split_weights(v, Wsup_raw, SupH[:, :, :], SupL[:, :, :], w1_split)
            for i in range(DK):
                job_low(v, 2 * DK + i)
            for j in range(TC):
                take_rows(NC - 1, j)
            row_variances(NC - 1)
            normalise(v, chunk_tiles(NC - 1), NC - 1, roots0, normed0)

        normed1, dots_taken = sem("normed_1"), sem("dots_taken")
        summed, weighted = sem("summed"), sem("weighted")
        with ExitStack() as lay:
            EdgeH = sb(lay, "EdgeH", [P, DK, D], F32R)
            EdgeL = sb(lay, "EdgeL", [P, DK, D], F32R)
            SupH = sb(lay, "SupH", [P, DK, D], F32R)
            SupL = sb(lay, "SupL", [P, DK, D], F32R)
            nodew = sb(lay, "nodew", [P, D])
            bias1 = sb(lay, "bias1", [P, D])
            XTH = sb(lay, "XTH", [P, DK, N], F32R)
            XTL = sb(lay, "XTL", [P, DK, N], F32R)
            HH = sb(lay, "HH", [P, DK, N], F32R)
            HL = sb(lay, "HL", [P, DK, N], F32R)
            bias_m = sb(lay, "bias_m", [P, N])
            WH = sb(lay, "WH", [P, NT, P], F32R)
            WL = sb(lay, "WL", [P, NT, P], F32R)
            SH = sb(lay, "SH", [P, 2, DK, P], F32R)
            SL = sb(lay, "SL", [P, 2, DK, P], F32R)
            row_dots = sb(lay, "row_dots", [P, 4, D])
            logit = sb(lay, "logit", [P, NT])
            natt = sb(lay, "natt", [P, NT])
            small1 = sb(lay, "small1", [P, 8])
            mx = sb(lay, "mx", [P, 2, NC])
            nmax = sb(lay, "nmax", [P, 2])
            Z = sb(lay, "Z", [P, 2])
            scale1 = sb(lay, "scale1", [P, 2])
        arow = flat_ring[:, 0:2 * N].rearrange("p (s n) -> p s n", s=2)
        S = flat_ring[:, 2 * N:4 * N].rearrange("p (s n) -> p s n", s=2)

        Wedge_raw, Wsup_raw = (flat_ring[:, (2 * N + i * DK * D):(2 * N + (i + 1) * DK * D)].rearrange(
            "p (k d) -> p k d", k=DK) for i in range(2))

        w1_loaded, w1_split, bias_added1 = sem("w1_loaded"), sem("w1_split"), sem("bias_added_1")
        arow_loaded = [sem(f"arow_loaded{i}") for i in range(2)]
        job_done, job_act, job_dve = sem("job_done"), sem("job_act"), sem("job_dve")
        logits_ready, logit_max, logit_gmax = sem("logits_ready"), sem("logit_max"), sem("logit_gmax")
        logit_exp, logit_sum = sem("logit_exp"), sem("logit_sum")
        staged = sem("staged")
        scored = sem("scored")
        masked = sem("masked")
        max_ready, exp_ready = sem("max_ready"), sem("exp_ready")
        turned = sem("turned")
        turned_high, turned_low = sem("turned_high"), sem("turned_low")
        rows_read1 = sem("rows_read_1")
        var1, roots1, multiplied = sem("var_1"), sem("roots_1"), sem("multiplied")

        early, last = range(NC - 1), range(NC - 1, NC)
        jobs = []
        for kind, some in (("turn", early), ("edge", early), ("turn", last), ("support", early),
                           ("edge", last), ("support", last)):
            if kind == "support":
                jobs += [(kind, t, 0) for c in some for t in range(c * TC, c * TC + TC, 2)]
            else:
                jobs += [(kind, c, k) for c in some for k in range(DK)]
        N_EARLY = DK * (NC - 1)
        turns_done = {c: max(n for n, j in enumerate(jobs) if j[:2] == ("turn", c)) + 1 for c in range(NC)}
        BANKS1 = 6

        def job_target(job):
            kind, i, k = job
            cols = slice(i * CW, i * CW + CW)
            if kind == "turn":
                return XTH[:, k, cols], XTL[:, k, cols]
            if kind == "edge":
                return HH[:, k, cols], HL[:, k, cols]
            return (UH[:, i:i + 2, :].rearrange("p t d -> p (t d)"),
                    UL[:, i:i + 2, :].rearrange("p t d -> p (t d)"))

        def prepare_job(pe, n):
            kind, i, k = jobs[n]
            if n >= BANKS1:
                pe.wait_ge(job_act, n - BANKS1 + 1)
                pe.wait_ge(job_dve, n - BANKS1 + 1)
            bank = PS[:, n % BANKS1, :]
            if kind == "turn":
                pe.wait_ge(normed0, TC * i + TC)
                for j in range(TC):
                    last = pe.transpose(bank[:, j * P:j * P + P],
                                        X[:, i * TC + j, k * P:k * P + P], ident[:, :])
            elif kind == "edge":
                pe.wait_ge(w1_split, 2)
                pe.wait_ge(job_dve, turns_done[i])
                cols = slice(i * CW, i * CW + CW)
                for kk in range(DK):
                    for m, (w, x) in enumerate(((EdgeH, XTH), (EdgeH, XTL), (EdgeL, XTH))):
                        last = pe.matmul(bank, w[:, kk, k * P:k * P + P], x[:, kk, cols],
                                         start=(kk == 0 and m == 0), stop=(kk == DK - 1 and m == 2))
            else:
                for h in range(2):
                    last = small_product(pe, bank[:, h * D:h * D + D], XTH, XTL, SupH, SupL, i + h)
            last.then_inc(job_done, 1)

        def job_high(act, n):
            act.wait_ge(job_done, n + 1)
            act.activation(job_target(jobs[n])[0], PS[:, n % BANKS1, :], ACT.Copy).then_inc(job_act, 1)

        def job_low(v, n):
            hi, lo = job_target(jobs[n])
            v.wait_ge(job_act, n + 1)
            v.tensor_tensor(lo, PS[:, n % BANKS1, :], hi.bitcast(F32), ALU.subtract).then_inc(job_dve, 1)

        @parts.sync
        def _(sp):
            sp.wait_ge(high0, last_tile[0] + 1)
            sp.wait_ge(low0, last_tile[0] + 1)
            sp.wait_ge(deg_odd, 2 * ADDS)

            def load(t, s):
                if later(t, 2):
                    sp.wait_ge(weighted, t - 1)
                sp.dma_start(arow[:, s, :], adj_rows[one(t), :, :].rearrange("o p n -> (o p) n"))\
                  .then_inc(arow_loaded[s], 16)

            load(0, 0)
            load(1, 1)
            sp.wait_ge(high0, last_tile[1] + 1)
            sp.wait_ge(low0, last_tile[1] + 1)
            load_all(sp, [(Wedge_raw, weight("edge_w")), (Wsup_raw, weight("weight")),
                          (nodew[:, :], T["node_w"].rearrange("d o -> (d o)").partition_broadcast(P)),
                          (bias1[:, :], T["b1"].partition_broadcast(P))], w1_loaded)
            with sp.Fori(1, NT // 2) as g:
                load(g * 2, 0)
                load(g * 2 + 1, 1)

        @parts.tensor
        def _(pe):
            for n in range(N_EARLY, len(jobs)):
                prepare_job(pe, n)

            def score(t, s, c):
                if c == 0:
                    pe.wait_ge(staged, t + 1)
                if later(t, 1):
                    pe.wait_ge(masked, (t - 1) * NC + c + 1)
                cols = slice(c * CW, c * CW + CW)
                for k in range(DK):
                    for n, (a, b) in enumerate(((SH, HH), (SH, HL), (SL, HH))):
                        last = pe.matmul(PS[:, c, :], a[:, s, k, :], b[:, k, cols],
                                         start=(k == 0 and n == 0), stop=(k == DK - 1 and n == 2))
                last.then_inc(scored, 1)

            def turn(t, s, g):
                if g == 0:
                    pe.wait_ge(weighted, t + 1)
                if later(t * NU + g, 2):
                    pe.wait_ge(turned_high, t * NU + g - 1)
                    pe.wait_ge(turned_low, t * NU + g - 1)
                for r in range(UJ):
                    jt = UJ * g + r
                    last = pe.transpose(PS[:, 4 + g % 2, r * P:r * P + P],
                                        S[:, s, jt * P:jt * P + P], ident[:, :])
                last.then_inc(turned, 1)

            def weigh(t, s):
                if later(t, 2):
                    pe.wait_ge(rows_read1, t - 1)
                for g in range(NU):
                    pe.wait_ge(turned_low, t * NU + g + 1)
                    for r in range(UJ):
                        jt = UJ * g + r
                        for n, (w, u) in enumerate(((WH, UH), (WH, UL), (WL, UH))):
                            last = pe.matmul(PS[:, 6 + s, 0:D], w[:, jt, :], u[:, jt, :],
                                             start=(jt == 0 and n == 0),
                                             stop=(jt == NT - 1 and n == 2))
                last.then_inc(summed, 1)

            def tile(t, s):
                score(t, s, 0)
                score(t, s, 1)
                turn(t - 1, 1 - s, 0)
                score(t, s, 2)
                turn(t - 1, 1 - s, 1)
                score(t, s, 3)
                turn(t - 1, 1 - s, 2)
                turn(t - 1, 1 - s, 3)
                weigh(t - 1, 1 - s)

            for c in range(NC):
                last = max(n for n in range(len(jobs)) if n % BANKS1 == c) + 1
                pe.wait_ge(job_act, last)
                pe.wait_ge(job_dve, last)
                score(0, 0, c)
            pe.wait_ge(job_act, len(jobs))
            pe.wait_ge(job_dve, len(jobs))
            tile(1, 1)
            tile(2, 0)
            with pe.Fori(1, NT // 2 - 1) as g:
                tile(g * 2 + 1, 1)
                tile(g * 2 + 2, 0)
            tile(NT - 1, 1)
            pe.wait_ge(masked, NT * NC)
            left_rows(pe, 0)
            for g in range(NU):
                turn(NT - 1, 1, g)
            weigh(NT - 1, 1)

        def sum_dots(act, t):
            wait_apart(act, multiplied, t * 4 + 4)
            for g in range(4):
                act.activation(row_dots[:, g, :], row_dots[:, g, :], ACT.Copy,
                               accum_out=flat(dots[:, one(t), g:g + 1])).then_inc(dots_taken, 1)

        @parts.scalar
        def _(act):
            for n in range(N_EARLY, len(jobs)):
                job_high(act, n)
            act.wait_ge(logit_gmax, 1)
            act.activation(natt[:, :], logit[:, :], ACT.Exp, bias=small1[:, 2:3],
                           accum_out=small1[:, 3:4]).then_inc(logit_exp, 1)

            def exponent(t, s):
                act.wait_ge(max_ready, t + 1)
                act.activation(S[:, s, :], S[:, s, :], ACT.Exp, bias=nmax[:, s:s + 1],
                               accum_out=Z[:, s:s + 1]).then_inc(exp_ready, 1)

            def high(t, s):
                for g in range(NU):
                    act.wait_ge(turned, t * NU + g + 1)
                    act.activation(WH[:, UJ * g:UJ * g + UJ, :].rearrange("p t i -> p (t i)"),
                                   PS[:, 4 + g % 2, :], ACT.Copy).then_inc(turned_high, 1)

            exponent(0, 0)
            high(0, 0)
            exponent(1, 1)
            high(1, 1)
            exponent(2, 0)
            high(2, 0)
            exponent(3, 1)
            sum_dots(act, 0)
            high(3, 1)
            exponent(4, 0)
            sum_dots(act, 1)
            with act.Fori(2, NT // 2 - 1) as g:
                for s in (1, 0):
                    high(g * 2 + 1 - s, 1 - s)
                    exponent(g * 2 + 2 - s, s)
                    sum_dots(act, g * 2 - 1 - s)
            high(NT - 2, 0)
            exponent(NT - 1, 1)
            sum_dots(act, NT - 4)
            high_half(act, 0, 0)
            high_half(act, 0, 1)
            copy_left(act, 0)
            high(NT - 1, 1)

        @parts.gpsimd
        def _(pool):
            for t in range(NT):
                if t % TC == 0:
                    pool.wait_ge(job_done, turns_done[t // TC])
                pool.wait_ge(logits_ready, t + 1)
                pool.tensor_tensor(X[:, t, :], X[:, t, :], bias1[:, :], ALU.add).then_inc(bias_added1, 1)
            pool.wait_ge(logit_max, 1)
            pool.partition_all_reduce(small1[:, 1:2], small1[:, 0:1], P, RMAX).then_inc(logit_max, 1)
            pool.wait_ge(logit_exp, 1)
            pool.partition_all_reduce(small1[:, 4:5], small1[:, 3:4], P, RADD).then_inc(logit_sum, 1)

            def inverse_root(t, s):
                pool.wait_ge(var1, t + 1)
                pool.tensor_tensor(rstd[:, s:s + 1], rstd[:, s:s + 1], mhalf[:, 0:1],
                                   ALU.pow).then_inc(roots1, 1)

            def multiply(t):
                if later(t, 1):
                    pool.wait_ge(dots_taken, t * 4)
                wait_apart(pool, normed1, t + 1)
                for g in range(4):
                    pool.tensor_tensor(row_dots[:, g, :], flat(X[:, one(t), :]), GW[:, g, :],
                                       ALU.mult).then_inc(multiplied, 1)

            inverse_root(0, 0)
            inverse_root(1, 1)
            multiply(0)
            with pool.Fori(1, NT // 2 - 1) as g:
                for s in range(2):
                    inverse_root(g * 2 + s, s)
                    multiply(g * 2 + s - 1)
            inverse_root(NT - 2, 0)
            multiply(NT - 3)
            low_half(pool, 0, 0, raw_half(0))
            multiply(NT - 2)
            low_half(pool, 0, 1, raw_half(1))
            inverse_root(NT - 1, 1)
            low_half(pool, 0, 2, raw_half(2))
            low_half(pool, 0, 3, raw_half(3))
            multiply(NT - 1)

        @parts.vector
        def _(v):
            def node_logit(t):
                v.tensor_tensor_reduce(S[:, t // 8, (t % 8) * D:(t % 8) * D + D], X[:, t, :],
                                       nodew[:, :], 1.0, 0.0, ALU.mult, ALU.add,
                                       logit[:, t:t + 1]).then_inc(logits_ready, 1)

            v.wait_ge(normed0, NT)
            v.wait_ge(w1_split, 2)
            def stage(t, s):
                if later(t, 2):
                    v.wait_ge(scored, (t - 1) * NC)
                cols = bass.ds(t * P, P)
                steps(v.tensor_scalar(SH[:, s, :, :], HH[:, :, cols].bitcast(F32), 1.0, None, ALU.mult))
                v.tensor_scalar(SL[:, s, :, :], HL[:, :, cols].bitcast(F32), 1.0, None,
                                ALU.mult).then_inc(staged, 1)

            def mask_bias(t, s, turns):
                v.wait_ge(arow_loaded[s], turns * 16 + 16)
                steps(v.tensor_scalar(bias_m[:, :], arow[:, s, :], 0.0, NEG_BIG, ALU.is_le, ALU.mult))

            def mask(t, s, c):
                cols = slice(c * CW, c * CW + CW)
                wait_apart(v, scored, t * NC + c + 1)
                v.tensor_tensor_reduce(S[:, s, cols], PS[:, c, :], bias_m[:, cols], 1.0, -3.0e38,
                                       ALU.add, ALU.max, mx[:, s, c:c + 1]).then_inc(masked, 1)

            def row_max(t, s):
                v.wait_ge(masked, t * NC + NC)
                v.tensor_reduce(nmax[:, s:s + 1], mx[:, s, :], AX_X, ALU.max,
                                negate=True).then_inc(max_ready, 1)

            def low(t, s, g):
                v.wait_ge(turned_high, t * NU + g + 1)
                w = slice(UJ * g, UJ * g + UJ)
                v.tensor_tensor(WL[:, w, :].rearrange("p t i -> p (t i)"), PS[:, 4 + g % 2, :],
                                WH[:, w, :].rearrange("p t i -> p (t i)").bitcast(F32),
                                ALU.subtract).then_inc(turned_low, 1)

            def weight_rows(t, s):
                v.wait_ge(exp_ready, t + 1)
                v.tensor_tensor(S[:, s, :], S[:, s, :], arow[:, s, :], ALU.mult).then_inc(weighted, 1)

            def take_rows(t, s):
                steps(v.reciprocal(scale1[:, s:s + 1], Z[:, s:s + 1]))
                steps.wait()
                steps(v.tensor_tensor(scale1[:, s:s + 1], scale1[:, s:s + 1], natt[:, one(t)], ALU.mult))
                steps.wait()
                v.wait_ge(summed, t + 1)
                Xt = flat(X[:, one(t), :])
                v.scalar_tensor_tensor(out=Xt, in0=PS[:, 6 + s, 0:D], scalar=scale1[:, s:s + 1],
                                       in1=Xt, op0=ALU.mult, op1=ALU.add).then_inc(rows_read1, 1)
                wait_apart(v, rows_read1, t + 1)
                steps(v.bn_stats(stats[:, s, :], Xt))
                wait_apart(v, steps.semaphore, steps.base + steps.count)
                steps(v.bn_aggr(mv[:, s, :], stats[:, s, :]))
                steps.wait()
                v.tensor_scalar(rstd[:, s:s + 1], mv[:, s, 1:2], EPS_LN, None, ALU.add).then_inc(var1, 1)

            def normalise_tile(t, s):
                v.wait_ge(roots1, t + 1)
                Xt = flat(X[:, one(t), :])
                v.tensor_scalar(Xt, Xt, mv[:, s, 0:1], rstd[:, s:s + 1],
                                ALU.subtract, ALU.mult).then_inc(normed1, 1)

            TILE_STEPS = 6

            def tile(t, s, half):
                if later(t, 2):
                    normalise_tile(t - 2, s)
                mask(t, s, 0)
                mask(t, s, 1)
                low(t - 1, 1 - s, 0)
                mask(t, s, 2)
                low(t - 1, 1 - s, 1)
                mask(t, s, 3)
                row_max(t, s)
                low(t - 1, 1 - s, 2)
                low(t - 1, 1 - s, 3)
                if not (isinstance(t, int) and t == NT - 1):
                    stage(t + 1, 1 - s)
                    mask_bias(t + 1, 1 - s, half)
                weight_rows(t, s)
                take_rows(t - 1, 1 - s)
                steps.wait()

            for n in range(N_EARLY, len(jobs)):
                job_low(v, n)
                if n < N_EARLY + NT:
                    node_logit(n - N_EARLY)
                if n == len(jobs) - 3:
                    v.wait_ge(job_act, n)
                    v.wait_ge(job_dve, n)
                    stage(0, 0)
                    mask_bias(0, 0, 0)
            v.wait_ge(logits_ready, NT)
            v.tensor_reduce(small1[:, 0:1], logit[:, :], AX_X, ALU.max).then_inc(logit_max, 1)
            v.wait_ge(job_dve, len(jobs))
            v.wait_ge(job_act, len(jobs))
            steps.wait()
            for c in range(NC):
                mask(0, 0, c)
            row_max(0, 0)
            v.wait_ge(logit_max, 2)
            v.tensor_scalar(small1[:, 2:3], small1[:, 1:2], -1.0, None, ALU.mult).then_inc(logit_gmax, 1)
            stage(1, 1)
            mask_bias(1, 1, 0)
            weight_rows(0, 0)
            v.wait_ge(logit_sum, 1)
            steps(v.reciprocal(small1[:, 5:6], small1[:, 4:5]))
            steps.wait()
            steps(v.tensor_scalar(natt[:, :], natt[:, :], small1[:, 5:6], None, ALU.mult))
            steps.wait()
            v.wait_ge(bias_added1, NT)
            before = steps.count
            tile(1, 1, 1)
            assert steps.count - before == TILE_STEPS
            tile(2, 0, 1)
            entry = steps.count
            with v.Fori(1, NT // 2 - 1) as g:
                steps.restart(entry + (g - 1) * (2 * TILE_STEPS))
                tile(g * 2 + 1, 1, g + 1)
                tile(g * 2 + 2, 0, g + 1)
            steps.restart(0)
            steps.count = entry + (NT // 2 - 2) * 2 * TILE_STEPS
            for q in range(NU - 1):
                right_scores(v, q)
            left_diagonals(v, 0)
            tile(NT - 1, 1, None)
            for g in range(NU):
                low(NT - 1, 1, g)
            normalise_tile(NT - 2, 0)
            left_diagonals(v, 1)
            left_diagonals(v, 2)
            mask_half(v, 0, 0)
            split_low(v, 0, high2, features2)
            take_rows(NT - 1, 1)
            split_low(v, 1, high2, features2)
            normalise_tile(NT - 1, 1)

        with ExitStack() as lay:
            GcnH = sb(lay, "GcnH", [P, DK, D + 2], F32R)
            GcnL = sb(lay, "GcnL", [P, DK, D + 2], F32R)
            SaH = sb(lay, "SaH", [P, DK, D], F32R)
            SaL = sb(lay, "SaL", [P, DK, D], F32R)
            bg = sb(lay, "bg", [P, D])
            bias3 = sb(lay, "bias3", [P, D])
            gate_b = sb(lay, "gate_b", [P, 2])
            MH2 = sb(lay, "MH2", [P, HS, HJ, CW], F32R)
            ML2 = sb(lay, "ML2", [P, HS, HJ, CW], F32R)
            sleft = sb(lay, "sleft", [P, N])
            EM = sb(lay, "EM", [P, 2, HJ, CW])
            TAH = sb(lay, "TAH", [P, DK, CW], F32R)
            EH = sb(lay, "EH", [P, HS, HJ, CW], F32R)
            EL = sb(lay, "EL", [P, HS, HJ, CW], F32R)
            Zacc = sb(lay, "Zacc", [P, CW])
            Zsum = sb(lay, "Zsum", [P, CW])
            TAL = sb(lay, "TAL", [P, DK, CW], F32R)
            TEH = sb(lay, "TEH", [P, DK, CW], F32R)
            RE = sb(lay, "RE", [P, TC, D + 1])
            TEL = sb(lay, "TEL", [P, DK, CW], F32R)
            RA = sb(lay, "RA", [P, TC, D])
            nsr = sb(lay, "nsr", [P, NT])
            nsr01 = sb(lay, "nsr01", [P, NT])
            gate = sb(lay, "gate", [P, TC, 2])
            zr = sb(lay, "zr", [P, TC])
        diag = RA[:, :, :].rearrange("p (a b) d -> p a (b d)", a=2)
        flat_RE = RE[:, :, :].rearrange("p a b -> p (a b)")
        Wgcn_raw = flat_RE[:, 0:DK * (D + 2)].rearrange("p (k d) -> p k d", k=DK)
        Wsa_raw = flat_RE[:, DK * (D + 2):DK * (2 * D + 2)].rearrange("p (k d) -> p k d", k=DK)
        W3_raw = Zacc[:, :].rearrange("p (k d) -> p k d", k=DK)

        def raw_half(h):
            return ring[:, HJ * (h % 4):HJ * (h % 4) + HJ, :]

        def exp_half(which, h):
            first = NT // 2 + 4 * which + HJ * (h % 2)
            return ring[:, first:first + HJ, :]

        w2_loaded, w3_loaded = sem("w2_loaded"), sem("w3_loaded")
        w2_split, w3_split = sem("w2_split"), sem("w3_split")
        low_a, low_e = sem("low_a"), sem("low_e")
        unit_loaded = [sem(f"unit_loaded{i}") for i in range(2)]
        unit3_loaded = [sem(f"unit3_loaded{i}") for i in range(NU)]
        high2, features2, high3, features3 = sem("high_2"), sem("features_2"), sem("high_3"), sem("features_3")
        nsr_made, diag_made, left_out, left_copied = sem("nsr_made"), sem("diag_made"), sem("left_out"), sem("left_copied")
        half_high, half_low = sem("half_high"), sem("half_low")
        exps = sem("exps")
        smaller, att_masked = sem("smaller"), sem("att_masked")
        att_high, att_low = sem("att_high"), sem("att_low")
        z_half, z_added = sem("z_half"), sem("z_added")
        adj_done, att_done = sem("adj_done"), sem("att_done")
        copied_a, copied_e = sem("copied_a"), sem("copied_e")
        rows_out2, rows_read2 = sem("rows_out_2"), sem("rows_read_2")
        gates_in, gates_tanh = sem("gates_in"), sem("gates_tanh")
        mix_in, mix_tanh = sem("mix_in"), sem("mix_tanh")
        var2, roots2, normed2 = sem("var_2"), sem("roots_2"), sem("normed_2")
        rows_out3, rows_read3, normed3, stored = sem("rows_out_3"), sem("rows_read_3"), sem("normed_3"), sem("stored")
        var3, roots3 = sem("var_3"), sem("roots_3")
        C3 = NC
        N_W2 = 16 * 9

        @parts.sync
        def _(sp):
            sp.wait_ge(job_done, len(jobs))
            plan = [(Wsa_raw, weight("W_sa")), (Wgcn_raw[:, :, 0:D], weight("W_gcnb")),
                    (bg[:, :], T["b_gcnb"].partition_broadcast(P)),
                    (gate_b[:, 0:1], T["ba"].partition_broadcast(P)),
                    (gate_b[:, 1:2], T["bb"].partition_broadcast(P))]
            for g, name in enumerate(("Wa", "Wb")):
                for k in range(DK):
                    plan.append((Wgcn_raw[:, k, D + g:D + g + 1],
                                 T[name][0, k * P:k * P + P].rearrange("(p o) -> p o", o=1)))

            def load(c, q):
                if isinstance(c, int) and c == 0 and q < 2:
                    sp.wait_ge(weighted, NT - 1 + q)
                else:
                    sp.wait_ge(half_low, c * NH + 2 * q - 2)
                    sp.wait_ge(att_masked, c * NH + 2 * q - 2)
                sp.dma_start(ring[:, UJ * (q % 2):UJ * (q % 2) + UJ, :], adj_units[q, :, :, bass.ds(c * CW, CW)])\
                  .then_inc(unit_loaded[q % 2], 16)

            load(0, 0)
            load(0, 1)
            sp.wait_ge(job_act, len(jobs))
            sp.wait_ge(logits_ready, NT)
            sp.wait_ge(rows_read1, NT)
            load_all(sp, plan, w2_loaded)
            load(0, 2)
            load(0, 3)
            with sp.Fori(1, NC) as c:
                for q in range(NU):
                    load(c, q)

            def load3(c, q):
                if isinstance(c, int):
                    last = (NC - 1) * NH + 2 * (q + 2) + 2 if q < 2 else NC * NH
                    sp.wait_ge(att_masked, last)
                    if q < 2:
                        sp.wait_ge(half_low, last)
                else:
                    sp.wait_ge(half_low, c * NH + NC * NH - NH + 2 * q + 2)
                sp.dma_start(ring[:, UJ * q:UJ * q + UJ, :], adj_units[q, :, :, bass.ds(c * CW, CW)])\
                  .then_inc(unit3_loaded[q], 16)

            for q in range(NU):
                load3(0, q)
            sp.wait_ge(z_added, NC * NH)
            load_all(sp, [(W3_raw, weight("W3T")), (bias3[:, :], T["b3"].partition_broadcast(P))], w3_loaded)
            with sp.Fori(1, NC) as c:
                for q in range(NU):
                    load3(c, q)
            for c in range(NC):
                sp.wait_ge(normed3, TC * (c + 1))
                t = slice(TC * c, TC * c + TC)
                sp.dma_start(out_rows[:, t, :], X[:, t, :]).then_inc(stored, 16)
            sp.wait_ge(stored, 16 * NC)

        def low_half(eng, c, h, raw):
            eng.wait_ge(half_high, c * NH + h + 1)
            eng.tensor_tensor(ML2[:, h % HS, :, :], raw, MH2[:, h % HS, :, :].bitcast(F32),
                              ALU.subtract).then_inc(half_low, 1)

        @parts.gpsimd
        def _(pool):
            def low(c, h):
                low_half(pool, c, h, raw_half(h))

            def add_z(c, h):
                s = h % 2
                if h:
                    pool.wait_ge(z_added, c * NH + h)
                elif later(c, 1):
                    pool.wait_ge(z_added, c * NH)
                pool.wait_ge(att_masked, c * NH + h + 1)
                if h == 0:
                    pool.tensor_tensor(Zacc[:, :], EM[:, s, 0, :], EM[:, s, 1, :], ALU.add).then_inc(z_added, 1)
                    return
                pool.tensor_tensor(Zacc[:, :], Zacc[:, :], EM[:, s, 0, :], ALU.add).then_inc(z_half, 1)
                pool.wait_ge(z_half, c * (NH - 1) + h)
                out = Zacc if h < NH - 1 else Zsum
                if h == NH - 1 and later(c, 1):
                    pool.wait_ge(rows_out2, c * TC)
                pool.tensor_tensor(out[:, :], Zacc[:, :], EM[:, s, 1, :], ALU.add).then_inc(z_added, 1)

            def chunk(c):
                low(c, 2)
                low(c, 3)
                add_z(c, 0)
                add_z(c, 1)
                for h in range(4, NH):
                    low(c, h)
                    add_z(c, h - 2)
                add_z(c, NH - 2)
                add_z(c, NH - 1)

            for h in range(4, NH):
                add_z(0, h - 4)
                low(0, h)
            for h in range(4, NH):
                add_z(0, h)
            low(1, 0)
            low(1, 1)
            with pool.Fori(1, NC) as c:
                chunk(c)
                low(c + 1, 0)
                low(c + 1, 1)
                inverse_roots(pool, TC, c - 1, var2, roots2)
            for h in range(2, NH - 1):
                low_half(pool, C3, h, ring[:, HJ * h:HJ * h + HJ, :])
            inverse_roots(pool, TC, NC - 1, var2, roots2)
            for h in range(NH - 1, NH):
                low_half(pool, C3, h, ring[:, HJ * h:HJ * h + HJ, :])
            for c in range(NC):
                inverse_roots(pool, TC, c, var3, roots3)

        def high_half(act, c, h):
            act.wait_ge(unit_loaded[(h // 2) % 2], (c * 2 + h // 4) * 16 + 16)
            if later(c * NH + h, HS):
                act.wait_ge(adj_done, c * NH + h - HS + 1)
            act.activation(MH2[:, h % HS, :, :], raw_half(h), ACT.Copy).then_inc(half_high, 1)

        def split_high(act, q, normed, high):
            act.wait_ge(normed, TC * q + TC)
            t = slice(UJ * q, UJ * q + UJ)
            act.activation(UH[:, t, :], X[:, t, :], ACT.Copy).then_inc(high, 1)

        def split_low(v, q, high, features):
            v.wait_ge(high, q + 1)
            t = slice(UJ * q, UJ * q + UJ)
            v.tensor_tensor(UL[:, t, :], X[:, t, :], UH[:, t, :].bitcast(F32), ALU.subtract).then_inc(features, 1)

        def exponents(act, c, h):
            if later(c * NH + h, 2):
                wait_apart(act, att_masked, c * NH + h - 1)
            if isinstance(c, int) and c == 0:
                act.wait_ge(nsr_made, 2 * (h // 2) + 2)
                act.wait_ge(left_copied, 1)
            for r in range(HJ):
                jt = HJ * h + r
                zl = sleft[:, bass.ds(c * CW, CW)]
                act.activation(exp_half(0, h)[:, r, :], zl, ACT.Exp, bias=nsr[:, jt:jt + 1],
                               scale=-1.0).then_inc(exps, 1)
                act.activation(exp_half(1, h)[:, r, :], zl, ACT.Exp, bias=nsr01[:, jt:jt + 1],
                               scale=-0.01).then_inc(exps, 1)

        def copy_left(act, c):
            act.wait_ge(left_out, c + 1)
            act.activation(sleft[:, c * CW:c * CW + CW], PS[:, 2 + c, :], ACT.Copy).then_inc(left_copied, 1)

        @parts.scalar
        def _(act):
            def high(c, h):
                high_half(act, c, h)

            def copy_a(c):
                act.wait_ge(adj_done, c * NH + NH)
                if later(c, 1):
                    act.wait_ge(rows_out2, c * TC)
                for k in range(DK):
                    act.activation(TAH[:, k, :], PS[:, k, :], ACT.Copy).then_inc(copied_a, 1)

            def copy_e(c):
                act.wait_ge(att_done, c * NH + NH)
                if later(c, 1):
                    act.wait_ge(rows_out2, c * TC)
                for k in range(DK):
                    act.activation(TEH[:, k, :], PS[:, 2 + k, :], ACT.Copy).then_inc(copied_e, 1)

            def tanh_gates(c):
                act.wait_ge(gates_in, c + 1)
                act.activation(gate[:, :, :], gate[:, :, :], ACT.Tanh, scale=0.5).then_inc(gates_tanh, 1)

            def tanh_mix(c):
                act.wait_ge(mix_in, c + 1)
                act.activation(RA[:, :, :], RA[:, :, :], ACT.Tanh, scale=0.5).then_inc(mix_tanh, 1)

            exponents(act, 0, 0)
            sum_dots(act, NT - 3)
            act.wait_ge(summed, NT)
            split_high(act, 0, normed1, high2)
            split_high(act, 1, normed1, high2)
            high(0, 2)
            exponents(act, 0, 1)
            high(0, 3)
            split_high(act, 2, normed1, high2)
            sum_dots(act, NT - 2)
            copy_left(act, 1)
            exponents(act, 0, 2)
            split_high(act, 3, normed1, high2)
            sum_dots(act, NT - 1)
            copy_left(act, 2)
            high(0, 4)
            exponents(act, 0, 3)
            for h in range(5, NH):
                high(0, h)
                exponents(act, 0, h - 1)
            exponents(act, 0, NH - 1)
            copy_left(act, 3)

            def chunk(c):
                high(c, 0)
                exponents(act, c, 0)
                high(c, 1)
                copy_a(c - 1)
                exponents(act, c, 1)
                high(c, 2)
                copy_e(c - 1)
                high(c, 3)
                exponents(act, c, 2)
                exponents(act, c, 3)
                for h in range(4, NH):
                    high(c, h)
                    exponents(act, c, h)
                tanh_gates(c - 1)
                tanh_mix(c - 1)

            chunk(1)
            with act.Fori(2, NC) as c:
                chunk(c)

            def high3_half(c, h):
                act.wait_ge(unit3_loaded[h // 2], c * 16 + 16)
                act.wait_ge(adj_done, c * NH + NC * NH + h - HS + 1)
                act.activation(MH2[:, h % HS, :, :], ring[:, HJ * h:HJ * h + HJ, :], ACT.Copy)\
                    .then_inc(half_high, 1)

            copy_a(NC - 1)
            high3_half(0, 0)
            high3_half(0, 1)
            high3_half(0, 2)
            copy_e(NC - 1)
            split_high(act, 0, normed2, high3)
            high3_half(0, 3)
            split_high(act, 1, normed2, high3)
            split_high(act, 2, normed2, high3)
            tanh_gates(NC - 1)
            high3_half(0, 4)
            tanh_mix(NC - 1)
            for h in range(5, NH):
                high3_half(0, h)
            split_high(act, NU - 1, normed2, high3)

            def copy_a3(c):
                wait_apart(act, adj_done, c * NH + NC * NH + NH)
                if isinstance(c, int) and c == 0:
                    act.wait_ge(rows_out2, NC * TC)
                else:
                    wait_apart(act, rows_out3, c * TC)
                for k in range(DK):
                    act.activation(TAH[:, k, :], flat(PS[:, one(c * 2 + k), :]), ACT.Copy).then_inc(copied_a, 1)

            def chunk3(c):
                for h in range(3):
                    high3_half(c, h)
                copy_a3(c - 1)
                for h in range(3, NH):
                    high3_half(c, h)

            chunk3(1)
            with act.Fori(2, NC) as c:
                chunk3(c)
            copy_a3(NC - 1)

        def left_rows(pe, c):
            pe.wait_ge(diag_made, (c + 1) * TC)
            pe.matmul(PS[:, 2 + c, :], ones[:, :], diag[:, c % 2, :],
                      start=True, stop=True).then_inc(left_out, 1)

        @parts.tensor
        def _(pe):
            def adj(c, h):
                pe.wait_ge(half_low, c * NH + h + 1)
                if isinstance(c, int) and c == 0:
                    pe.wait_ge(features2, h // 2 + 1)
                if h == 0 and later(c, 1):
                    pe.wait_ge(low_a, c * DK)
                half_unit(pe, h, MH2[:, h % HS, :, :], ML2[:, h % HS, :, :], 0).then_inc(adj_done, 1)

            def att(c, h):
                pe.wait_ge(att_low, c * NH + h + 1)
                if h == 0:
                    if isinstance(c, int) and c == 0:
                        pe.wait_ge(left_copied, 2)
                    else:
                        pe.wait_ge(low_e, c * DK)
                half_unit(pe, h, EH[:, h % HS, :, :], EL[:, h % HS, :, :], 2).then_inc(att_done, 1)

            def rows_a(c, j):
                if j == 0:
                    pe.wait_ge(low_a, c * DK + DK)
                if later(c * TC + j, 2):
                    pe.wait_ge(rows_read2, 2 * (c * TC + j) - 2)
                small_product(pe, PS[:, 4 + j % 2, 0:D + 2], TAH, TAL, GcnH, GcnL, j)

            def rows_e(c, j):
                if j == 0:
                    pe.wait_ge(low_e, c * DK + DK)
                    pe.wait_ge(z_added, c * NH + NH)
                small_product(pe, PS[:, 6 + j % 2, 0:D], TEH, TEL, SaH, SaL, j)
                pe.matmul(PS[:, 6 + j % 2, D:D + 1], Zsum[:, j * P:j * P + P], ones[:, 0:1],
                          start=True, stop=True).then_inc(rows_out2, 1)

            def rows(c, j):
                rows_a(c, j)
                rows_e(c, j)

            def last_halves(c):
                adj(c, 6)
                att(c, 4)
                adj(c, 7)
                att(c, 5)
                att(c, 6)
                att(c, 7)

            left_rows(pe, 1)
            left_rows(pe, 2)
            adj(0, 0)
            adj(0, 1)
            adj(0, 2)
            adj(0, 3)
            for h in range(4, NH):
                att(0, h - 4)
                adj(0, h)
            left_rows(pe, 3)
            for h in range(4, NH):
                att(0, h)
            pe.wait_ge(w2_split, 2)
            pe.wait_ge(left_copied, NC)

            def chunk(c):
                adj(c, 0)
                adj(c, 1)
                adj(c, 2)
                rows(c - 1, 0)
                att(c, 0)
                adj(c, 3)
                rows(c - 1, 1)
                att(c, 1)
                adj(c, 4)
                rows(c - 1, 2)
                att(c, 2)
                adj(c, 5)
                rows(c - 1, 3)
                att(c, 3)
                last_halves(c)

            chunk(1)
            with pe.Fori(2, NC) as c:
                chunk(c)
            rows_a(NC - 1, 0)
            rows_a(NC - 1, 1)
            rows_e(NC - 1, 0)
            rows_e(NC - 1, 1)
            rows(NC - 1, 2)
            rows(NC - 1, 3)

            def adj3(c, h):
                pe.wait_ge(half_low, c * NH + NC * NH + h + 1)
                if isinstance(c, int) and c == 0:
                    pe.wait_ge(features3, h // 2 + 1)
                for r in range(HJ):
                    jt = HJ * h + r
                    for k in range(DK):
                        fc = slice(k * P, k * P + P)
                        for n, (u, m) in enumerate(((UH, MH2), (UH, ML2), (UL, MH2))):
                            last = pe.matmul(flat(PS[:, one(c * 2 + k), :]), u[:, jt, fc], m[:, h % HS, r, :],
                                             start=(jt == 0 and n == 0), stop=(jt == NT - 1 and n == 2))
                last.then_inc(adj_done, 1)

            def rows3(c, j):
                if j == 0:
                    pe.wait_ge(low_a, c * DK + NC * DK + DK)
                if j >= 2:
                    pe.wait_ge(rows_read3, c * TC + j - 1)
                small_product(pe, flat(PS[:, one(c * 2 + j % 2), 0:D]), TAH, TAL, SaH, SaL, j)\
                    .then_inc(rows_out3, 1)

            for h in range(NH):
                adj3(0, h)
            pe.wait_ge(w3_split, 1)
            with pe.Fori(1, NC) as c:
                adj3(c, 0)
                adj3(c, 1)
                rows3(c - 1, 0)
                rows3(c - 1, 1)
                adj3(c, 2)
                rows3(c - 1, 2)
                rows3(c - 1, 3)
                for h in range(3, NH):
                    adj3(c, h)
            for j in range(TC):
                rows3(NC - 1, j)

        def right_scores(v, q):
            t = slice(UJ * q, UJ * q + UJ)
            v.wait_ge(dots_taken, 4 * UJ * (q + 1))
            v.tensor_scalar(nsr[:, t], dots[:, t, 1], -1.0, None, ALU.mult).then_inc(nsr_made, 1)
            v.tensor_scalar(nsr01[:, t], dots[:, t, 1], -0.01, None, ALU.mult).then_inc(nsr_made, 1)

        def left_diagonals(v, c):
            if c >= 2:
                v.wait_ge(left_out, c - 1)
            for j in range(TC):
                v.tensor_scalar(diag[:, c % 2, j * P:j * P + P], ident[:, :],
                                dots[:, c * TC + j, 0:1], None, ALU.mult).then_inc(diag_made, 1)

        def smaller_half(v, c, h):
            u = c * NH + h
            Ea, Eb = exp_half(0, h), exp_half(1, h)
            v.wait_ge(exps, u * 4 + 4)
            v.tensor_tensor(Eb, Ea, Eb, ALU.min).then_inc(smaller, 1)

        def masked_half(v, c, h):
            u = c * NH + h
            v.wait_ge(smaller, u + 1)
            if later(u, 2):
                v.wait_ge(z_added, u - 1)
                v.wait_ge(att_low, u - 1)
            v.scalar_tensor_tensor(out=EM[:, h % 2, :, :].rearrange("p r w -> p (r w)"),
                                   in0=raw_half(h).rearrange("p r w -> p (r w)"),
                                   scalar=0.0, in1=exp_half(1, h).rearrange("p r w -> p (r w)"),
                                   op0=ALU.not_equal, op1=ALU.mult).then_inc(att_masked, 1)

        def mask_half(v, c, h):
            smaller_half(v, c, h)
            masked_half(v, c, h)

        def att_high_half(v, c, h):
            u = c * NH + h
            v.wait_ge(att_masked, u + 1)
            if later(u, HS):
                v.wait_ge(att_done, u - HS + 1)
            v.tensor_copy(EH[:, h % HS, :, :], EM[:, h % 2, :, :]).then_inc(att_high, 1)

        def att_low_half(v, c, h):
            v.wait_ge(att_high, c * NH + h + 1)
            v.tensor_tensor(EL[:, h % HS, :, :], EM[:, h % 2, :, :], EH[:, h % HS, :, :].bitcast(F32),
                            ALU.subtract).then_inc(att_low, 1)

        def split_half(v, c, h):
            att_high_half(v, c, h)
            att_low_half(v, c, h)

        @parts.vector
        def _(v):
            def attention(c, h):
                mask_half(v, c, h)
                split_half(v, c, h)

            def low_of(c, TH, TL, bank, copied, low):
                for k in range(DK):
                    v.wait_ge(copied, c * DK + k + 1)
                    v.tensor_tensor(TL[:, k, :], PS[:, bank + k, :], TH[:, k, :].bitcast(F32),
                                    ALU.subtract).then_inc(low, 1)

            def copy_rows(c, j):
                v.wait_ge(rows_out2, c * TC + j + 1)
                v.tensor_tensor(RA[:, j, :], PS[:, 4 + j % 2, 0:D], bg[:, :], ALU.add).then_inc(rows_read2, 1)
                steps(v.tensor_copy(gate[:, j, :], PS[:, 4 + j % 2, D:D + 2]))
                v.tensor_copy(RE[:, j, :], PS[:, 6 + j % 2, 0:D + 1]).then_inc(rows_read2, 1)

            def add_gates(c):
                steps.wait()
                v.tensor_tensor(gate[:, :, :], gate[:, :, :], dots[:, bass.ds(c * TC, TC), 2:4],
                                ALU.add).then_inc(gates_in, 1)

            def mix_rows(c):
                v.wait_ge(rows_read2, 2 * TC * (c + 1))
                steps(v.tensor_scalar(zr[:, :], RE[:, :, D], EPS_ATT, None, ALU.add))
                steps.wait()
                steps(v.reciprocal(zr[:, :], zr[:, :]))
                v.wait_ge(gates_tanh, c + 1)
                steps(v.tensor_scalar(gate[:, :, :], gate[:, :, :], 0.5, 0.5, ALU.mult, ALU.add))
                steps.wait()
                steps(v.tensor_tensor(zr[:, :], zr[:, :], gate[:, :, 0], ALU.mult))
                steps.wait()
                for j in range(TC):
                    steps(v.tensor_scalar(RE[:, j, 0:D], RE[:, j, 0:D], zr[:, j:j + 1], None, ALU.mult))
                steps.wait()
                for j in range(TC):
                    ins = v.scalar_tensor_tensor(out=RA[:, j, :], in0=RA[:, j, :],
                                                 scalar=gate[:, j, 1:2], in1=RE[:, j, 0:D],
                                                 op0=ALU.mult, op1=ALU.add)
                    steps(ins) if j < TC - 1 else ins.then_inc(mix_in, 1)

            def take_rows(c):
                v.wait_ge(mix_tanh, c + 1)
                steps(v.tensor_scalar(RA[:, :, :], RA[:, :, :], 0.5, 0.5, ALU.mult, ALU.add))
                steps.wait()
                Xc = X[:, bass.ds(c * TC, TC), :]
                steps(v.tensor_tensor(Xc, Xc, RA[:, :, :], ALU.add))

            PER_CHUNK = TC + 4 + TC + (TC - 1) + 2 + 2 * TC

            mask_half(v, 0, 1)
            split_half(v, 0, 0)
            split_low(v, 2, high2, features2)
            split_half(v, 0, 1)
            attention(0, 2)
            split_low(v, 3, high2, features2)
            for h in range(3, NH - 1):
                if h == 4:
                    right_scores(v, 3)
                    left_diagonals(v, 3)
                attention(0, h)
            v.wait_ge(w2_loaded, N_W2)
            split_weights(v, Wgcn_raw, GcnH[:, :, :], GcnL[:, :, :], w2_split)
            split_weights(v, Wsa_raw, SaH[:, :, :], SaL[:, :, :], w2_split)
            for g in range(2):
                steps(v.tensor_scalar(dots[:, :, 2 + g], dots[:, :, 2 + g], gate_b[:, g:g + 1], None, ALU.add))
            attention(0, NH - 1)
            low_of(0, TAH, TAL, 0, copied_a, low_a)
            low_of(0, TEH, TEL, 2, copied_e, low_e)
            steps.wait()
            entry = steps.count
            with v.Fori(1, NC) as c:
                steps.restart(entry + (c - 1) * PER_CHUNK)
                for h in (0, 2):
                    smaller_half(v, c, h)
                    smaller_half(v, c, h + 1)
                    masked_half(v, c, h)
                    masked_half(v, c, h + 1)
                    att_high_half(v, c, h)
                    att_high_half(v, c, h + 1)
                    att_low_half(v, c, h)
                    att_low_half(v, c, h + 1)
                for j in range(TC - 1):
                    copy_rows(c - 1, j)
                    attention(c, 4 + j)
                copy_rows(c - 1, TC - 1)
                add_gates(c - 1)
                mix_rows(c - 1)
                attention(c, 7)
                take_rows(c - 1)
                low_of(c, TAH, TAL, 0, copied_a, low_a)
                variances(v, chunk_tiles(c - 1), var2)
                low_of(c, TEH, TEL, 2, copied_e, low_e)
                assert steps.count == PER_CHUNK
                normalise(v, chunk_tiles(c - 1), c - 1, roots2, normed2)
            steps.restart(0)
            steps.count = entry + (NC - 1) * PER_CHUNK
            copy_rows(NC - 1, 0)
            copy_rows(NC - 1, 1)
            split_low(v, 0, high3, features3)
            copy_rows(NC - 1, 2)
            copy_rows(NC - 1, 3)
            add_gates(NC - 1)
            mix_rows(NC - 1)
            split_low(v, 1, high3, features3)
            take_rows(NC - 1)
            split_low(v, 2, high3, features3)
            variances(v, chunk_tiles(NC - 1), var2)
            normalise(v, chunk_tiles(NC - 1), NC - 1, roots2, normed2)
            split_low(v, 3, high3, features3)
            v.wait_ge(rows_out2, NT)
            v.wait_ge(w3_loaded, 32)
            split_weights(v, W3_raw, SaH[:, :, :], SaL[:, :, :], w3_split)
            v.wait_ge(half_low, NC * NH + NH)

            def low_a3(c):
                for k in range(DK):
                    wait_apart(v, copied_a, c * DK + NC * DK + k + 1)
                    v.tensor_tensor(TAL[:, k, :], flat(PS[:, one(c * 2 + k), :]), TAH[:, k, :].bitcast(F32),
                                    ALU.subtract).then_inc(low_a, 1)

            def add_bias3(c):
                for t in chunk_tiles(c):
                    Xt = flat(X[:, one(t), :])
                    steps(v.scalar_tensor_tensor(out=Xt, in0=bias3[:, :], scalar=deg[:, one(t)],
                                                 in1=Xt, op0=ALU.mult, op1=ALU.add))
                steps.wait()

            def low3(c, h):
                low_half(v, c + C3, h, ring[:, HJ * h:HJ * h + HJ, :])

            def take_rows3(c, j):
                v.wait_ge(rows_out3, c * TC + j + 1)
                Xt = flat(X[:, one(c * TC + j), :])
                v.tensor_tensor(Xt, flat(PS[:, one(c * 2 + j % 2), 0:D]), Xt, ALU.add).then_inc(rows_read3, 1)

            def row_variances3(c):
                wait_apart(v, rows_read3, c * TC + TC)
                variances(v, chunk_tiles(c), var3)

            entry = steps.count
            with v.Fori(1, NC) as c:
                steps.restart(entry + (c - 1) * (3 * TC))
                for h in range(3):
                    low3(c, h)
                low_a3(c - 1)
                low3(c, 3)
                low3(c, 4)
                add_bias3(c - 1)
                low3(c, 5)
                take_rows3(c - 1, 0)
                take_rows3(c - 1, 1)
                low3(c, 6)
                take_rows3(c - 1, 2)
                take_rows3(c - 1, 3)
                row_variances3(c - 1)
                assert steps.count == 3 * TC
                low3(c, 7)
                normalise(v, chunk_tiles(c - 1), c - 1, roots3, normed3)
            steps.restart(0)
            steps.count = entry + (NC - 1) * 3 * TC
            add_bias3(NC - 1)
            low_a3(NC - 1)
            for j in range(TC + 1):
                if j < TC:
                    take_rows3(NC - 1, j)
                if j:
                    v.wait_ge(rows_read3, NT - TC + j)
                    steps(v.bn_stats(stats[:, j - 1, :], X[:, NT - TC + j - 1, :]))
            variances_of_stats(v, TC, var3)
            normalise(v, chunk_tiles(NC - 1), NC - 1, roots3, normed3)

        parts.run(nc)


def kernel(x, adj, L0_gnn_W, L0_gnn_b, L1_gnn_weight, L1_gnn_bias, L1_gnn_node_w, L1_gnn_edge_w,
           L2_gnn_W_sa, L2_gnn_a_sa, L2_gnn_W_gcnb, L2_gnn_b_gcnb, L2_gnn_Wa, L2_gnn_ba, L2_gnn_Wb,
           L2_gnn_bb, L3_gnn_W, L3_gnn_b):
    import numpy as np
    import concourse.bacc as bacc
    from concourse.bass_utils import run_bass_kernel_spmd

    arrays = {
        "x": x, "adj": adj, "adjT": np.transpose(adj), "W0T": np.transpose(L0_gnn_W), "b0": L0_gnn_b,
        "weight": L1_gnn_weight, "b1": L1_gnn_bias, "node_w": L1_gnn_node_w, "edge_w": L1_gnn_edge_w,
        "W_sa": L2_gnn_W_sa, "W_saT": np.transpose(L2_gnn_W_sa), "a_sa": L2_gnn_a_sa,
        "W_gcnb": L2_gnn_W_gcnb, "b_gcnb": L2_gnn_b_gcnb, "Wa": L2_gnn_Wa, "ba": L2_gnn_ba,
        "Wb": L2_gnn_Wb, "bb": L2_gnn_bb, "W3T": np.transpose(L3_gnn_W), "b3": L3_gnn_b,
    }
    arrays = {name: np.ascontiguousarray(a) for name, a in arrays.items()}
    nc = bacc.Bacc("TRN2", target_bir_lowering=False, num_devices=1)
    T = {name: nc.dram_tensor(name, a.shape, mybir.dt.from_np(a.dtype), kind="ExternalInput").ap()
         for name, a in arrays.items()}
    T["out"] = nc.dram_tensor("out", (N, D), F32, kind="ExternalOutput").ap()
    graph_kernel(nc, T)
    r = run_bass_kernel_spmd(nc, [arrays], core_ids=[0])
    return r.results[0]["out"]
```
